# Optimizing a Trainium2 kernel written in Bass

```python
import numpy as np
import jax
import jax.numpy as jnp

def _softmax(x, axis=-1):
    return jax.nn.softmax(x, axis=axis)

def _gelu(x):
    return jax.nn.gelu(x, approximate=True)

def _silu(x):
    return jax.nn.silu(x)

def _sigmoid(x):
    return jax.nn.sigmoid(x)

def _layernorm(x, axis=-1, eps=1e-05):
    m = jnp.mean(x, axis=axis, keepdims=True)
    v = jnp.var(x, axis=axis, keepdims=True)
    return (x - m) / jnp.sqrt(v + eps)

def _scatter_add(tgt, idx, src, axis=0):
    return tgt.at[idx].add(src)

def _segment_sum(src, seg, n):
    return jax.ops.segment_sum(src, seg, n)
kernel_name = 'mk_xattn_ffn_d1_seqx_r4_77a25b'

def setup_inputs(seed: int=0):
    np.random.seed(seed)
    _w = jnp.asarray

    def _rec_inputs():
        import jax
        import jax.numpy as jnp
        _rk = jax.random.key(seed)
        x = 0.002226 + 0.9996 * jax.random.normal(jax.random.fold_in(_rk, 1), (4, 1024, 256), jnp.float32)
        _lenS = 1024 - jax.random.randint(jax.random.fold_in(_rk, 7), (4,), 0, max(1, 1024 // 4) + 1, jnp.int32)
        _lenS2 = 154 - jax.random.randint(jax.random.fold_in(_rk, 8), (4,), 0, max(1, 154 // 4) + 1, jnp.int32)
        _ctx_1024P = jax.random.normal(jax.random.fold_in(_rk, 11), (4, 16, 256), jnp.float32)
        _ctx_1024c = jax.random.dirichlet(jax.random.fold_in(_rk, 511), 0.3 * jnp.ones((16,), jnp.float32), (4, 154))
        _ctx_1024t = jnp.einsum('bsk,bkd->bsd', _ctx_1024c, _ctx_1024P)
        _ctx_1024t = _ctx_1024t * jax.lax.rsqrt(jnp.mean(jnp.square(_ctx_1024t)) + 1e-12) * 0.953939
        ctx_1024 = -0.000125008 + 0.999885 * (_ctx_1024t + 0.3 * jax.random.normal(jax.random.fold_in(_rk, 611), (4, 154, 256), jnp.float32))
        return (x, ctx_1024)
    x, ctx_1024 = _rec_inputs()

    def _L0_xattn_setup():
        import jax, jax.numpy as jnp
        import numpy as np
        EPS = 1e-05

        def layer_norm(x, g, b):
            mu = jnp.mean(x, axis=-1, keepdims=True)
            var = jnp.var(x, axis=-1, keepdims=True)
            return (x - mu) * jax.lax.rsqrt(var + EPS) * g + b
        key = jax.random.key(seed)
        ks = jax.random.split(key, 8)
        dim, heads, dim_head = (256, 16, 64)
        inner = heads * dim_head
        b, n, m = (8, 1024, 64)
        s = dim ** (-0.5)
        return {'x': jax.random.normal(ks[0], (b, n, dim), jnp.float32), 'latents': jax.random.normal(ks[1], (b, m, dim), jnp.float32), 'ln_m_g': jnp.ones((dim,), jnp.float32), 'ln_m_b': jnp.zeros((dim,), jnp.float32), 'ln_l_g': jnp.ones((dim,), jnp.float32), 'ln_l_b': jnp.zeros((dim,), jnp.float32), 'Wq': jax.random.normal(ks[2], (dim, inner), jnp.float32) * s, 'Wkv': jax.random.normal(ks[3], (dim, 2 * inner), jnp.float32) * s, 'Wout': jax.random.normal(ks[4], (inner, dim), jnp.float32) * s}
    _L0_xattn_all = _L0_xattn_setup()
    _L0_xattn_in = {k: v for k, v in _L0_xattn_all.items() if k in ('ln_m_g', 'ln_m_b', 'ln_l_g', 'ln_l_b', 'Wq', 'Wkv', 'Wout')}
    del _L0_xattn_all

    def _L0_ffn_setup():
        import jax, jax.numpy as jnp
        import numpy as np
        D_MODEL = 256
        D_HIDDEN = 1024
        NUM_EXPERTS = 8
        B, T = (2, 512)
        key = jax.random.key(seed)
        ks = jax.random.split(key, 8)
        s = 0.02
        x = jax.random.normal(ks[0], (B, T, D_MODEL), dtype=jnp.float32)
        Wg = jax.random.normal(ks[1], (D_MODEL, NUM_EXPERTS), dtype=jnp.float32) * s
        bg = jnp.zeros((NUM_EXPERTS,), dtype=jnp.float32)
        W1 = jax.random.normal(ks[2], (NUM_EXPERTS, D_MODEL, D_HIDDEN), dtype=jnp.float32) * s
        b1 = jnp.zeros((NUM_EXPERTS, D_HIDDEN), dtype=jnp.float32)
        W2 = jax.random.normal(ks[3], (NUM_EXPERTS, D_HIDDEN, D_MODEL), dtype=jnp.float32) * s
        b2 = jnp.zeros((NUM_EXPERTS, D_MODEL), dtype=jnp.float32)
        return {'x': x, 'Wg': Wg, 'bg': bg, 'W1': W1, 'b1': b1, 'W2': W2, 'b2': b2}
    _L0_ffn_all = _L0_ffn_setup()
    _L0_ffn_in = {k: v for k, v in _L0_ffn_all.items() if k in ('Wg', 'bg', 'W1', 'b1', 'W2', 'b2')}
    del _L0_ffn_all
    return {'x': x, 'ctx_1024': ctx_1024, 'L0_xattn_ln_m_g': _L0_xattn_in['ln_m_g'], 'L0_xattn_ln_m_b': _L0_xattn_in['ln_m_b'], 'L0_xattn_ln_l_g': _L0_xattn_in['ln_l_g'], 'L0_xattn_ln_l_b': _L0_xattn_in['ln_l_b'], 'L0_xattn_Wq': _L0_xattn_in['Wq'], 'L0_xattn_Wkv': _L0_xattn_in['Wkv'], 'L0_xattn_Wout': _L0_xattn_in['Wout'], 'L0_ffn_Wg': _L0_ffn_in['Wg'], 'L0_ffn_bg': _L0_ffn_in['bg'], 'L0_ffn_W1': _L0_ffn_in['W1'], 'L0_ffn_b1': _L0_ffn_in['b1'], 'L0_ffn_W2': _L0_ffn_in['W2'], 'L0_ffn_b2': _L0_ffn_in['b2']}

def reference(x, ctx_1024, L0_xattn_ln_m_g, L0_xattn_ln_m_b, L0_xattn_ln_l_g, L0_xattn_ln_l_b, L0_xattn_Wq, L0_xattn_Wkv, L0_xattn_Wout, L0_ffn_Wg, L0_ffn_bg, L0_ffn_W1, L0_ffn_b1, L0_ffn_W2, L0_ffn_b2):
    import jax
    import jax.numpy as jnp

    def _L0_xattn_ref(x, latents, ln_m_g, ln_m_b, ln_l_g, ln_l_b, Wq, Wkv, Wout):
        import jax, jax.numpy as jnp
        import numpy as np
        EPS = 1e-05

        def layer_norm(x, g, b):
            mu = jnp.mean(x, axis=-1, keepdims=True)
            var = jnp.var(x, axis=-1, keepdims=True)
            return (x - mu) * jax.lax.rsqrt(var + EPS) * g + b
        heads, dim_head = (16, 64)
        scale = dim_head ** (-0.5)
        x = layer_norm(x, ln_m_g, ln_m_b)
        lat = layer_norm(latents, ln_l_g, ln_l_b)
        b, m, _ = lat.shape
        q = lat @ Wq
        kv_input = jnp.concatenate([x, lat], axis=1)
        kv = kv_input @ Wkv
        k, v = jnp.split(kv, 2, axis=-1)

        def split_heads(t):
            return t.reshape(t.shape[0], t.shape[1], heads, dim_head).transpose(0, 2, 1, 3)
        q, k, v = (split_heads(q), split_heads(k), split_heads(v))
        dots = jnp.einsum('bhid,bhjd->bhij', q, k) * scale
        attn = jax.nn.softmax(dots, axis=-1)
        out = jnp.einsum('bhij,bhjd->bhid', attn, v)
        out = out.transpose(0, 2, 1, 3).reshape(b, m, heads * dim_head)
        return out @ Wout

    def _L0_ffn_ref(x, Wg, bg, W1, b1, W2, b2):
        import jax, jax.numpy as jnp
        import numpy as np
        D_MODEL = 256
        D_HIDDEN = 1024
        NUM_EXPERTS = 8
        B, T = (2, 512)
        gate_logits = jnp.einsum('btd,de->bte', x, Wg) + bg
        gate_scores = jax.nn.softmax(gate_logits, axis=-1)
        top1_idx = jnp.argmax(gate_scores, axis=-1)
        top1_mask = jax.nn.one_hot(top1_idx, NUM_EXPERTS, dtype=x.dtype)
        top1_weight = jnp.sum(gate_scores * top1_mask, axis=-1, keepdims=True)
        h = jax.nn.silu(jnp.einsum('btd,edh->bteh', x, W1) + b1)
        o = jnp.einsum('bteh,ehd->bted', h, W2) + b2
        y = jnp.sum(o * top1_mask[..., None], axis=2) * top1_weight
        return y
    x = x + _L0_xattn_ref(ctx_1024, _layernorm(x, axis=-1), L0_xattn_ln_m_g, L0_xattn_ln_m_b, L0_xattn_ln_l_g, L0_xattn_ln_l_b, L0_xattn_Wq, L0_xattn_Wkv, L0_xattn_Wout)
    x = x + _L0_ffn_ref(_layernorm(x, axis=-1), L0_ffn_Wg, L0_ffn_bg, L0_ffn_W1, L0_ffn_b1, L0_ffn_W2, L0_ffn_b2)
    return x

_drawn_inputs = setup_inputs


def setup_inputs(seed=0):
    import zlib

    import numpy as np

    out = dict(_drawn_inputs(seed))
    spreads = {'L0_xattn_ln_m_g': (1.0, 0.2),
     'L0_xattn_ln_m_b': (0.0, 0.289),
     'L0_xattn_ln_l_g': (1.0, 0.2),
     'L0_xattn_ln_l_b': (0.0, 0.1),
     'L0_ffn_bg': (0.0, 0.527),
     'L0_ffn_b1': (0.0, 0.8),
     'L0_ffn_b2': (0.0, 0.413)}
    factors = {'L0_ffn_W1': 2.823, 'L0_ffn_W2': 2.667}
    for name, (base, spread) in spreads.items():
        noise = np.random.default_rng([zlib.crc32(name.encode()), seed]).standard_normal(out[name].shape)
        drawn = base * np.exp(spread * noise) if base else spread * noise
        out[name] = jnp.asarray(drawn.astype(out[name].dtype))
    for name, factor in factors.items():
        out[name] = (out[name] * factor).astype(out[name].dtype)
    return out
```

```python
import concourse.bass as bass
from concourse import mybir
from contextlib import ExitStack

F32 = mybir.dt.float32
F16 = mybir.dt.float16
I32 = mybir.dt.int32
ALU = mybir.AluOpType
ACT = mybir.ActivationFunctionType
AX = mybir.AxisListType
ds = bass.ds

P = 128
B, N, D = 4, 1024, 256
C = 154
H, DH = 16, 64
INNER = H * DH
E, F = 8, 1024
KD = D // P
NT = N // P
KEYS = N + C
JT = 10
TAIL = C - P
PAIRS = H // 2
CT = B * C
CTILES = -(-CT // P)
TOK = B * N
TT = TOK // P
EPS = 1e-5
SCALE = float(DH) ** -0.5
HALF = 512
SORTED = TT + E
NOBODY = 2 * TOK
STATS = 6


def key_rows(j):
    return TAIL if j == JT - 1 else P


MAX_TAILS = [(0, 1, 2), (3, 4, 5), (6, 7)]
VALUE_TILES = [(0, 1, 2), (3, 4, 5), (6, 7), (8, 9)]
SLOTS = 4 * JT


def schedule(with_values):
    at = {s: [] for s in range(SLOTS)}
    for s, chunk in zip((4, 6), [("q", 0), ("q", 1)]):
        at[s].append(chunk)
    for s, chunk in zip((8, 9, 10), [("k", 0), ("k", 1), ("k", 2)]):
        at[s].append(chunk)
    maxima = [("max", t, c) for t in range(NT) for c in range(2)] + [("tail", g) for g in range(len(MAX_TAILS))]
    for s, chunk in zip(range(12, 12 + len(maxima)), maxima):
        at[s].append(chunk)
    at[33].append(("turn",))
    if with_values:
        for s, g in zip((31, 32, 34, 35), range(len(VALUE_TILES))):
            at[s].append(("v", g))
    return at


def numbered(at):
    n, out = 0, {}
    for s in range(SLOTS):
        out[s] = []
        for chunk in at[s]:
            out[s].append((n, chunk))
            n += 1
    return out, n


FOR_ODD, N_ODD = numbered(schedule(False))
FOR_EVEN, N_EVEN = numbered(schedule(True))
N_PAIR = N_ODD + N_EVEN
QK = 5
TURN = {0: max(n for c in FOR_EVEN.values() for n, k in c if k[0] == "turn"),
        1: max(n for c in FOR_ODD.values() for n, k in c if k[0] == "turn")}
FIRST_BANK = {0: 0, 1: N_EVEN % 2}
AHEAD = {0: FOR_EVEN, 1: FOR_ODD}
assert N_PAIR % 2 == 0


class Steps:

    def __init__(self, sem, start):
        self.sem, self.start, self.n = sem, start, 0

    def mark(self, ins):
        ins.then_inc(self.sem, 1)
        self.n += 1

    def reached(self):
        return self.start + self.n


def attention(nc, x, ctx_in, ln, Wq, Wkv, Wout, x2_dram):
    x_rows = x.rearrange("b (t p) d -> b p t d", p=P)
    ctx_rows = ctx_in.rearrange("b c d -> (b c) d")
    x2_rows = x2_dram.rearrange("(b t p) d -> b t p d", b=B, p=P)
    weights = [Wq.rearrange("(k p) n -> p k n", p=P),
               Wkv[:, 0:INNER].rearrange("(k p) n -> p k n", p=P),
               Wkv[:, INNER:2 * INNER].rearrange("(k p) n -> p k n", p=P),
               Wout.rearrange("(k p) n -> p k n", p=P)]

    stack = ExitStack()
    with stack:
        def sb(name, shape, dt):
            return stack.enter_context(nc.sbuf_tensor(name, shape, dt))

        def pb(name, shape, dt):
            return stack.enter_context(nc.psum_tensor(name, shape, dt))

        def sem(name):
            return stack.enter_context(nc.semaphore(name))

        ident = sb("ident", [P, P], F32)
        ln_rows = sb("ln_rows", [8, P], F32)
        ln_cols = sb("ln_cols", [P, 8], F32)
        wq = [sb(f"wq{i}", [P, KD, H, 2, DH], F16) for i in range(2)]
        wk = [sb(f"wk{i}", [P, KD, H, 2, DH], F16) for i in range(2)]
        wv = [sb(f"wv{i}", [P, KD, INNER], F16) for i in range(2)]
        wo = [sb(f"wo{i}", [P, INNER // P, D], F16) for i in range(2)]
        zx = [sb(f"zx{i}", [P, KD, TOK], F16) for i in range(2)]
        zc = [sb(f"zc{i}", [P, KD, CT], F16) for i in range(2)]
        q_both = [sb(f"q_both{i}", [P, N], F16) for i in range(2)]
        k_high = [sb(f"k_high{i}", [P, KEYS], F16) for i in range(2)]
        q_max = [sb(f"q_max{i}", [DH + 1, N], F16) for i in range(2)]
        k_low = [sb(f"k_low{i}", [DH + 1, KEYS], F16) for i in range(2)]
        max_row = [sb(f"max_row{i}", [NT, P], F16) for i in range(2)]
        max_parts = sb("max_parts", [P, NT, 3], F32)
        neg_max = sb("neg_max", [P, NT], F32)
        probs = [sb(f"probs{i}", [P, N], F32) for i in range(2)]
        values = [sb(f"values{i}", [P, JT, P], F32) for i in range(2)]
        values_wait = sb("values_wait", [P, JT, DH], F32)
        head_out = sb("head_out", [P, N], F32)
        recip = sb("recip", [DH, N], F32)
        normed = sb("normed", [P, N], F32)
        att = [sb(f"att{i}", [P, PAIRS, N], F16) for i in range(2)]
        x_res = [sb(f"x_res{i}", [P, D], F32) for i in range(2)]
        x2_tile = [sb(f"x2_tile{i}", [P, D], F32) for i in range(2)]
        stats = sb("stats", [P, NT, STATS], F32)
        mean_var = sb("mean_var", [P, NT, 2], F32)
        std = sb("std", [P, NT], F32)
        rstd = sb("rstd", [P, NT], F32)
        eps_col = sb("eps_col", [P, 1], F32)
        w_stage = [att[0][:, 4 * i:4 * i + 4, :].rearrange("p a n -> p (a n)").bitcast(F32) for i in range(2)]
        x_stage = [att[1][:, 4 * i:4 * i + 4, :].rearrange("p a n -> p (a n)").bitcast(F32)
                   .rearrange("p (t d) -> p t d", d=D) for i in range(2)]

        score = [pb(f"score{i}", [P, N], F32) for i in range(2)]
        acc = pb("acc", [P, N], F32)
        aux = [pb(f"aux{i}", [P, HALF], F32) for i in range(2)]

        pool_turns = sem("pool_turns")
        dve_turns = sem("dve_turns")
        ident_ready = sem("ident_ready")
        ln_loaded = sem("ln_loaded")
        ln_turned = sem("ln_turned")
        ln_ready = sem("ln_ready")
        w_loaded = [sem(f"w_loaded{i}") for i in range(2)]
        w_high = sem("w_high")
        w_low = sem("w_low")
        x_loaded = [sem(f"x_loaded{i}") for i in range(2)]
        z_step = sem("z_step")
        var_ready = sem("var_ready")
        std_ready = sem("std_ready")
        z_ready = sem("z_ready")
        z_turned = sem("z_turned")
        z_affine = sem("z_affine")
        z_high = sem("z_high")
        z_low = sem("z_low")
        ones_ready = sem("ones_ready")
        aux_full = sem("aux_full")
        aux_high = sem("aux_high")
        aux_done = sem("aux_done")
        q_copied = sem("q_copied")
        max_ready = sem("max_ready")
        max_sent = sem("max_sent")
        odd_values = sem("odd_values")
        score_full = sem("score_full")
        exp_done = sem("exp_done")
        av_done = sem("av_done")
        acc_copied = sem("acc_copied")
        norm_step = sem("norm_step")
        att_ready = sem("att_ready")
        res_loaded = [sem(f"res_loaded{i}") for i in range(2)]
        out_full = sem("out_full")
        out_read = sem("out_read")
        x2_stored = [sem(f"x2_stored{i}") for i in range(2)]

        C_ROWS = [min(P, CT - t * P) for t in range(CTILES)]
        C_HALVES = [C_ROWS[0:4], C_ROWS[4:]]
        X_HALVES = [[P] * 4, [P] * 4]

        def odd_base(n):
            return N_EVEN + N_PAIR * n

        def even_base(n):
            return N_PAIR * n

        def aux_bank(par, place):
            return aux[(FIRST_BANK[par] + place) % 2]

        block = stack.enter_context(nc.Block())

        @block.sync
        def _(sp):
            for i, v in enumerate(ln):
                sp.dma_start(ln_rows[2 * i:2 * i + 2, :], v.rearrange("(k p) -> k p", p=P)).then_inc(ln_loaded, 16)
            full = CTILES - 1
            sp.dma_start(x_stage[0][:, 0:full, :], ctx_rows[0:full * P, :].rearrange("(t p) d -> p t d", p=P))\
                .then_inc(x_loaded[0], 16)
            sp.dma_start(x_stage[0][0:C_ROWS[full], full, :], ctx_rows[full * P:CT, :]).then_inc(x_loaded[0], 16)
            for i in range(2):
                sp.dma_start(w_stage[i].rearrange("p (k n) -> p k n", k=KD), weights[i]).then_inc(w_loaded[i], 16)
            for b in range(B):
                if b >= 1:
                    sp.wait_ge(z_turned, 2 * b)
                i = (b + 1) % 2
                sp.dma_start(x_stage[i], x_rows[b]).then_inc(x_loaded[i], 16)
                if b < 2:
                    sp.wait_ge(w_low, b + 1)
                    sp.dma_start(w_stage[b].rearrange("p (k n) -> p k n", k=weights[b + 2].shape[1]),
                                 weights[b + 2]).then_inc(w_loaded[b], 16)

            def send_max(sent, buf):
                sp.wait_ge(aux_done, sent)
                sp.dma_start(q_max[buf][DH:DH + 1, :],
                             max_row[buf][:, :]).then_inc(max_sent, 16)

            send_max(TURN[0] + 1, 0)
            with sp.Fori(0, B) as b:
                with sp.Fori(0, PAIRS) as hp:
                    n = b * PAIRS + hp
                    send_max(odd_base(n) + TURN[1] + 1, 1)
                    send_max(even_base(n + 1) + TURN[0] + 1, 0)
                for t in range(NT):
                    if t >= 2:
                        sp.wait_ge(out_read, b * NT + t - 1)
                    sp.dma_start(x_res[t % 2][:, :], x_rows[ds(b, 1), :, t, :].rearrange("o p d -> (o p) d"))\
                        .then_inc(res_loaded[t % 2], 16)
                    if t >= 1:
                        sp.wait_ge(out_read, b * NT + t)
                        sp.dma_start(x2_rows[ds(b, 1), t - 1, :, :].rearrange("o p d -> (o p) d"),
                                     x2_tile[(t - 1) % 2][:, :]).then_inc(x2_stored[(t - 1) % 2], 16)
                sp.wait_ge(out_read, b * NT + NT)
                sp.dma_start(x2_rows[ds(b, 1), NT - 1, :, :].rearrange("o p d -> (o p) d"),
                             x2_tile[(NT - 1) % 2][:, :]).then_inc(x2_stored[(NT - 1) % 2], 16)
            for i in range(2):
                sp.wait_ge(x2_stored[i], 16 * TT // 2)

        @block.gpsimd
        def _(pool):
            nc.gpsimd.memset(ident[:, :], 0.0).then_inc(ident_ready, 1)
            pool.wait_ge(ident_ready, 1)
            nc.gpsimd.affine_select(out=ident[:, :], in_=ident[:, :], compare_op=ALU.not_equal, fill=1.0,
                                    base=0, pattern=[[-1, P]], channel_multiplier=1).then_inc(ident_ready, 1)
            def staged(i):
                return w_stage[i % 2]
            for i, w in enumerate((wq, wk)):
                pool.wait_ge(w_high, 2 * i + 2)
                src = staged(i).rearrange("p (k h d) -> p (k h) d", k=KD, h=H)
                hi = w[0][:, :, :, :, :].rearrange("p k h c d -> p (k h) c d")
                lo = w[1][:, :, :, :, :].rearrange("p k h c d -> p (k h) c d")
                for c in range(2):
                    last = nc.gpsimd.tensor_tensor(out=lo[:, :, c, :], in0=src, in1=hi[:, :, c, :], op=ALU.subtract)
                last.then_inc(w_low, 1)
            for i, w in ((2, wv), (3, wo)):
                pool.wait_ge(w_high, i + 3)
                nc.gpsimd.tensor_tensor(out=w[1][:, :, :].rearrange("p k n -> p (k n)"), in0=staged(i),
                                        in1=w[0][:, :, :].rearrange("p k n -> p (k n)"), op=ALU.subtract)\
                    .then_inc(w_low, 1)

            def copy_q(highs, buf, copied):
                pool.wait_ge(aux_high, highs)
                pool.sem_inc(pool_turns, 1)
                nc.gpsimd.tensor_copy(q_max[buf][0:DH, :], q_both[buf][0:DH, :]).then_inc(q_copied, 1)
                pool.wait_ge(q_copied, copied)
                pool.sem_inc(pool_turns, 1)

            copy_q(2, 0, 1)
            pool.wait_ge(aux_done, N_EVEN)
            nc.gpsimd.tensor_copy(values[1][:, :, 0:DH], values_wait[:, :, :]).then_inc(odd_values, 1)
            pool.wait_ge(odd_values, 1)
            with pool.Fori(0, B * PAIRS) as n:
                copy_q(QK * (2 * n + 1) + 2, 1, 2 * n + 2)
                copy_q(QK * (2 * n + 2) + 2, 0, 2 * n + 3)
                pool.wait_ge(aux_done, odd_base(n + 1))
                pool.wait_ge(av_done, 2 + 2 * JT * (n + 1))
                pool.sem_inc(pool_turns, 1)
                nc.gpsimd.tensor_copy(values[1][:, :, 0:DH], values_wait[:, :, :]).then_inc(odd_values, 1)
                pool.wait_ge(odd_values, n + 2)
                pool.sem_inc(pool_turns, 1)

        @block.scalar
        def _(act):
            for i, w in enumerate((wq, wk)):
                act.wait_ge(w_loaded[i], 16)
                src = w_stage[i].rearrange("p (k h d) -> p (k h) d", k=KD, h=H)
                hi = w[0][:, :, :, :, :].rearrange("p k h c d -> p (k h) c d")
                for c in range(2):
                    nc.scalar.activation(hi[:, :, c, :], src, ACT.Copy).then_inc(w_high, 1)

            def late_weight(i):
                w = (wv, wo)[i]
                act.wait_ge(w_loaded[i], 32)
                nc.scalar.activation(w[0][:, :, :].rearrange("p k n -> p (k n)"), w_stage[i], ACT.Copy)\
                    .then_inc(w_high, 1)

            def root(n, tiles):
                act.wait_ge(var_ready, n)
                nc.scalar.activation(std[:, 0:tiles], mean_var[:, 0:tiles, 1], ACT.Sqrt, bias=eps_col[:, :])\
                    .then_inc(std_ready, 1)

            def high_half(done, i, dst, cols):
                act.wait_ge(z_affine, done)
                src = probs[i][:, :].rearrange("p (k c) -> p k c", k=KD)[:, :, 0:cols]
                nc.scalar.activation(dst, src, ACT.Copy).then_inc(z_high, 1)

            act.wait_ge(ones_ready, 1)
            root(1, CTILES)
            for i, half in enumerate(C_HALVES):
                high_half(i + 1, i, zc[0][:, :, HALF * i:HALF * i + sum(half)], sum(half))
            with act.Fori(0, B) as b:
                root(2 * b + 2, NT)
                root(2 * b + 3, NT)
                for i in range(2):
                    high_half(2 * b + 2 + i + 1, i, zx[0][:, :, ds(b * N + i * HALF, HALF)], HALF)
            late_weight(0)
            late_weight(1)

            def high_parts(par, base, slots):
                for s in slots:
                    for place, chunk in AHEAD[par][s]:
                        if chunk[0] not in ("q", "k"):
                            continue
                        act.wait_ge(aux_full, base + place + 1)
                        dst = (q_both if chunk[0] == "q" else k_high)[par]
                        lo = chunk[1] * HALF
                        hi = min(lo + HALF, dst.shape[1])
                        nc.scalar.activation(dst[:, lo:hi], aux_bank(par, place)[:, 0:hi - lo], ACT.Copy)\
                            .then_inc(aux_high, 1)

            def exponent(tile, j):
                act.wait_ge(score_full, tile + 1)
                act.wait_ge(av_done, tile + 1)
                r = key_rows(j)
                nc.scalar.activation(probs[j % 2][0:r, :], score[j % 2][0:r, :], ACT.Exp, scale=SCALE)\
                    .then_inc(exp_done, 1)

            def head(g, nxt, base):
                for j in range(JT):
                    high_parts(nxt, base, (4 * j, 4 * j + 1))
                    exponent(JT * g + j + 1, (j + 1) % JT)
                    high_parts(nxt, base, (4 * j + 2, 4 * j + 3))
                act.wait_ge(av_done, JT * g + JT + 2)
                act.wait_ge(att_ready, g + 1)
                nc.scalar.activation(head_out[:, :], acc[:, :], ACT.Copy).then_inc(acc_copied, 1)

            high_parts(0, 0, range(SLOTS))
            exponent(0, 0)
            with act.Fori(0, B * PAIRS) as n:
                head(2 * n, 1, odd_base(n))
                head(2 * n + 1, 0, even_base(n + 1))

        @block.vector
        def _(dve):
            dve.sem_inc(att_ready, 1)
            for i in range(2):
                nc.vector.memset(values[i][:, :, DH:P], 1.0)
                nc.vector.memset(k_low[i][DH:DH + 1, :], 1.0)
            nc.vector.memset(values_wait[:, :, :], 0.0)
            nc.vector.memset(eps_col[:, :], EPS).then_inc(ones_ready, 1)
            nc.vector.memset(mean_var[:, :, :], 1.0).then_inc(z_step, 1)
            dve.wait_ge(z_step, 1)
            dve.wait_ge(ln_turned, 1)
            nc.vector.tensor_copy(ln_cols[:, :], aux[0][:, 0:8]).then_inc(ln_ready, 1)
            dve.wait_ge(ln_ready, 1)

            def normalise(rows, tiles, steps, roots):
                for t, r in enumerate(tiles):
                    last = nc.vector.bn_stats(stats[0:r, t, :], rows[0:r, t, :])
                steps.mark(last)
                dve.wait_ge(z_step, steps.reached())
                dve.sem_inc(dve_turns, 1)
                for t, r in enumerate(tiles):
                    last = nc.vector.bn_aggr(mean_var[0:r, t, :], stats[0:r, t, :])
                last.then_inc(var_ready, 1)
                dve.wait_ge(std_ready, roots)
                steps.mark(nc.vector.reciprocal(rstd[:, 0:len(tiles)], std[:, 0:len(tiles)]))
                dve.wait_ge(z_step, steps.reached())
                for t, r in enumerate(tiles):
                    last = nc.vector.tensor_scalar(rows[0:r, t, :], rows[0:r, t, :], mean_var[0:r, t, 0:1],
                                                   rstd[0:r, t:t + 1], ALU.subtract, ALU.mult)
                return last

            def split(group, halves, param, dst):
                for i, cols in enumerate(halves):
                    dve.wait_ge(z_turned, 2 * group + i + 1)
                    for k in range(KD):
                        last = nc.vector.tensor_scalar(probs[i][:, k * HALF:k * HALF + cols],
                                                       score[i][:, k * HALF:k * HALF + cols],
                                                       ln_cols[:, param + k:param + k + 1],
                                                       ln_cols[:, param + 2 + k:param + 3 + k], ALU.mult, ALU.add)
                    last.then_inc(z_affine, 1)
                for i, cols in enumerate(halves):
                    dve.wait_ge(z_high, 2 * group + i + 1)
                    nc.vector.tensor_tensor(out=dst(1, i, cols),
                                            in0=probs[i][:, :].rearrange("p (k c) -> p k c", k=KD)[:, :, 0:cols],
                                            in1=dst(0, i, cols), op=ALU.subtract).then_inc(z_low, 1)

            steps = Steps(z_step, 1)
            dve.wait_ge(x_loaded[0], 32)
            normalise(x_stage[0], C_ROWS, steps, 1).then_inc(z_ready, 1)
            split(0, [sum(h) for h in C_HALVES], 4, lambda w, i, cols: zc[w][:, :, HALF * i:HALF * i + cols])
            CTX_STEPS, X_STEPS = steps.reached(), 5
            with dve.Fori(0, B // 2) as i:
                for odd in range(2):
                    b = 2 * i + odd
                    steps = Steps(z_step, CTX_STEPS + X_STEPS * b)
                    if odd:
                        dve.wait_ge(x_loaded[0], 16 * i + 48)
                    else:
                        dve.wait_ge(x_loaded[1], 16 * i + 16)
                    rows = x_stage[1 - odd]
                    steps.mark(normalise(rows, [P] * NT, steps, 2 * b + 2))
                    dve.wait_ge(z_step, steps.reached())
                    normalise(rows, [P] * NT, steps, 2 * b + 3).then_inc(z_ready, 1)
                    assert steps.n == X_STEPS
                    split(b + 1, [HALF, HALF], 0, lambda w, i, cols: zx[w][:, :, ds(b * N + i * HALF, HALF)])

            def consume(par, idx, base, pair, slots):
                for s in slots:
                    for place, chunk in AHEAD[par][s]:
                        bank = aux_bank(par, place)
                        kind = chunk[0]
                        if kind in ("q", "k"):
                            c = chunk[1]
                            dve.wait_ge(aux_high, QK * idx + place + 1)
                            lo = c * HALF
                            hi = min(lo + HALF, N if kind == "q" else KEYS)
                            if kind == "q":
                                nc.vector.tensor_tensor(out=q_both[par][DH:P, lo:hi], in0=bank[DH:P, 0:hi - lo],
                                                        in1=q_both[par][DH:P, lo:hi], op=ALU.subtract)\
                                    .then_inc(aux_done, 1)
                            else:
                                nc.vector.tensor_tensor(out=k_low[par][0:DH, lo:hi], in0=bank[0:DH, 0:hi - lo],
                                                        in1=k_high[par][0:DH, lo:hi], op=ALU.subtract)\
                                    .then_inc(aux_done, 1)
                            continue
                        dve.wait_ge(aux_full, base + place + 1)
                        if kind == "max":
                            _, t, c = chunk
                            nc.vector.tensor_reduce(max_parts[:, t, c:c + 1], bank[:, :], AX.X, ALU.max)\
                                .then_inc(aux_done, 1)
                        elif kind == "tail":
                            ts = MAX_TAILS[chunk[1]]
                            nc.vector.tensor_reduce(max_parts[:, ts[0]:ts[-1] + 1, 2],
                                                    bank[:, 0:C * len(ts)].rearrange("p (t c) -> p t c", c=C),
                                                    AX.X, ALU.max).then_inc(aux_done, 1)
                            if chunk[1] == len(MAX_TAILS) - 1:
                                dve.wait_ge(aux_done, base + place + 1)
                                nc.vector.tensor_reduce(neg_max[:, :], max_parts[:, :, :], AX.X, ALU.max,
                                                        negate=True).then_inc(max_ready, 1)
                        elif kind == "turn":
                            nc.vector.tensor_copy(max_row[par][:, :], bank[0:NT, 0:P]).then_inc(aux_done, 1)
                        else:
                            js = VALUE_TILES[chunk[1]]
                            both = bank[:, 0:len(js) * P].rearrange("p (j c d) -> p j c d", j=len(js), c=2)
                            if pair is not None and chunk[1] == 0:
                                dve.wait_ge(odd_values, pair + 1)
                            groups = [(js, P)] if js[-1] < JT - 1 else [(js[:-1], P), (js[-1:], TAIL)]
                            for part, r in groups:
                                a = part[0] - js[0]
                                span = slice(part[0], part[-1] + 1)
                                nc.vector.tensor_copy(values[0][0:r, span, 0:DH], both[0:r, a:a + len(part), 0, :])
                                last = nc.vector.tensor_copy(values_wait[0:r, span, :],
                                                             both[0:r, a:a + len(part), 1, :])
                            last.then_inc(aux_done, 1)

            def normalise_head(g, par, hp):
                steps = Steps(norm_step, 3 * g)
                rows = slice(par * DH, par * DH + DH)
                dve.wait_ge(acc_copied, g + 2)
                steps.mark(nc.vector.reciprocal(recip[:, :], head_out[DH:P, :]))
                dve.wait_ge(norm_step, steps.reached())
                steps.mark(nc.vector.tensor_tensor(out=normed[rows, :], in0=head_out[0:DH, :], in1=recip[:, :],
                                                   op=ALU.mult))
                dve.wait_ge(norm_step, steps.reached())
                high = att[0][rows, ds(hp, 1), :].rearrange("p o n -> p (o n)")
                low = att[1][rows, ds(hp, 1), :].rearrange("p o n -> p (o n)")
                steps.mark(nc.vector.tensor_copy(high, normed[rows, :]))
                dve.wait_ge(norm_step, steps.reached())
                nc.vector.tensor_tensor(out=low, in0=normed[rows, :], in1=high, op=ALU.subtract)\
                    .then_inc(att_ready, 1)

            consume(0, 0, 0, None, range(SLOTS))
            with dve.Fori(0, B) as b:
                with dve.Fori(0, PAIRS) as hp:
                    n = b * PAIRS + hp
                    consume(1, 2 * n + 1, odd_base(n), n, range(SLOTS))
                    normalise_head(2 * n, 0, hp)
                    consume(0, 2 * n + 2, even_base(n + 1), n, range(SLOTS))
                    normalise_head(2 * n + 1, 1, hp)
                for t in range(NT):
                    dve.wait_ge(out_full, b * NT + t + 1)
                    dve.wait_ge(res_loaded[t % 2], 16 * (b * (NT // 2) + t // 2 + 1))
                    if t >= 2:
                        dve.wait_ge(x2_stored[t % 2], 16 * (b * (NT // 2) + t // 2))
                    nc.vector.tensor_tensor(out=x2_tile[t % 2][:, :], in0=acc[:, (t % 2) * HALF:(t % 2) * HALF + D],
                                            in1=x_res[t % 2][:, :], op=ALU.add).then_inc(out_read, 1)
                for i in range(2):
                    dve.wait_ge(x2_stored[i], 16 * (b + 1) * (NT // 2))
                    dve.sem_inc(dve_turns, 1)

        @block.tensor
        def _(pe):
            pe.sem_inc(av_done, 2)
            pe.sem_inc(exp_done, 2)
            pe.sem_inc(acc_copied, 1)
            pe.wait_ge(ident_ready, 2)
            pe.wait_ge(ln_loaded, 64)
            nc.tensor.transpose(aux[0][:, 0:8], ln_rows[:, :], ident[0:8, 0:8]).then_inc(ln_turned, 1)

            def turn(rows, group, halves):
                pe.wait_ge(z_ready, group + 1)
                t = 0
                for i, half in enumerate(halves):
                    if not isinstance(group, int) or group >= 1:
                        pe.wait_ge(z_affine, 2 * group + i - 1)
                    for q, r in enumerate(half):
                        for k in range(KD):
                            lo = k * HALF + q * P
                            last = nc.tensor.transpose(score[i][:, lo:lo + r], rows[0:r, t, k * P:k * P + P],
                                                       ident[0:r, 0:r])
                        t += 1
                    last.then_inc(z_turned, 1)

            turn(x_stage[0], 0, C_HALVES)
            with pe.Fori(0, B // 2) as i:
                turn(x_stage[1], 2 * i + 1, X_HALVES)
                turn(x_stage[0], 2 * i + 2, X_HALVES)
            pe.wait_ge(z_low, 2 * (B + 1))
            pe.wait_ge(w_low, 4)
            pe.wait_ge(ones_ready, 1)

            def summed(out, pairs):
                for i, (a, b) in enumerate(pairs):
                    last = nc.tensor.matmul(out, a, b, start=(i == 0), stop=(i == len(pairs) - 1))
                return last

            def produce(par, idx, base, batch, head, pair, slots):
                for s in slots:
                    for place, chunk in AHEAD[par][s]:
                        bank = aux_bank(par, place)
                        if not (isinstance(base, int) and base + place < 2):
                            pe.wait_ge(aux_done, base + place - 1)
                        kind = chunk[0]
                        if kind in ("q", "k"):
                            c = chunk[1]
                            w = wq if kind == "q" else wk
                            if c < 2:
                                cols = HALF
                                rhs = [[z[:, k, ds(batch * N + c * HALF, HALF)] for z in zx] for k in range(KD)]
                            else:
                                cols = C
                                rhs = [[z[:, k, ds(batch * C, C)] for z in zc] for k in range(KD)]
                            pairs = []
                            for k in range(KD):
                                lhs = [m[:, k, ds(head, 1), :, :].rearrange("p o c d -> p (o c d)") for m in w]
                                pairs += [(lhs[0], rhs[k][0]), (lhs[0], rhs[k][1]), (lhs[1], rhs[k][0])]
                            last = summed(bank[:, 0:cols], pairs)
                        elif kind == "max":
                            _, t, c = chunk
                            if t == 0 and c == 0:
                                pe.wait_ge(aux_done, base + QK)
                            last = summed(bank[:, :], [(q_both[par][:, t * P:t * P + P],
                                                        k_high[par][:, c * HALF:c * HALF + HALF])])
                        elif kind == "tail":
                            for i, t in enumerate(MAX_TAILS[chunk[1]]):
                                last = summed(bank[:, i * C:i * C + C],
                                              [(q_both[par][:, t * P:t * P + P], k_high[par][:, N:KEYS])])
                        elif kind == "turn":
                            pe.wait_ge(max_ready, idx + 1)
                            last = nc.tensor.transpose(bank[0:NT, 0:P], neg_max[:, :], ident[:, :])
                        else:
                            js = VALUE_TILES[chunk[1]]
                            for i, j in enumerate(js):
                                r = key_rows(j)
                                pairs = []
                                for k in range(KD):
                                    if j < NT:
                                        lhs = [z[:, k, ds(batch * N + j * P, r)] for z in zx]
                                    else:
                                        lhs = [z[:, k, ds(batch * C + (j - NT) * P, r)] for z in zc]
                                    rhs = [m[:, k, ds(pair * P, P)] for m in wv]
                                    pairs += [(lhs[0], rhs[0]), (lhs[1], rhs[0]), (lhs[0], rhs[1])]
                                last = summed(bank[0:r, i * P:i * P + P], pairs)
                        last.then_inc(aux_full, 1)

            def scores(par, tile, j, i):
                r = key_rows(j)
                cols = slice(i * HALF, i * HALF + HALF)
                return summed(score[j % 2][0:r, cols], [(k_high[par][:, j * P:j * P + r], q_both[par][:, cols]),
                                                        (k_low[par][:, j * P:j * P + r], q_max[par][:, cols])])

            def next_scores(par, idx, base, tile, j, i):
                if i == 0:
                    pe.wait_ge(exp_done, tile + 1)
                    if j == 0:
                        pe.wait_ge(aux_done, base + TURN[par] + 1)
                        pe.wait_ge(q_copied, idx + 1)
                        pe.wait_ge(max_sent, 16 * (idx + 1))
                last = scores(par, tile, j, i)
                if i == 1:
                    last.then_inc(score_full, 1)

            def weigh(par, g, n, j, i):
                if i == 0:
                    pe.wait_ge(exp_done, JT * g + j + 3)
                    if j == 0:
                        pe.wait_ge(acc_copied, g + 1)
                        if par == 0:
                            pe.wait_ge(aux_done, odd_base(n))
                        else:
                            pe.wait_ge(odd_values, n + 1)
                r = key_rows(j)
                cols = slice(i * HALF, i * HALF + HALF)
                last = nc.tensor.matmul(acc[:, cols], values[par][0:r, j, :], probs[j % 2][0:r, cols],
                                        start=(j == 0), stop=(j == JT - 1))
                if i == 1:
                    last.then_inc(av_done, 1)

            def head(par, g, n, nxt, nxt_base, batch, nxt_head, pair, own_base):
                for j in range(JT):
                    tile = JT * g + j + 1
                    for i in range(2):
                        if j + 1 < JT:
                            next_scores(par, g, own_base, tile, j + 1, i)
                        else:
                            next_scores(nxt, g + 1, nxt_base, tile, 0, i)
                        produce(nxt, g + 1, nxt_base, batch, nxt_head, pair, (4 * j + i,))
                    for i in range(2):
                        weigh(par, g, n, j, i)
                        produce(nxt, g + 1, nxt_base, batch, nxt_head, pair, (4 * j + 2 + i,))

            produce(0, 0, 0, 0, 0, 0, range(SLOTS))
            for i in range(2):
                next_scores(0, 0, 0, 0, 0, i)
            with pe.Fori(0, B) as b:
                with pe.Fori(0, PAIRS) as hp:
                    n = b * PAIRS + hp
                    head(0, 2 * n, n, 1, odd_base(n), b, 2 * hp + 1, None, None)
                    m = n + 1
                    batch = pe.snap((m >> 3) & (B - 1))
                    pair = pe.snap(m & (PAIRS - 1))
                    head(1, 2 * n + 1, n, 0, even_base(n + 1), batch, 2 * pair, pair, None)
                pe.wait_ge(att_ready, 2 * PAIRS * (b + 1) + 1)
                for t in range(NT):
                    if t >= 2:
                        pe.wait_ge(out_read, b * NT + t - 1)
                    pairs = []
                    for k in range(INNER // P):
                        lhs = [a[:, k, t * P:t * P + P] for a in att]
                        rhs = [w[:, k, :] for w in wo]
                        pairs += [(lhs[0], rhs[0]), (lhs[1], rhs[0]), (lhs[0], rhs[1])]
                    summed(acc[:, (t % 2) * HALF:(t % 2) * HALF + D], pairs).then_inc(out_full, 1)
                pe.wait_ge(out_read, b * NT + NT)


def experts(nc, x2_dram, listing, Wg, bg, W1, b1, W2, b2, out):
    x2_tiles = x2_dram.rearrange("(b t p) d -> b p t d", b=B, p=P)
    out_rows = out.rearrange("b n d -> (b n) d")
    KF = F // P
    GROUP = 4
    BANK = HALF // P
    META = 4
    OWN = 4

    stack = ExitStack()
    with stack:
        def sb(name, shape, dt):
            return stack.enter_context(nc.sbuf_tensor(name, shape, dt))

        def pb(name, shape, dt):
            return stack.enter_context(nc.psum_tensor(name, shape, dt))

        def sem(name):
            return stack.enter_context(nc.semaphore(name))

        ident = sb("e_ident", [P, P], F32)
        w1 = [sb(f"w1_{i}", [P, E, KD, F], F16) for i in range(2)]
        w2 = [sb(f"w2_{i}", [P, E, KF, D], F16) for i in range(2)]
        stage = [sb(f"e_stage{i}", [P, KD * F], F32) for i in range(2)]
        b2_all = sb("b2_all", [P, E, D], F32)
        b1_rows = sb("b1_rows", [E * KF, P], F32)
        b1_cols = sb("b1_cols", [P, E * KF], F32)
        wg = sb("wg", [P, KD, E], F32)
        bg_all = sb("bg_all", [P, E], F32)
        eps_col = sb("e_eps_col", [P, 1], F32)
        x2_all = sb("x2_all", [P, TT, D], F32)
        shared = x2_all[:, :, :].rearrange("p t d -> p (t d)")
        hidden = [shared[:, i * F:i * F + F] for i in range(2)]
        hidden_split = [[shared[:, (4 + 2 * h + i) * (F // 2):(5 + 2 * h + i) * (F // 2)].bitcast(F16)
                         .rearrange("p (k t) -> p k t", t=P) for i in range(2)] for h in range(2)]
        base = 8 * (F // 2)
        own_rows = [shared[:, base + i * D:base + i * D + D] for i in range(OWN)]
        base += OWN * D
        z_rows = [shared[:, base + i * D:base + i * D + D] for i in range(2)]
        base += 2 * D
        biased = [shared[:, base + i * D:base + i * D + D] for i in range(2)]
        base += 2 * D
        z_split = [[shared[:, base + (2 * h + i) * (D // 2):base + (2 * h + i + 1) * (D // 2)].bitcast(F16)
                    .rearrange("p (k t) -> p k t", t=P) for i in range(2)] for h in range(2)]
        base += 4 * (D // 2)
        z_group = [sb(f"z_group{i}", [P, GROUP, D], F32) for i in range(2)]
        z_cols = sb("z_cols", [P, GROUP, KD, P], F32)
        parts = sb("parts", [P, TT, STATS], F32)
        mean_var = sb("e_mean_var", [P, TT, 2], F32)
        std = sb("e_std", [P, TT], F32)
        rstd = sb("e_rstd", [P, TT], F32)
        logits = sb("logits", [P, TT, E], F32)
        top = sb("top", [P, TT], F32)
        work = [sb(f"work{i}", [P, TT, E], F32) for i in range(3)]
        chosen = sb("chosen", [P, TT, E], F16)
        first = sb("first", [P, TT], F32)
        e_less = sb("e_less", [P, E], F32)
        counts = sb("counts", [P, E], F32)
        counts_i = sb("counts_i", [P, E], I32)
        ends = [sb(f"ends{i}", [P, E], F32) for i in range(2)]
        place = sb("place", [P, TT], F32)
        place_i = sb("place_i", [P, TT], I32)
        rows = sb("rows", [P, TT, META], F32)
        rows_i = rows[:, :, :].bitcast(I32)
        upper = sb("upper", [P, P], F16)
        ones = sb("ones", [P, P], F16)
        fill = sb("fill", [P, SORTED, META], F32)
        fill_i = fill[:, :, :].bitcast(I32)
        meta = sb("meta", [P, SORTED, META], F32)
        meta_i = meta[:, :, :].bitcast(I32)
        read_f = sb("read_f", [P, SORTED], F32)
        read_i = sb("read_i", [P, SORTED], I32)
        starts = sb("starts", [P, SORTED], F32)
        past = z_group[0][:, :, :].rearrange("p t d -> p (t d)")[:, 0:SORTED * E].rearrange("p (t e) -> p t e", e=E)
        tile_f = sb("tile_f", [P, SORTED], F32)
        tile_expert = sb("tile_expert", [P, SORTED], I32)
        token = sb("token", [P, TT], I32)
        read_col = [sb(f"read_col{i}", [P, 1], I32) for i in range(OWN)]
        write_col = [sb(f"write_col{i}", [P, 1], I32) for i in range(OWN)]
        place_col = [sb(f"place_col{i}", [P, 1], I32) for i in range(2)]

        turned = [pb(f"turned{i}", [P, HALF], F32) for i in range(2)]
        up = [pb(f"up{i}", [P, F], F32) for i in range(2)]
        down = [pb(f"down{i}", [P, HALF], F32) for i in range(2)]

        c_step = sem("c_step")
        consts = sem("consts")
        small_loaded = sem("small_loaded")
        b1_turned = sem("b1_turned")
        b1_ready = sem("b1_ready")
        x2_loaded = sem("x2_loaded")
        r_step = sem("r_step")
        r_var = sem("r_var")
        r_std = sem("r_std")
        g_rows = sem("g_rows")
        g_turned = sem("g_turned")
        g_cols = sem("g_cols")
        g_logits = sem("g_logits")
        g_taken = sem("g_taken")
        shifted = sem("shifted")
        powers = sem("powers")
        chosen_ready = sem("chosen_ready")
        ranks = sem("ranks")
        e_loaded = [sem(f"e_loaded{i}") for i in range(2)]
        e_high = sem("e_high")
        e_low = sem("e_low")
        filled = sem("filled")
        placed = sem("placed")
        listed = sem("listed")
        meta_loaded = sem("meta_loaded")
        meta_ready = sem("meta_ready")
        col_step = sem("col_step")
        gathered = [sem(f"gathered{i}") for i in range(OWN)]
        scattered = [sem(f"scattered{i}") for i in range(OWN)]
        z_ready = sem("e_z_ready")
        z_turned = sem("e_z_turned")
        z_high = sem("e_z_high")
        z_done = sem("e_z_done")
        up_full = sem("up_full")
        silu_done = sem("silu_done")
        h_high = sem("h_high")
        h_done = sem("h_done")
        down_full = sem("down_full")
        bias_added = sem("bias_added")
        y_ready = sem("y_ready")
        turns = {e: sem("e_turns_" + e) for e in ("pool", "dve", "act")}

        def at_least(eng, s, value, carry=None):
            if isinstance(value, int) and value <= 0:
                return
            eng.wait_ge(s, value)
            if carry and not isinstance(value, int):
                eng.sem_inc(turns[carry], 1)

        def tile_steps(eng, step):
            for u in range(OWN):
                step(0, u)
            with eng.Fori(1, SORTED // OWN - 1) as i:
                for u in range(OWN):
                    step(i, u)
            for u in range(OWN):
                step(SORTED // OWN - 1, u)

        def number(i, u):
            return OWN * i + u

        def exists(i, u):
            return not (isinstance(i, int) and number(i, u) >= SORTED)

        block = stack.enter_context(nc.Block())

        @block.sync
        def _(sp):
            sp.dma_start(b1_rows[:, :], b1.rearrange("e (k p) -> (e k) p", p=P)).then_inc(small_loaded, 16)
            sp.dma_start(wg[:, :, :], Wg.rearrange("(k p) e -> p k e", p=P)).then_inc(small_loaded, 16)
            sp.dma_start(bg_all[:, :], bg.rearrange("(o e) -> o e", o=1).to_broadcast([P, E])).then_inc(small_loaded, 16)
            sp.dma_start(b2_all[:, :, :].rearrange("p e d -> p (e d)"),
                         b2.rearrange("(o e) d -> o (e d)", o=1).to_broadcast([P, E * D])).then_inc(small_loaded, 16)
            for b in range(B):
                sp.dma_start(x2_all[:, b * NT:b * NT + NT, :], x2_tiles[b]).then_inc(x2_loaded, 16)
            w1_rows = W1.rearrange("e (k p) n -> e p k n", p=P)
            w2_rows = W2.rearrange("e (k p) n -> e p k n", p=P)

            def load(e, i, src):
                dst = stage[i][:, :].rearrange("p (k n) -> p k n", k=src.shape[2])
                sp.dma_start(dst, src[ds(e, 1), :, :, :].rearrange("o p k n -> (o p) k n")).then_inc(e_loaded[i], 16)

            load(0, 0, w1_rows)
            load(0, 1, w2_rows)
            with sp.Fori(1, E) as e:
                sp.wait_ge(e_low, 2 * e - 1)
                load(e, 0, w1_rows)
                sp.wait_ge(e_low, 2 * e)
                load(e, 1, w2_rows)
            sp.wait_ge(listed, 16 * TT)
            sp.dma_start(meta[:, :, :], listing.rearrange("(k p) c -> p k c", p=P)).then_inc(meta_loaded, 16)

        @block.gpsimd
        def _(pool):
            nc.gpsimd.memset(ident[:, :], 0.0).then_inc(c_step, 1)
            nc.gpsimd.memset(ones[:, :], 1.0).then_inc(c_step, 1)
            pool.wait_ge(c_step, 2)
            nc.gpsimd.affine_select(out=ident[:, :], in_=ident[:, :], compare_op=ALU.not_equal, fill=1.0,
                                    base=0, pattern=[[-1, P]], channel_multiplier=1).then_inc(c_step, 1)
            nc.gpsimd.affine_select(out=upper[:, :], in_=ones[:, :], compare_op=ALU.is_gt, fill=0.0,
                                    base=0, pattern=[[1, P]], channel_multiplier=-1).then_inc(c_step, 1)
            nc.gpsimd.iota(e_less[:, :], [[1, E]], base=-E, channel_multiplier=0,
                           allow_small_or_imprecise_dtypes=True).then_inc(c_step, 1)
            nc.gpsimd.iota(starts[:, :], [[P, SORTED]], base=0, channel_multiplier=0,
                           allow_small_or_imprecise_dtypes=True).then_inc(c_step, 1)
            nc.gpsimd.iota(token[:, :], [[P, TT]], base=0, channel_multiplier=1).then_inc(c_step, 1)
            nc.gpsimd.memset(fill[:, :, :], 0.0).then_inc(c_step, 1)
            pool.wait_ge(c_step, 8)
            nc.gpsimd.iota(fill_i[:, :, 0], [[0, SORTED]], base=NOBODY, channel_multiplier=0).then_inc(c_step, 1)
            pool.wait_ge(c_step, 9)
            nc.gpsimd.memset(eps_col[:, :], EPS).then_inc(consts, 1)
            pool.dma_start(listing.rearrange("(k p) c -> p k c", p=P), fill[:, :, :]).then_inc(filled, 16)
            with pool.Fori(0, E) as e:
                for i, w in enumerate((w1, w2)):
                    high, low = [m[:, ds(e, 1), :, :].rearrange("p o k n -> p (o k n)") for m in w]
                    pool.wait_ge(e_high, 2 * e + i + 1)
                    pool.sem_inc(turns["pool"], 1)
                    nc.gpsimd.tensor_tensor(out=low, in0=stage[i][:, :], in1=high, op=ALU.subtract)\
                        .then_inc(e_low, 1)
            pool.wait_ge(filled, 16)
            pool.wait_ge(placed, 1)
            for t in range(TT):
                nc.gpsimd.indirect_dma_start(out=listing, out_offset=bass.IndirectOffsetOnAxis(place_i[:, t:t + 1], 0),
                                             in_=rows[:, t, :], in_offset=None).then_inc(listed, 16)
            pool.wait_ge(meta_ready, 1)

            def gather(i, u):
                if not exists(i, u):
                    return
                q = u % OWN
                at_least(pool, scattered[q], 16 * (i + u // OWN), "pool")
                k = number(i, u)
                nc.gpsimd.tensor_copy(read_col[q][:, :], read_i[:, ds(k, 1)]).then_inc(col_step, 1)
                nc.gpsimd.tensor_copy(write_col[q][:, :], meta_i[:, ds(k, 1), 0]).then_inc(col_step, 1)
                at_least(pool, col_step, 2 * k + 2, "pool")
                nc.gpsimd.indirect_dma_start(out=own_rows[q], out_offset=None, in_=x2_dram,
                                             in_offset=bass.IndirectOffsetOnAxis(read_col[q][:, :], 0))\
                    .then_inc(gathered[q], 16)

            def step(i, u):
                gather(i, u + 2)
                at_least(pool, y_ready, number(i, u) + 1, "pool")
                nc.gpsimd.indirect_dma_start(out=out_rows, out_offset=bass.IndirectOffsetOnAxis(write_col[u][:, :], 0),
                                             in_=own_rows[u], in_offset=None, bounds_check=TOK - 1,
                                             oob_is_err=False).then_inc(scattered[u], 16)

            gather(0, 0)
            gather(0, 1)
            tile_steps(pool, step)
            for q in range(OWN):
                pool.wait_ge(scattered[q], 16 * (SORTED // OWN))

        @block.scalar
        def _(act):
            act.wait_ge(consts, 1)
            act.wait_ge(r_var, 1)
            nc.scalar.activation(std[:, :], mean_var[:, :, 1], ACT.Sqrt, bias=eps_col[:, :]).then_inc(r_std, 1)

            def high_weights(e):
                for i, w in enumerate((w1, w2)):
                    act.wait_ge(e_loaded[i], 16 * (e + 1))
                    act.sem_inc(turns["act"], 1)
                    nc.scalar.activation(w[0][:, ds(e, 1), :, :].rearrange("p o k n -> p (o k n)"), stage[i][:, :],
                                         ACT.Copy).then_inc(e_high, 1)

            act.sem_inc(g_logits, 1)
            with act.Fori(0, TT // GROUP // 2) as i:
                for par in range(2):
                    g = 2 * i + par
                    act.wait_ge(g_turned, g + 1)
                    act.wait_ge(g_logits, g + 1)
                    nc.scalar.activation(z_cols[:, :, :, :].rearrange("p t k c -> p (t k c)"), up[par][:, :],
                                         ACT.Copy).then_inc(g_cols, 1)
                high_weights(i)
            act.wait_ge(shifted, 1)
            nc.scalar.activation(work[1][:, :, :], work[0][:, :, :], ACT.Exp).then_inc(powers, 1)
            with act.Fori(TT // GROUP // 2, E) as e:
                high_weights(e)

            act.wait_ge(meta_ready, 1)

            def z_high_half(i, u):
                if not exists(i, u):
                    return
                at_least(act, z_turned, number(i, u) + 1)
                nc.scalar.activation(z_split[0][u % 2], turned[u % 2][:, 0:D].rearrange("p (k t) -> p k t", t=P),
                                     ACT.Copy).then_inc(z_high, 1)

            def hidden_layer(i, u):
                if not exists(i, u):
                    return
                k = number(i, u)
                e = act.value_load(tile_expert[0:1, ds(k, 1)], min_val=0, max_val=E - 1)
                at_least(act, h_done, k - 1)
                for c in range(KF):
                    if c % BANK == 0:
                        at_least(act, up_full, KF // BANK * k + c // BANK + 1, "act")
                    nc.scalar.activation(hidden[u % 2][:, c * P:c * P + P], up[u % 2][:, c * P:c * P + P], ACT.Silu,
                                         bias=b1_cols[:, ds(e * KF + c, 1)]).then_inc(silu_done, 1)

            def hidden_high(i, u):
                if not exists(i, u):
                    return
                k = number(i, u)
                at_least(act, down_full, k - 1)
                at_least(act, silu_done, KF * k + KF)
                nc.scalar.activation(hidden_split[0][u % 2].rearrange("p k t -> p (k t)"), hidden[u % 2], ACT.Copy)\
                    .then_inc(h_high, 1)

            z_high_half(0, 0)
            hidden_layer(0, 0)
            z_high_half(0, 1)
            hidden_high(0, 0)

            def step(i, u):
                hidden_layer(i, u + 1)
                z_high_half(i, u + 2)
                hidden_high(i, u + 1)

            tile_steps(act, step)

        @block.vector
        def _(dve):
            r = Steps(r_step, 0)

            def link(ins):
                r.mark(ins)
                dve.wait_ge(r_step, r.reached())

            dve.wait_ge(b1_turned, 1)
            nc.vector.tensor_copy(b1_cols[:, :], turned[0][:, 0:E * KF]).then_inc(b1_ready, 1)
            for b in range(B):
                dve.wait_ge(x2_loaded, 16 * B)
                for t in range(b * NT, b * NT + NT):
                    last = nc.vector.bn_stats(parts[:, t, :], x2_all[:, t, :])
            link(last)
            for t in range(TT):
                last = nc.vector.bn_aggr(mean_var[:, t, :], parts[:, t, :])
            last.then_inc(r_var, 1)
            dve.wait_ge(r_std, 1)
            link(nc.vector.reciprocal(rstd[:, :], std[:, :]))
            dve.wait_ge(small_loaded, 64)

            def group_rows(i, par, ahead):
                g = 2 * i + par
                if ahead:
                    dve.wait_ge(g_turned, g - 1)
                for q in range(GROUP):
                    t = GROUP * g + q
                    last = nc.vector.tensor_scalar(
                        z_group[par][:, q, :], x2_all[:, ds(t, 1), :].rearrange("p o d -> p (o d)"),
                        mean_var[:, ds(t, 1), 0], rstd[:, ds(t, 1)], ALU.subtract, ALU.mult)
                last.then_inc(g_rows, 1)

            def take_logits(i, par):
                g = 2 * i + par
                dve.wait_ge(g_logits, g + 2)
                nc.vector.tensor_tensor(out=logits[:, ds(GROUP * g, GROUP), :],
                                        in0=down[par][:, 0:GROUP * E].rearrange("p (t e) -> p t e", e=E),
                                        in1=bg_all[:, :].unsqueeze(1).to_broadcast([P, GROUP, E]),
                                        op=ALU.add).then_inc(g_taken, 1)

            group_rows(0, 0, False)
            group_rows(0, 1, False)
            with dve.Fori(1, TT // GROUP // 2) as i:
                for par in range(2):
                    group_rows(i, par, True)
                for par in range(2):
                    take_logits(i - 1, par)
            for par in range(2):
                take_logits(TT // GROUP // 2 - 1, par)
            dve.wait_ge(g_taken, TT // GROUP)

            def tt(out, a, b, op):
                link(nc.vector.tensor_tensor(out=out, in0=a, in1=b, op=op))

            def per_token(a):
                return a.unsqueeze(2).to_broadcast([P, TT, E])

            def per_expert(a):
                return a.unsqueeze(1).to_broadcast([P, TT, E])

            dve.wait_ge(consts, 1)
            link(nc.vector.tensor_reduce(top[:, :], logits[:, :, :], AX.X, ALU.max))
            nc.vector.tensor_tensor(out=work[0][:, :, :], in0=logits[:, :, :], in1=per_token(top[:, :]),
                                    op=ALU.subtract).then_inc(shifted, 1)
            tt(work[2][:, :, :], logits[:, :, :], per_token(top[:, :]), ALU.is_equal)
            tt(work[2][:, :, :], work[2][:, :, :], per_expert(e_less[:, :]), ALU.mult)
            link(nc.vector.tensor_reduce(first[:, :], work[2][:, :, :], AX.X, ALU.min))
            dve.wait_ge(powers, 1)
            nc.vector.tensor_tensor(out=chosen[:, :, :], in0=per_expert(e_less[:, :]), in1=per_token(first[:, :]),
                                    op=ALU.is_equal).then_inc(chosen_ready, 1)
            link(nc.vector.tensor_reduce(place[:, :], work[1][:, :, :], AX.X, ALU.add))
            link(nc.vector.reciprocal(rows[:, :, 1], place[:, :]))
            nc.vector.tensor_copy(rows_i[:, :, 0], token[:, :])
            nc.vector.tensor_copy(rows[:, :, 2], mean_var[:, :, 0])
            nc.vector.tensor_copy(rows[:, :, 3], rstd[:, :])
            dve.wait_ge(ranks, 1)
            before = turned[0][:, 0:TT * E].rearrange("p (t e) -> p t e", e=E)
            totals = turned[1][:, 0:TT * E].rearrange("p (t e) -> p t e", e=E)
            link(nc.vector.tensor_copy(work[0][:, :, :], totals))
            at, to, reach = 0, 1, 1
            while reach < TT:
                nc.vector.tensor_copy(work[to][:, 0:reach, :], work[at][:, 0:reach, :])
                tt(work[to][:, reach:TT, :], work[at][:, reach:TT, :], work[at][:, 0:TT - reach, :], ALU.add)
                at, to, reach = to, at, 2 * reach
            sums, spare = work[at], work[to]
            link(nc.vector.tensor_scalar(counts[:, :], sums[:, TT - 1, :], float(P - 1), None, ALU.add))
            link(nc.vector.tensor_copy(counts_i[:, :], counts[:, :]))
            shift = P.bit_length() - 1
            link(nc.vector.tensor_scalar(counts_i[:, :], counts_i[:, :], shift, shift, ALU.logical_shift_right,
                                         ALU.logical_shift_left))
            link(nc.vector.tensor_copy(counts[:, :], counts_i[:, :]))
            link(nc.vector.tensor_copy(ends[0][:, :], counts[:, :]))
            e_at, e_to, reach = 0, 1, 1
            while reach < E:
                nc.vector.tensor_copy(ends[e_to][:, 0:reach], ends[e_at][:, 0:reach])
                tt(ends[e_to][:, reach:E], ends[e_at][:, reach:E], ends[e_at][:, 0:E - reach], ALU.add)
                e_at, e_to, reach = e_to, e_at, 2 * reach
            end, start = ends[e_at], ends[e_to]
            tt(start[:, :], end[:, :], counts[:, :], ALU.subtract)
            tt(spare[:, :, :], totals, sums[:, :, :], ALU.subtract)
            tt(sums[:, :, :], before, spare[:, :, :], ALU.subtract)
            tt(sums[:, :, :], sums[:, :, :], per_expert(start[:, :]), ALU.add)
            tt(sums[:, :, :], sums[:, :, :], chosen[:, :, :], ALU.mult)
            link(nc.vector.tensor_reduce(place[:, :], sums[:, :, :], AX.X, ALU.add))
            nc.vector.tensor_copy(place_i[:, :], place[:, :]).then_inc(placed, 1)
            tt(past, end[:, :].unsqueeze(1).to_broadcast([P, SORTED, E]),
               starts[:, :].unsqueeze(2).to_broadcast([P, SORTED, E]), ALU.is_le)
            link(nc.vector.tensor_reduce(tile_f[:, :], past, AX.X, ALU.add))
            link(nc.vector.tensor_scalar(tile_expert[:, :], tile_f[:, :], float(E - 1), None, ALU.min))
            dve.wait_ge(meta_loaded, 16)
            link(nc.vector.tensor_copy(read_f[:, :], meta_i[:, :, 0]))
            nc.vector.tensor_scalar(read_i[:, :], read_f[:, :], float(TOK - 1), None, ALU.min).then_inc(meta_ready, 1)

            def normalise_rows(i, u):
                if not exists(i, u):
                    return
                k = number(i, u)
                at_least(dve, gathered[u % OWN], 16 * (i + u // OWN + 1))
                at_least(dve, z_turned, k - 1)
                nc.vector.tensor_scalar(z_rows[u % 2], own_rows[u % OWN], meta[:, ds(k, 1), 2], meta[:, ds(k, 1), 3],
                                        ALU.subtract, ALU.mult).then_inc(z_ready, 1)

            def z_low_half(i, u):
                if not exists(i, u):
                    return
                at_least(dve, z_high, number(i, u) + 1)
                nc.vector.tensor_tensor(out=z_split[1][u % 2],
                                        in0=turned[u % 2][:, 0:D].rearrange("p (k t) -> p k t", t=P),
                                        in1=z_split[0][u % 2], op=ALU.subtract).then_inc(z_done, 1)

            def hidden_low(i, u):
                if not exists(i, u):
                    return
                at_least(dve, h_high, number(i, u) + 1)
                nc.vector.tensor_tensor(out=hidden_split[1][u % 2].rearrange("p k t -> p (k t)"), in0=hidden[u % 2],
                                        in1=hidden_split[0][u % 2].rearrange("p k t -> p (k t)"),
                                        op=ALU.subtract).then_inc(h_done, 1)

            def finish(i, u):
                k = number(i, u)
                e = dve.value_load(tile_expert[0:1, ds(k, 1)], min_val=0, max_val=E - 1)
                at_least(dve, down_full, k + 1)
                nc.vector.tensor_tensor(out=biased[u % 2], in0=down[u % 2][:, 0:D],
                                        in1=b2_all[:, ds(e, 1), :].rearrange("p o d -> p (o d)"),
                                        op=ALU.add).then_inc(bias_added, 1)
                at_least(dve, bias_added, k + 1)
                nc.vector.scalar_tensor_tensor(out=own_rows[u], in0=biased[u % 2], scalar=meta[:, ds(k, 1), 1],
                                               in1=own_rows[u], op0=ALU.mult, op1=ALU.add).then_inc(y_ready, 1)

            normalise_rows(0, 0)
            normalise_rows(0, 1)
            z_low_half(0, 0)
            z_low_half(0, 1)
            hidden_low(0, 0)

            def step(i, u):
                normalise_rows(i, u + 2)
                z_low_half(i, u + 2)
                hidden_low(i, u + 1)
                finish(i, u)

            tile_steps(dve, step)

        @block.tensor
        def _(pe):
            pe.wait_ge(consts, 1)
            pe.wait_ge(small_loaded, 64)
            nc.tensor.transpose(turned[0][:, 0:E * KF], b1_rows[:, :], ident[0:E * KF, 0:E * KF])\
                .then_inc(b1_turned, 1)

            def turn_group(i, par, again):
                g = 2 * i + par
                pe.wait_ge(g_rows, g + 1)
                if again:
                    pe.wait_ge(g_cols, g - 1)
                for q in range(GROUP):
                    for k in range(KD):
                        lo = (q * KD + k) * P
                        last = nc.tensor.transpose(up[par][:, lo:lo + P], z_group[par][:, q, k * P:k * P + P],
                                                   ident[:, :])
                last.then_inc(g_turned, 1)

            def gate(i, par, again):
                g = 2 * i + par
                pe.wait_ge(g_cols, g + 1)
                if again:
                    pe.wait_ge(g_taken, g - 1)
                for q in range(GROUP):
                    for k in range(KD):
                        last = nc.tensor.matmul(down[par][:, q * E:q * E + E], z_cols[:, q, k, :], wg[:, k, :],
                                                start=(k == 0), stop=(k == KD - 1))
                last.then_inc(g_logits, 1)

            def groups(i, again):
                for par in range(2):
                    turn_group(i, par, again)
                for par in range(2):
                    gate(i, par, again)

            groups(0, False)
            with pe.Fori(1, TT // GROUP // 2) as i:
                groups(i, True)
            pe.wait_ge(chosen_ready, 1)
            pe.wait_ge(b1_ready, 1)
            one_hot = chosen[:, :, :].rearrange("p t e -> p (t e)")
            nc.tensor.matmul(turned[0][:, 0:TT * E], upper[:, :], one_hot, start=True, stop=True)
            nc.tensor.matmul(turned[1][:, 0:TT * E], ones[:, :], one_hot, start=True, stop=True).then_inc(ranks, 1)
            pe.wait_ge(e_low, 2 * E)
            pe.wait_ge(meta_ready, 1)

            def turn(i, u):
                if not exists(i, u):
                    return
                k = number(i, u)
                at_least(pe, z_ready, k + 1)
                at_least(pe, z_done, k - 1)
                for c in range(KD):
                    last = nc.tensor.transpose(turned[u % 2][:, c * P:c * P + P], z_rows[u % 2][:, c * P:c * P + P],
                                               ident[:, :])
                last.then_inc(z_turned, 1)

            def upward(i, u):
                if not exists(i, u):
                    return
                k = number(i, u)
                e = pe.value_load(tile_expert[0:1, ds(k, 1)], min_val=0, max_val=E - 1)
                at_least(pe, z_done, k + 1)
                at_least(pe, silu_done, KF * (k - 1))
                for c in range(KF):
                    n = 0
                    for kk in range(KD):
                        for a, b in ((0, 0), (0, 1), (1, 0)):
                            lhs = w1[a][:, ds(e, 1), kk, c * P:c * P + P].rearrange("p o n -> p (o n)")
                            last = nc.tensor.matmul(up[u % 2][:, c * P:c * P + P], lhs, z_split[b][u % 2][:, kk, :],
                                                    start=(n == 0), stop=(n == 3 * KD - 1))
                            n += 1
                    if c % BANK == BANK - 1:
                        last.then_inc(up_full, 1)

            def downward(i, u):
                k = number(i, u)
                e = pe.value_load(tile_expert[0:1, ds(k, 1)], min_val=0, max_val=E - 1)
                at_least(pe, h_done, k + 1)
                at_least(pe, y_ready, k - 1)
                n = 0
                for kk in range(KF):
                    for a, b in ((0, 0), (0, 1), (1, 0)):
                        rhs = w2[b][:, ds(e, 1), kk, :].rearrange("p o n -> p (o n)")
                        last = nc.tensor.matmul(down[u % 2][:, 0:D], hidden_split[a][u % 2][:, kk, :], rhs,
                                                start=(n == 0), stop=(n == 3 * KF - 1))
                        n += 1
                last.then_inc(down_full, 1)

            turn(0, 0)
            upward(0, 0)
            turn(0, 1)

            def step(i, u):
                upward(i, u + 1)
                turn(i, u + 2)
                downward(i, u)

            tile_steps(pe, step)


def build_kernel(nc, x, ctx_1024, lmg, lmb, llg, llb, Wq, Wkv, Wout, Wg, bg, W1, b1, W2, b2, out):
    x2 = nc.dram_tensor("x2", (TOK, D), F32, kind="Internal").ap()
    listing = nc.dram_tensor("listing", (SORTED * P, 4), F32, kind="Internal").ap()
    attention(nc, x, ctx_1024, (llg, llb, lmg, lmb), Wq, Wkv, Wout, x2)
    experts(nc, x2, listing, Wg, bg, W1, b1, W2, b2, out)


_INS = ['x', 'ctx_1024', 'L0_xattn_ln_m_g', 'L0_xattn_ln_m_b', 'L0_xattn_ln_l_g', 'L0_xattn_ln_l_b',
        'L0_xattn_Wq', 'L0_xattn_Wkv', 'L0_xattn_Wout', 'L0_ffn_Wg', 'L0_ffn_bg', 'L0_ffn_W1', 'L0_ffn_b1',
        'L0_ffn_W2', 'L0_ffn_b2']


def kernel(**inputs):
    import numpy as np
    import concourse.bacc as bacc
    from concourse.bass_utils import run_bass_kernel_spmd

    nc = bacc.Bacc("TRN2", target_bir_lowering=False, num_devices=1)
    arrays, args = {}, []
    for name in _INS:
        a = np.ascontiguousarray(inputs[name])
        arrays["in_" + name] = a
        args.append(nc.dram_tensor("in_" + name, a.shape, mybir.dt.from_np(a.dtype), kind="ExternalInput").ap())
    out = nc.dram_tensor("out", (B, N, D), F32, kind="ExternalOutput").ap()
    build_kernel(nc, *args, out)
    result = run_bass_kernel_spmd(nc, [arrays], core_ids=[0])
    return result.results[0]["out"]
```

```python
import concourse.bass as bass
from concourse import mybir
from contextlib import ExitStack

F32 = mybir.dt.float32
F16 = mybir.dt.float16
I32 = mybir.dt.int32
ALU = mybir.AluOpType
ACT = mybir.ActivationFunctionType
AX = mybir.AxisListType
ds = bass.ds

P = 128
B, N, D = 4, 1024, 256
C = 154
H, DH = 16, 64
INNER = H * DH
E, F = 8, 1024
KD = D // P
NT = N // P
KEYS = N + C
JT = 10
TAIL = C - P
PAIRS = H // 2
CT = B * C
CTILES = -(-CT // P)
TOK = B * N
TT = TOK // P
EPS = 1e-5
SCALE = float(DH) ** -0.5
HALF = 512
SORTED = TT + E
NOBODY = 2 * TOK
STATS = 6


def key_rows(j):
    return TAIL if j == JT - 1 else P


MAX_TAILS = [(0, 1, 2), (3, 4, 5), (6, 7)]
VALUE_TILES = [(0, 1, 2), (3, 4, 5), (6, 7), (8, 9)]
SLOTS = 4 * JT
QK = 3
AHEAD_STEPS = 2
SPLITS = 5

ROWS_SLOTS = (2, 3)
MAX_SLOTS = [s for s in range(SLOTS) if s % 4 != 2 and s not in (0, 3)]
TURN_SLOT = 28
VALUE_SLOTS = (29, 30, 31, 33)
QK_SLOTS = (34, 36, 38)


def schedule(name):
    at = {s: [] for s in range(SLOTS)}
    if name == "start":
        at[0] += [("qk", c, 0, 0) for c in range(QK)]
    else:
        for half, s in enumerate(ROWS_SLOTS):
            at[s].append(("rows", half))
    maxima = [("max", t, c) for t in range(NT) for c in range(2)] + [("tail", g) for g in range(len(MAX_TAILS))]
    for s, chunk in zip(MAX_SLOTS, maxima):
        at[s].append(chunk)
    at[TURN_SLOT].append(("turn",))
    if name != 1:
        for g, s in enumerate(VALUE_SLOTS):
            at[s].append(("v", g))
    for c, s in enumerate(QK_SLOTS):
        at[s].append(("qk", c, 1 if name == "start" else 1 - name, 1))
    n, out = 0, {}
    for s in range(SLOTS):
        out[s] = []
        for chunk in at[s]:
            out[s].append((n, chunk))
            n += 1
    return out, n


AHEAD, AMOUNT = {}, {}
for name in (1, 0, "start"):
    AHEAD[name], AMOUNT[name] = schedule(name)
N_PAIR = AMOUNT[0] + AMOUNT[1]
PARITY = {"start": 0, 1: AMOUNT["start"] % 2, 0: (AMOUNT["start"] + AMOUNT[1]) % 2}
TURN = {name: max(n for c in at.values() for n, k in c if k[0] == "turn") for name, at in AHEAD.items()}
LAST_VALUES = {name: max(n for c in AHEAD[name].values() for n, k in c if k[0] == "v") for name in (0, "start")}
assert N_PAIR % 2 == 0


class Steps:

    def __init__(self, sem, start):
        self.sem, self.start, self.n = sem, start, 0

    def mark(self, ins):
        ins.then_inc(self.sem, 1)
        self.n += 1

    def reached(self):
        return self.start + self.n


def attention(nc, x, ctx_in, ln, Wq, Wkv, Wout, x2_dram):
    x_rows = x.rearrange("b (t p) d -> b p t d", p=P)
    ctx_rows = ctx_in.rearrange("b c d -> (b c) d")
    x2_rows = x2_dram.rearrange("(b t p) d -> b t p d", b=B, p=P)
    weights = [Wq.rearrange("(k p) n -> p k n", p=P),
               Wkv[:, 0:INNER].rearrange("(k p) n -> p k n", p=P),
               Wkv[:, INNER:2 * INNER].rearrange("(k p) n -> p k n", p=P),
               Wout.rearrange("(k p) n -> p k n", p=P)]

    stack = ExitStack()
    with stack:
        def sb(name, shape, dt):
            return stack.enter_context(nc.sbuf_tensor(name, shape, dt))

        def pb(name, shape, dt):
            return stack.enter_context(nc.psum_tensor(name, shape, dt))

        def sem(name):
            return stack.enter_context(nc.semaphore(name))

        ident = sb("ident", [P, P], F32)
        ln_rows = sb("ln_rows", [8, P], F32)
        ln_cols = sb("ln_cols", [P, 8], F32)
        wqk = [sb(f"wqk{i}", [P, KD, H, 2, DH], F16) for i in range(2)]
        wv = [sb(f"wv{i}", [P, KD, INNER], F16) for i in range(2)]
        wo = [sb(f"wo{i}", [P, INNER // P, D], F16) for i in range(2)]
        zx = [sb(f"zx{i}", [P, KD, TOK], F16) for i in range(2)]
        zc = [sb(f"zc{i}", [P, KD, CT], F16) for i in range(2)]
        q_both = [sb(f"q_both{i}", [P, N], F16) for i in range(2)]
        k_high = [sb(f"k_high{i}", [P, KEYS], F16) for i in range(2)]
        q_max = [sb(f"q_max{i}", [DH + 1, N], F16) for i in range(2)]
        k_low = [sb(f"k_low{i}", [DH + 1, KEYS], F16) for i in range(2)]
        max_row = [sb(f"max_row{i}", [NT, P], F16) for i in range(2)]
        max_parts = sb("max_parts", [P, NT, 3], F32)
        neg_max = sb("neg_max", [P, NT], F32)
        probs = [sb(f"probs{i}", [P, N], F32) for i in range(2)]
        probs_split = [[sb(f"probs_split{h}{i}", [P, N], F16) for i in range(SPLITS)] for h in range(2)]
        values = [sb(f"values{i}", [P, JT, 3, DH], F16) for i in range(2)]
        values_pair = sb("values_pair", [P, JT, 2, 2, DH], F16)
        head_out = sb("head_out", [P, N], F32)
        recip = sb("recip", [P, NT], F32)
        att_rows = sb("att_rows", [P, NT, H, DH], F32)
        att_cols = [[sb(f"att_cols{h}{i}", [P, INNER // P, P], F16) for i in range(2)] for h in range(2)]
        x_res = [sb(f"x_res{i}", [P, D], F32) for i in range(2)]
        x2_tile = [sb(f"x2_tile{i}", [P, D], F32) for i in range(2)]
        stats = sb("stats", [P, NT, STATS], F32)
        mean_var = sb("mean_var", [P, NT, 2], F32)
        std = sb("std", [P, NT], F32)
        rstd = sb("rstd", [P, NT], F32)
        eps_col = sb("eps_col", [P, 1], F32)
        staging = att_rows[:, :, :, :].rearrange("p t h d -> p (t h d)")
        w_stage = [staging[:, i * KD * N:(i + 1) * KD * N] for i in range(2)]
        x_stage = [staging[:, (i + 2) * KD * N:(i + 3) * KD * N].rearrange("p (t d) -> p t d", d=D) for i in range(2)]

        score = [pb(f"score{i}", [P, N], F32) for i in range(2)]
        acc = pb("acc", [P, N], F32)
        aux = [pb(f"aux{i}", [P, HALF], F32) for i in range(2)]

        pool_turns = sem("pool_turns")
        dve_turns = sem("dve_turns")
        ident_ready = sem("ident_ready")
        ln_loaded = sem("ln_loaded")
        ln_turned = sem("ln_turned")
        ln_ready = sem("ln_ready")
        w_loaded = [sem(f"w_loaded{i}") for i in range(2)]
        w_high = sem("w_high")
        w_low = sem("w_low")
        x_loaded = [sem(f"x_loaded{i}") for i in range(2)]
        z_step = sem("z_step")
        var_ready = sem("var_ready")
        std_ready = sem("std_ready")
        z_ready = sem("z_ready")
        z_turned = sem("z_turned")
        z_affine = sem("z_affine")
        z_high = sem("z_high")
        z_low = sem("z_low")
        ones_ready = sem("ones_ready")
        aux_full = sem("aux_full")
        aux_high = sem("aux_high")
        aux_done = sem("aux_done")
        q_copied = sem("q_copied")
        max_ready = sem("max_ready")
        max_sent = sem("max_sent")
        values_moved = [sem("even_values"), sem("odd_values")]
        score_full = sem("score_full")
        exp_done = sem("exp_done")
        values_high = sem("values_high")
        act_turns = sem("act_turns")
        probs_high = sem("probs_high")
        probs_low = sem("probs_low")
        av_done = sem("av_done")
        acc_copied = sem("acc_copied")
        recip_done = sem("recip_done")
        att_turned = sem("att_turned")
        att_high = sem("att_high")
        att_low = sem("att_low")
        res_loaded = [sem(f"res_loaded{i}") for i in range(2)]
        x2_stored = [sem(f"x2_stored{i}") for i in range(2)]

        C_ROWS = [min(P, CT - t * P) for t in range(CTILES)]
        C_HALVES = [C_ROWS[0:4], C_ROWS[4:]]
        X_HALVES = [[P] * 4, [P] * 4]

        def beside_even(n, outs):
            return n * N_PAIR + outs * NT + AMOUNT["start"]

        def beside_odd(n, outs):
            return n * N_PAIR + outs * NT + AMOUNT["start"] + AMOUNT[1]

        def out_base(b):
            return beside_odd((b + 1) * PAIRS, b)

        LAST_OUT = beside_even(B * PAIRS, B - 1)

        def aux_bank(name, place):
            return aux[(PARITY[name] + place) % 2]

        OUT_PARITY = PARITY[0]
        FINAL_PARITY = PARITY[1]

        def value_groups(g):
            js = VALUE_TILES[g]
            return [(js, P)] if js[-1] < JT - 1 else [(js[:-1], P), (js[-1:], TAIL)]

        def value_bank(bank, g):
            return bank[:, 0:len(VALUE_TILES[g]) * P].rearrange("p (j c d) -> p j c d", c=2, d=DH)

        def whole_program(loop, head, put_out, finish):
            head(0, 0, 0, 0, 0)

            def rest(b):
                head(1, b * PAIRS, b, 0, b)
                with loop.Fori(1, PAIRS) as hp:
                    for par in range(2):
                        head(par, b * PAIRS + hp, b, hp, b)

            with loop.Fori(0, B - 1) as b:
                rest(b)
                head(0, b * PAIRS + PAIRS, b + 1, 0, b)
                put_out(b, out_base(b), OUT_PARITY)
            rest(B - 1)
            finish()

        block = stack.enter_context(nc.Block())

        @block.sync
        def _(sp):
            for i, v in enumerate(ln):
                sp.dma_start(ln_rows[2 * i:2 * i + 2, :], v.rearrange("(k p) -> k p", p=P)).then_inc(ln_loaded, 16)
            full = CTILES - 1
            sp.dma_start(x_stage[0][:, 0:full, :], ctx_rows[0:full * P, :].rearrange("(t p) d -> p t d", p=P))\
                .then_inc(x_loaded[0], 16)
            sp.dma_start(x_stage[0][0:C_ROWS[full], full, :], ctx_rows[full * P:CT, :]).then_inc(x_loaded[0], 16)
            for i in range(2):
                sp.dma_start(w_stage[i].rearrange("p (k n) -> p k n", k=KD), weights[i]).then_inc(w_loaded[i], 16)
            for b in range(B):
                if b >= 1:
                    sp.wait_ge(z_turned, 2 * b)
                i = (b + 1) % 2
                sp.dma_start(x_stage[i], x_rows[b]).then_inc(x_loaded[i], 16)
                if b < 2:
                    sp.wait_ge(w_low, b + 1)
                    sp.dma_start(w_stage[b].rearrange("p (k n) -> p k n", k=weights[b + 2].shape[1]),
                                 weights[b + 2]).then_inc(w_loaded[b], 16)

            def send_max(sent, buf):
                sp.wait_ge(aux_done, sent)
                sp.dma_start(q_max[buf][DH:DH + 1, :], max_row[buf][:, :]).then_inc(max_sent, 16)

            def head(par, n, b, hp, outs):
                base = beside_odd(n, outs) if par else beside_even(n, outs)
                send_max(base + TURN[1 - par] + 1, 1 - par)

            def put_out(b, base, parity):
                for t in range(NT):
                    if t >= 2:
                        sp.wait_ge(aux_done, base + t - 1)
                    sp.dma_start(x_res[t % 2][:, :], x_rows[ds(b, 1), :, t, :].rearrange("o p d -> (o p) d"))\
                        .then_inc(res_loaded[t % 2], 16)
                    if t >= 1:
                        sp.wait_ge(aux_done, base + t)
                        sp.dma_start(x2_rows[ds(b, 1), t - 1, :, :].rearrange("o p d -> (o p) d"),
                                     x2_tile[(t - 1) % 2][:, :]).then_inc(x2_stored[(t - 1) % 2], 16)
                sp.wait_ge(aux_done, base + NT)
                sp.dma_start(x2_rows[ds(b, 1), NT - 1, :, :].rearrange("o p d -> (o p) d"),
                             x2_tile[(NT - 1) % 2][:, :]).then_inc(x2_stored[(NT - 1) % 2], 16)

            send_max(TURN["start"] + 1, 0)
            whole_program(sp, head, put_out, lambda: put_out(B - 1, LAST_OUT + 2, FINAL_PARITY))
            for i in range(2):
                sp.wait_ge(x2_stored[i], 16 * TT // 2)

        @block.gpsimd
        def _(pool):
            nc.gpsimd.memset(ident[:, :], 0.0).then_inc(ident_ready, 1)
            pool.wait_ge(ident_ready, 1)
            nc.gpsimd.affine_select(out=ident[:, :], in_=ident[:, :], compare_op=ALU.not_equal, fill=1.0,
                                    base=0, pattern=[[-1, P]], channel_multiplier=1).then_inc(ident_ready, 1)

            for i in range(2):
                pool.wait_ge(w_high, i + 1)
                nc.gpsimd.tensor_tensor(out=wqk[1][:, :, :, i, :].rearrange("p k h d -> p (k h) d"),
                                        in0=w_stage[i].rearrange("p (k d) -> p k d", d=DH),
                                        in1=wqk[0][:, :, :, i, :].rearrange("p k h d -> p (k h) d"),
                                        op=ALU.subtract).then_inc(w_low, 1)
            for i, w in enumerate((wv, wo)):
                pool.wait_ge(w_high, i + 3)
                nc.gpsimd.tensor_tensor(out=w[1][:, :, :].rearrange("p k n -> p (k n)"), in0=w_stage[i],
                                        in1=w[0][:, :, :].rearrange("p k n -> p (k n)"), op=ALU.subtract)\
                    .then_inc(w_low, 1)

            def copy_q(idx, buf):
                pool.wait_ge(aux_high, idx * QK + 2)
                pool.sem_inc(pool_turns, 1)
                nc.gpsimd.tensor_copy(q_max[buf][0:DH, :], q_both[buf][0:DH, :]).then_inc(q_copied, 1)
                pool.wait_ge(q_copied, idx + 1)
                pool.sem_inc(pool_turns, 1)

            def move_values(par, count):
                nc.gpsimd.tensor_copy(values[par][:, :, 0:3:2, :], values_pair[:, :, par, :, :])\
                    .then_inc(values_moved[par], 1)
                pool.wait_ge(values_moved[par], count)
                pool.sem_inc(pool_turns, 1)

            def head(par, n, b, hp, outs):
                if par == 0:
                    if not isinstance(n, int):
                        pool.wait_ge(av_done, SPLITS + 2 * JT * n)
                        pool.sem_inc(pool_turns, 1)
                    move_values(1, n + 1)
                    copy_q(2 * n + 2, 0)
                else:
                    pool.wait_ge(aux_done, beside_odd(n, outs) + LAST_VALUES[0] + 1)
                    pool.wait_ge(av_done, SPLITS + 2 * JT * n + JT)
                    pool.sem_inc(pool_turns, 1)
                    move_values(0, n + 2)
                    copy_q(2 * n + 3, 1)

            copy_q(0, 0)
            pool.wait_ge(aux_done, LAST_VALUES["start"] + 1)
            move_values(0, 1)
            copy_q(1, 1)
            whole_program(pool, head, lambda b, base, parity: None, lambda: None)

        @block.scalar
        def _(act):
            for i in range(2):
                act.wait_ge(w_loaded[i], 16)
                nc.scalar.activation(wqk[0][:, :, :, i, :].rearrange("p k h d -> p (k h) d"),
                                     w_stage[i].rearrange("p (k d) -> p k d", d=DH), ACT.Copy).then_inc(w_high, 1)

            def late_weight(i):
                w = (wv, wo)[i]
                act.wait_ge(w_loaded[i], 32)
                nc.scalar.activation(w[0][:, :, :].rearrange("p k n -> p (k n)"), w_stage[i], ACT.Copy)\
                    .then_inc(w_high, 1)

            def root(n, tiles):
                act.wait_ge(var_ready, n)
                nc.scalar.activation(std[:, 0:tiles], mean_var[:, 0:tiles, 1], ACT.Sqrt, bias=eps_col[:, :])\
                    .then_inc(std_ready, 1)

            def high_half(done, i, dst, cols):
                act.wait_ge(z_affine, done)
                src = probs[i][:, :].rearrange("p (k c) -> p k c", k=KD)[:, :, 0:cols]
                nc.scalar.activation(dst, src, ACT.Copy).then_inc(z_high, 1)

            act.wait_ge(ones_ready, 1)
            root(1, CTILES)
            for i, half in enumerate(C_HALVES):
                high_half(i + 1, i, zc[0][:, :, HALF * i:HALF * i + sum(half)], sum(half))
            with act.Fori(0, B) as b:
                root(2 * b + 2, NT)
                root(2 * b + 3, NT)
                for i in range(2):
                    high_half(2 * b + 2 + i + 1, i, zx[0][:, :, ds(b * N + i * HALF, HALF)], HALF)
            late_weight(0)
            late_weight(1)

            def high_parts(name, base, n, slots):
                for s in slots:
                    for place, chunk in AHEAD[name][s]:
                        bank = aux_bank(name, place)
                        if chunk[0] == "qk":
                            act.wait_ge(aux_full, base + place + 1)
                            of = chunk[2]
                            lo = chunk[1] * HALF
                            hi = min(lo + HALF, KEYS)
                            for half in range(2):
                                last = nc.scalar.activation(k_high[of][half * DH:half * DH + DH, lo:hi],
                                                            bank[DH:P, 0:hi - lo], ACT.Copy)
                            if lo < N:
                                last = nc.scalar.activation(q_both[of][0:DH, lo:hi], bank[0:DH, 0:hi - lo], ACT.Copy)
                            last.then_inc(aux_high, 1)
                        elif chunk[0] == "v":
                            act.wait_ge(aux_full, base + place + 1)
                            if name != "start" and chunk[1] == 0:
                                act.wait_ge(values_moved[1], n + 1)
                            for js, r in value_groups(chunk[1]):
                                both = value_bank(bank, chunk[1])
                                a = js[0] - VALUE_TILES[chunk[1]][0]
                                last = nc.scalar.activation(
                                    values_pair[0:r, js[0]:js[-1] + 1, :, 0, :],
                                    both[0:r, a:a + len(js), :, :], ACT.Copy)
                            last.then_inc(values_high, 1)

            def exponent(tile, j):
                r = key_rows(j)
                act.wait_ge(score_full, tile + 1)
                act.wait_ge(probs_low, tile + 1)
                nc.scalar.activation(probs[j % 2][0:r, :], score[j % 2][0:r, :], ACT.Exp, scale=SCALE)\
                    .then_inc(exp_done, 1)

            def probs_high_half(tile, j):
                r = key_rows(j)
                act.wait_ge(exp_done, tile + 3)
                act.wait_ge(av_done, tile + 1)
                nc.scalar.activation(probs_split[0][j % SPLITS][0:r, :], probs[j % 2][0:r, :], ACT.Copy)\
                    .then_inc(probs_high, 1)

            def head(par, n, b, hp, outs):
                g = 2 * n + par
                nxt = 1 - par
                base = beside_odd(n, outs) if par else beside_even(n, outs)
                for j in range(JT):
                    high_parts(nxt, base, n, (4 * j, 4 * j + 1))
                    exponent(JT * g + j + AHEAD_STEPS, (j + AHEAD_STEPS) % JT)
                    probs_high_half(JT * g + j + AHEAD_STEPS, (j + AHEAD_STEPS) % JT)
                    high_parts(nxt, base, n, (4 * j + 2, 4 * j + 3))
                act.wait_ge(av_done, JT * g + JT + SPLITS)
                nc.scalar.activation(head_out[:, :], acc[:, :], ACT.Copy).then_inc(acc_copied, 1)

            def put_out(b, base, parity):
                for t in range(NT):
                    act.wait_ge(att_turned, b * NT + t + 1)
                    act.sem_inc(act_turns, 1)
                    nc.scalar.activation(att_cols[0][t % 2][:, :, :].rearrange("p k t -> p (k t)"), acc[:, :],
                                         ACT.Copy).then_inc(att_high, 1)

            high_parts("start", 0, 0, range(SLOTS))
            for j in range(AHEAD_STEPS):
                exponent(j, j)
                probs_high_half(j, j)
            whole_program(act, head, put_out, lambda: put_out(B - 1, 0, 0))

        @block.vector
        def _(dve):
            for i in range(2):
                nc.vector.memset(values[i][:, :, 1, :], 1.0)
                nc.vector.memset(k_low[i][DH:DH + 1, :], 1.0)
            nc.vector.memset(values_pair[:, :, :, :, :], 0.0)
            nc.vector.memset(head_out[:, :], 1.0)
            nc.vector.memset(eps_col[:, :], EPS).then_inc(ones_ready, 1)
            nc.vector.memset(mean_var[:, :, :], 1.0).then_inc(z_step, 1)
            dve.wait_ge(z_step, 1)
            dve.wait_ge(ln_turned, 1)
            nc.vector.tensor_copy(ln_cols[:, :], aux[0][:, 0:8]).then_inc(ln_ready, 1)
            dve.wait_ge(ln_ready, 1)

            def normalise(rows, tiles, steps, roots):
                for t, r in enumerate(tiles):
                    last = nc.vector.bn_stats(stats[0:r, t, :], rows[0:r, t, :])
                steps.mark(last)
                dve.wait_ge(z_step, steps.reached())
                dve.sem_inc(dve_turns, 1)
                for t, r in enumerate(tiles):
                    last = nc.vector.bn_aggr(mean_var[0:r, t, :], stats[0:r, t, :])
                last.then_inc(var_ready, 1)
                dve.wait_ge(std_ready, roots)
                steps.mark(nc.vector.reciprocal(rstd[:, 0:len(tiles)], std[:, 0:len(tiles)]))
                dve.wait_ge(z_step, steps.reached())
                for t, r in enumerate(tiles):
                    last = nc.vector.tensor_scalar(rows[0:r, t, :], rows[0:r, t, :], mean_var[0:r, t, 0:1],
                                                   rstd[0:r, t:t + 1], ALU.subtract, ALU.mult)
                return last

            def split(group, halves, param, dst):
                for i, cols in enumerate(halves):
                    dve.wait_ge(z_turned, 2 * group + i + 1)
                    for k in range(KD):
                        last = nc.vector.tensor_scalar(probs[i][:, k * HALF:k * HALF + cols],
                                                       score[i][:, k * HALF:k * HALF + cols],
                                                       ln_cols[:, param + k:param + k + 1],
                                                       ln_cols[:, param + 2 + k:param + 3 + k], ALU.mult, ALU.add)
                    last.then_inc(z_affine, 1)
                for i, cols in enumerate(halves):
                    dve.wait_ge(z_high, 2 * group + i + 1)
                    nc.vector.tensor_tensor(out=dst(1, i, cols),
                                            in0=probs[i][:, :].rearrange("p (k c) -> p k c", k=KD)[:, :, 0:cols],
                                            in1=dst(0, i, cols), op=ALU.subtract).then_inc(z_low, 1)

            steps = Steps(z_step, 1)
            dve.wait_ge(x_loaded[0], 32)
            normalise(x_stage[0], C_ROWS, steps, 1).then_inc(z_ready, 1)
            split(0, [sum(h) for h in C_HALVES], 4, lambda w, i, cols: zc[w][:, :, HALF * i:HALF * i + cols])
            CTX_STEPS, X_STEPS = steps.reached(), 5
            with dve.Fori(0, B // 2) as i:
                for odd in range(2):
                    b = 2 * i + odd
                    steps = Steps(z_step, CTX_STEPS + X_STEPS * b)
                    if odd:
                        dve.wait_ge(x_loaded[0], 16 * i + 48)
                    else:
                        dve.wait_ge(x_loaded[1], 16 * i + 16)
                    rows = x_stage[1 - odd]
                    steps.mark(normalise(rows, [P] * NT, steps, 2 * b + 2))
                    dve.wait_ge(z_step, steps.reached())
                    normalise(rows, [P] * NT, steps, 2 * b + 3).then_inc(z_ready, 1)
                    assert steps.n == X_STEPS
                    split(b + 1, [HALF, HALF], 0, lambda w, i, cols: zx[w][:, :, ds(b * N + i * HALF, HALF)])

            def consume(name, idx, base, n, slots, hp=None):
                par = 1 if name == 1 else 0
                for s in slots:
                    for place, chunk in AHEAD[name][s]:
                        bank = aux_bank(name, place)
                        kind = chunk[0]
                        if kind == "qk":
                            dve.wait_ge(aux_high, QK * (idx + chunk[3]) + chunk[1] + 1)
                            of = chunk[2]
                            lo = chunk[1] * HALF
                            hi = min(lo + HALF, KEYS)
                            if lo < N:
                                nc.vector.tensor_tensor(out=q_both[of][DH:P, lo:hi], in0=bank[0:DH, 0:hi - lo],
                                                        in1=q_both[of][0:DH, lo:hi], op=ALU.subtract)
                            nc.vector.tensor_tensor(out=k_low[of][0:DH, lo:hi], in0=bank[DH:P, 0:hi - lo],
                                                    in1=k_high[of][DH:P, lo:hi], op=ALU.subtract)\
                                .then_inc(aux_done, 1)
                            continue
                        if kind == "v":
                            dve.wait_ge(values_high, len(VALUE_TILES) * n + chunk[1] + 1)
                            for js, r in value_groups(chunk[1]):
                                both = value_bank(bank, chunk[1])
                                a = js[0] - VALUE_TILES[chunk[1]][0]
                                last = nc.vector.tensor_tensor(out=values_pair[0:r, js[0]:js[-1] + 1, :, 1, :],
                                                               in0=both[0:r, a:a + len(js), :, :],
                                                               in1=values_pair[0:r, js[0]:js[-1] + 1, :, 0, :],
                                                               op=ALU.subtract)
                            last.then_inc(aux_done, 1)
                            continue
                        dve.wait_ge(aux_full, base + place + 1)
                        if kind == "max":
                            _, t, c = chunk
                            nc.vector.tensor_reduce(max_parts[:, t, c:c + 1], bank[:, :], AX.X, ALU.max)\
                                .then_inc(aux_done, 1)
                        elif kind == "tail":
                            ts = MAX_TAILS[chunk[1]]
                            nc.vector.tensor_reduce(max_parts[:, ts[0]:ts[-1] + 1, 2],
                                                    bank[:, 0:C * len(ts)].rearrange("p (t c) -> p t c", c=C),
                                                    AX.X, ALU.max).then_inc(aux_done, 1)
                            if chunk[1] == len(MAX_TAILS) - 1:
                                dve.wait_ge(aux_done, base + place + 1)
                                nc.vector.tensor_reduce(neg_max[:, :], max_parts[:, :, :], AX.X, ALU.max,
                                                        negate=True).then_inc(max_ready, 1)
                        elif kind == "turn":
                            nc.vector.tensor_copy(max_row[par][:, :], bank[0:NT, 0:P]).then_inc(aux_done, 1)
                        else:
                            take_rows(bank, chunk[1], hp, 2 * idx - 2 + chunk[1] + 1)

            def take_rows(bank, half, head_col, step):
                t = slice(half * NT // 2, (half + 1) * NT // 2)
                turned = bank[:, 0:(NT // 2) * (DH + 1)].rearrange("p (t c) -> p t c", c=DH + 1)
                nc.vector.reciprocal(recip[:, t], turned[:, :, DH]).then_inc(recip_done, 1)
                dve.wait_ge(recip_done, step)
                nc.vector.tensor_tensor(
                    out=att_rows[:, t, ds(head_col, 1), :].rearrange("p t o d -> p t (o d)"),
                    in0=turned[:, :, 0:DH], in1=recip[:, t].unsqueeze(2).to_broadcast([P, NT // 2, DH]),
                    op=ALU.mult).then_inc(aux_done, 1)

            def probs_low_half(tile, j):
                r = key_rows(j)
                dve.wait_ge(probs_high, tile + 1)
                nc.vector.tensor_tensor(out=probs_split[1][j % SPLITS][0:r, :], in0=probs[j % 2][0:r, :],
                                        in1=probs_split[0][j % SPLITS][0:r, :], op=ALU.subtract).then_inc(probs_low, 1)

            def head(par, n, b, hp, outs):
                g = 2 * n + par
                nxt = 1 - par
                base = beside_odd(n, outs) if par else beside_even(n, outs)
                before = 2 * hp if par else ((2 * hp + H - 1) & (H - 1) if not isinstance(hp, int)
                                             else (2 * hp + H - 1) % H)
                for j in range(JT):
                    consume(nxt, g + 1, base, n + 1, (4 * j, 4 * j + 1), before)
                    probs_low_half(JT * g + j + 1, (j + 1) % JT)
                    consume(nxt, g + 1, base, n + 1, (4 * j + 2, 4 * j + 3), before)

            def put_out(b, base, parity):
                for t in range(NT):
                    dve.wait_ge(att_high, b * NT + t + 1)
                    nc.vector.tensor_tensor(out=att_cols[1][t % 2][:, :, :].rearrange("p k t -> p (k t)"),
                                            in0=acc[:, :],
                                            in1=att_cols[0][t % 2][:, :, :].rearrange("p k t -> p (k t)"),
                                            op=ALU.subtract).then_inc(att_low, 1)
                    if t >= 1:
                        add_residual(b, base, parity, t - 1)
                add_residual(b, base, parity, NT - 1)
                for i in range(2):
                    dve.wait_ge(x2_stored[i], 16 * (b + 1) * (NT // 2))
                    dve.sem_inc(dve_turns, 1)

            def add_residual(b, base, parity, t):
                dve.wait_ge(aux_full, base + t + 1)
                dve.wait_ge(res_loaded[t % 2], 16 * (b * (NT // 2) + t // 2 + 1))
                if t >= 2:
                    dve.wait_ge(x2_stored[t % 2], 16 * (b * (NT // 2) + t // 2))
                nc.vector.tensor_tensor(out=x2_tile[t % 2][:, :], in0=aux[(parity + t) % 2][:, 0:D],
                                        in1=x_res[t % 2][:, :], op=ALU.add).then_inc(aux_done, 1)

            def finish():
                for half in range(2):
                    dve.wait_ge(aux_full, LAST_OUT + half + 1)
                    take_rows(aux[(FINAL_PARITY + half) % 2], half, H - 1, 2 * (2 * B * PAIRS) + half + 1)
                put_out(B - 1, LAST_OUT + 2, FINAL_PARITY)

            consume("start", 0, 0, 0, range(SLOTS))
            probs_low_half(0, 0)
            whole_program(dve, head, put_out, finish)

        @block.tensor
        def _(pe):
            pe.sem_inc(av_done, SPLITS)
            pe.sem_inc(exp_done, 2)
            pe.sem_inc(probs_low, 2)
            pe.sem_inc(acc_copied, 1)
            pe.wait_ge(ident_ready, 2)
            pe.wait_ge(ln_loaded, 64)
            nc.tensor.transpose(aux[0][:, 0:8], ln_rows[:, :], ident[0:8, 0:8]).then_inc(ln_turned, 1)

            def turn(rows, group, halves):
                pe.wait_ge(z_ready, group + 1)
                t = 0
                for i, half in enumerate(halves):
                    if not isinstance(group, int) or group >= 1:
                        pe.wait_ge(z_affine, 2 * group + i - 1)
                    for q, r in enumerate(half):
                        for k in range(KD):
                            lo = k * HALF + q * P
                            last = nc.tensor.transpose(score[i][:, lo:lo + r], rows[0:r, t, k * P:k * P + P],
                                                       ident[0:r, 0:r])
                        t += 1
                    last.then_inc(z_turned, 1)

            turn(x_stage[0], 0, C_HALVES)
            with pe.Fori(0, B // 2) as i:
                turn(x_stage[1], 2 * i + 1, X_HALVES)
                turn(x_stage[0], 2 * i + 2, X_HALVES)
            pe.wait_ge(z_low, 2 * (B + 1))
            pe.wait_ge(w_low, 4)
            pe.wait_ge(ones_ready, 1)

            def summed(out, pairs):
                for i, (a, b) in enumerate(pairs):
                    last = nc.tensor.matmul(out, a, b, start=(i == 0), stop=(i == len(pairs) - 1))
                return last

            def transposed_rows(bank, half):
                for i in range(NT // 2):
                    t = half * (NT // 2) + i
                    last = nc.tensor.transpose(bank[:, i * (DH + 1):(i + 1) * (DH + 1)],
                                               head_out[0:DH + 1, t * P:t * P + P], ident[0:DH + 1, 0:DH + 1])
                return last

            def produce(name, idx, base, batch, pair, slots):
                par = 1 if name == 1 else 0
                for s in slots:
                    for place, chunk in AHEAD[name][s]:
                        bank = aux_bank(name, place)
                        if not (isinstance(base, int) and base + place < 2):
                            pe.wait_ge(aux_done, base + place - 1)
                        kind = chunk[0]
                        if kind == "qk":
                            c = chunk[1]
                            if c < 2:
                                cols = HALF
                                rhs = [[z[:, k, ds(batch * N + c * HALF, HALF)] for z in zx] for k in range(KD)]
                            else:
                                cols = C
                                rhs = [[z[:, k, ds(batch * C, C)] for z in zc] for k in range(KD)]
                            pairs = []
                            for k in range(KD):
                                lhs = [m[:, k, ds(2 * pair + chunk[2], 1), :, :].rearrange("p o c d -> p (o c d)") for m in wqk]
                                pairs += [(lhs[0], rhs[k][0]), (lhs[0], rhs[k][1]), (lhs[1], rhs[k][0])]
                            last = summed(bank[:, 0:cols], pairs)
                        elif kind == "max":
                            _, t, c = chunk
                            if t == 0 and c == 0:
                                pe.wait_ge(aux_done, base + (QK if name == "start" else 0))
                            last = summed(bank[:, :], [(q_both[par][:, t * P:t * P + P],
                                                        k_high[par][:, c * HALF:c * HALF + HALF])])
                        elif kind == "tail":
                            for i, t in enumerate(MAX_TAILS[chunk[1]]):
                                last = summed(bank[:, i * C:i * C + C],
                                              [(q_both[par][:, t * P:t * P + P], k_high[par][:, N:KEYS])])
                        elif kind == "turn":
                            pe.wait_ge(max_ready, idx + 1)
                            last = nc.tensor.transpose(bank[0:NT, 0:P], neg_max[:, :], ident[:, :])
                        elif kind == "rows":
                            if chunk[1] == 0:
                                pe.wait_ge(acc_copied, idx)
                            last = transposed_rows(bank, chunk[1])
                        else:
                            js = VALUE_TILES[chunk[1]]
                            for i, j in enumerate(js):
                                r = key_rows(j)
                                pairs = []
                                for k in range(KD):
                                    if j < NT:
                                        lhs = [z[:, k, ds(batch * N + j * P, r)] for z in zx]
                                    else:
                                        lhs = [z[:, k, ds(batch * C + (j - NT) * P, r)] for z in zc]
                                    rhs = [m[:, k, ds(pair * P, P)] for m in wv]
                                    pairs += [(lhs[0], rhs[0]), (lhs[0], rhs[1]), (lhs[1], rhs[0])]
                                last = summed(bank[0:r, i * P:i * P + P], pairs)
                        last.then_inc(aux_full, 1)

            def scores(name, idx, base, tile, j, i):
                par = 1 if name == 1 else 0
                if i == 0:
                    pe.wait_ge(exp_done, tile + 1)
                    if j == 0:
                        pe.wait_ge(aux_done, base + TURN[name] + 1)
                        pe.wait_ge(q_copied, idx + 1)
                        pe.wait_ge(max_sent, 16 * (idx + 1))
                r = key_rows(j)
                cols = slice(i * HALF, i * HALF + HALF)
                last = summed(score[j % 2][0:r, cols], [(k_high[par][:, j * P:j * P + r], q_both[par][:, cols]),
                                                        (k_low[par][:, j * P:j * P + r], q_max[par][:, cols])])
                if i == 1:
                    last.then_inc(score_full, 1)

            def weigh(par, g, n, j, i):
                if i == 0:
                    pe.wait_ge(probs_low, JT * g + j + 3)
                    if j == 0:
                        pe.wait_ge(acc_copied, g + 1)
                        pe.wait_ge(values_moved[par], n + 1)
                r = key_rows(j)
                cols = slice(i * HALF, i * HALF + HALF)
                high, low = [p[j % SPLITS][0:r, cols] for p in probs_split]
                value = values[par][0:r, j, :, :].rearrange("p c d -> p (c d)")
                nc.tensor.matmul(acc[:, cols], value[:, 0:P], high, start=(j == 0), stop=False)
                nc.tensor.matmul(acc[0:DH, cols], value[:, P:P + DH], high, start=False, stop=False)
                last = nc.tensor.matmul(acc[:, cols], value[:, 0:P], low, start=False, stop=(j == JT - 1))
                if i == 1:
                    last.then_inc(av_done, 1)

            def head(par, n, b, hp, outs):
                g = 2 * n + par
                nxt = 1 - par
                base = beside_odd(n, outs) if par else beside_even(n, outs)
                m = n + 1
                batch = pe.snap((m >> 3) & (B - 1)) if not isinstance(m, int) else (m // PAIRS) % B
                pair = pe.snap(m & (PAIRS - 1)) if not isinstance(m, int) else m % PAIRS
                for j in range(JT):
                    jj = j + AHEAD_STEPS
                    for i in range(2):
                        if jj < JT:
                            scores(par, g, None, JT * g + jj, jj, i)
                        else:
                            scores(nxt, g + 1, base, JT * g + jj, jj - JT, i)
                        produce(nxt, g + 1, base, batch, pair, (4 * j + i,))
                    for i in range(2):
                        weigh(par, g, n, j, i)
                        produce(nxt, g + 1, base, batch, pair, (4 * j + 2 + i,))

            def turn_tile(b, t):
                if t >= 1:
                    pe.wait_ge(att_low, b * NT + t)
                for k in range(INNER // P):
                    last = nc.tensor.transpose(acc[:, k * P:k * P + P], att_rows[:, t, 2 * k:2 * k + 2, :]
                                               .rearrange("p h d -> p (h d)"), ident[:, :])
                last.then_inc(att_turned, 1)

            def project(b, base, parity, t):
                pe.wait_ge(att_low, b * NT + t + 1)
                pe.wait_ge(aux_done, base + t - 1)
                pairs = []
                for k in range(INNER // P):
                    lhs = [a[t % 2][:, k, :] for a in att_cols]
                    rhs = [w[:, k, :] for w in wo]
                    pairs += [(lhs[0], rhs[0]), (lhs[0], rhs[1]), (lhs[1], rhs[0])]
                summed(aux[(parity + t) % 2][:, 0:D], pairs).then_inc(aux_full, 1)

            def put_out(b, base, parity):
                pe.wait_ge(aux_done, base)
                pe.wait_ge(acc_copied, heads_before_out(b))
                turn_tile(b, 0)
                for t in range(NT):
                    if t + 1 < NT:
                        turn_tile(b, t + 1)
                    project(b, base, parity, t)

            def heads_before_out(b):
                return min(H * (b + 1) + 1, B * H) + 1 if isinstance(b, int) else H * (b + 1) + 2

            def finish():
                pe.wait_ge(acc_copied, B * H + 1)
                for half in range(2):
                    pe.wait_ge(aux_done, LAST_OUT + half - 1)
                    transposed_rows(aux[(FINAL_PARITY + half) % 2], half).then_inc(aux_full, 1)
                put_out(B - 1, LAST_OUT + 2, FINAL_PARITY)

            produce("start", 0, 0, 0, 0, range(SLOTS))
            for j in range(AHEAD_STEPS):
                for i in range(2):
                    scores("start", 0, 0, j, j, i)
            whole_program(pe, head, put_out, finish)


def experts(nc, x2_dram, listing, Wg, bg, W1, b1, W2, b2, out):
    x2_tiles = x2_dram.rearrange("(b t p) d -> b p t d", b=B, p=P)
    out_rows = out.rearrange("b n d -> (b n) d")
    KF = F // P
    GROUP = 4
    BANK = HALF // P
    META = 4
    OWN = 4

    stack = ExitStack()
    with stack:
        def sb(name, shape, dt):
            return stack.enter_context(nc.sbuf_tensor(name, shape, dt))

        def pb(name, shape, dt):
            return stack.enter_context(nc.psum_tensor(name, shape, dt))

        def sem(name):
            return stack.enter_context(nc.semaphore(name))

        ident = sb("e_ident", [P, P], F32)
        w1 = [sb(f"w1_{i}", [P, E, KD, F], F16) for i in range(2)]
        w2 = [sb(f"w2_{i}", [P, E, KF, D], F16) for i in range(2)]
        stage = [sb(f"e_stage{i}", [P, KD * F], F32) for i in range(2)]
        b2_all = sb("b2_all", [P, E, D], F32)
        b1_rows = sb("b1_rows", [E * KF, P], F32)
        b1_cols = sb("b1_cols", [P, E * KF], F32)
        wg = sb("wg", [P, KD, E], F32)
        bg_all = sb("bg_all", [P, E], F32)
        eps_col = sb("e_eps_col", [P, 1], F32)
        x2_all = sb("x2_all", [P, TT, D], F32)
        shared = x2_all[:, :, :].rearrange("p t d -> p (t d)")
        hidden = [shared[:, i * F:i * F + F] for i in range(2)]
        hidden_split = [[shared[:, (4 + 2 * h + i) * (F // 2):(5 + 2 * h + i) * (F // 2)].bitcast(F16)
                         .rearrange("p (k t) -> p k t", t=P) for i in range(2)] for h in range(2)]
        base = 8 * (F // 2)
        own_rows = [shared[:, base + i * D:base + i * D + D] for i in range(OWN)]
        base += OWN * D
        z_rows = [shared[:, base + i * D:base + i * D + D] for i in range(2)]
        base += 2 * D
        biased = [shared[:, base + i * D:base + i * D + D] for i in range(2)]
        base += 2 * D
        z_split = [[shared[:, base + (2 * h + i) * (D // 2):base + (2 * h + i + 1) * (D // 2)].bitcast(F16)
                    .rearrange("p (k t) -> p k t", t=P) for i in range(2)] for h in range(2)]
        base += 4 * (D // 2)
        z_group = [sb(f"z_group{i}", [P, GROUP, D], F32) for i in range(2)]
        z_cols = sb("z_cols", [P, GROUP, KD, P], F32)
        parts = sb("parts", [P, TT, STATS], F32)
        mean_var = sb("e_mean_var", [P, TT, 2], F32)
        std = sb("e_std", [P, TT], F32)
        rstd = sb("e_rstd", [P, TT], F32)
        logits = sb("logits", [P, TT, E], F32)
        top = sb("top", [P, TT], F32)
        work = [sb(f"work{i}", [P, TT, E], F32) for i in range(3)]
        chosen = sb("chosen", [P, TT, E], F16)
        first = sb("first", [P, TT], F32)
        e_less = sb("e_less", [P, E], F32)
        counts = sb("counts", [P, E], F32)
        counts_i = sb("counts_i", [P, E], I32)
        ends = [sb(f"ends{i}", [P, E], F32) for i in range(2)]
        place = sb("place", [P, TT], F32)
        place_i = sb("place_i", [P, TT], I32)
        rows = sb("rows", [P, TT, META], F32)
        rows_i = rows[:, :, :].bitcast(I32)
        upper = sb("upper", [P, P], F16)
        ones = sb("ones", [P, P], F16)
        fill = sb("fill", [P, SORTED, META], F32)
        fill_i = fill[:, :, :].bitcast(I32)
        meta = sb("meta", [P, SORTED, META], F32)
        meta_i = meta[:, :, :].bitcast(I32)
        read_f = sb("read_f", [P, SORTED], F32)
        read_i = sb("read_i", [P, SORTED], I32)
        starts = sb("starts", [P, SORTED], F32)
        past = z_group[0][:, :, :].rearrange("p t d -> p (t d)")[:, 0:SORTED * E].rearrange("p (t e) -> p t e", e=E)
        tile_f = sb("tile_f", [P, SORTED], F32)
        tile_expert = sb("tile_expert", [P, SORTED], I32)
        token = sb("token", [P, TT], I32)
        read_col = [sb(f"read_col{i}", [P, 1], I32) for i in range(OWN)]
        write_col = [sb(f"write_col{i}", [P, 1], I32) for i in range(OWN)]
        place_col = [sb(f"place_col{i}", [P, 1], I32) for i in range(2)]

        turned = [pb(f"turned{i}", [P, HALF], F32) for i in range(2)]
        up = [pb(f"up{i}", [P, F], F32) for i in range(2)]
        down = [pb(f"down{i}", [P, HALF], F32) for i in range(2)]

        c_step = sem("c_step")
        consts = sem("consts")
        small_loaded = sem("small_loaded")
        b1_turned = sem("b1_turned")
        b1_ready = sem("b1_ready")
        x2_loaded = sem("x2_loaded")
        r_step = sem("r_step")
        r_var = sem("r_var")
        r_std = sem("r_std")
        g_rows = sem("g_rows")
        g_turned = sem("g_turned")
        g_cols = sem("g_cols")
        g_logits = sem("g_logits")
        g_taken = sem("g_taken")
        shifted = sem("shifted")
        powers = sem("powers")
        chosen_ready = sem("chosen_ready")
        ranks = sem("ranks")
        e_loaded = [sem(f"e_loaded{i}") for i in range(2)]
        e_high = sem("e_high")
        e_low = sem("e_low")
        filled = sem("filled")
        placed = sem("placed")
        listed = sem("listed")
        meta_loaded = sem("meta_loaded")
        meta_ready = sem("meta_ready")
        col_step = sem("col_step")
        gathered = [sem(f"gathered{i}") for i in range(OWN)]
        scattered = [sem(f"scattered{i}") for i in range(OWN)]
        z_ready = sem("e_z_ready")
        z_turned = sem("e_z_turned")
        z_high = sem("e_z_high")
        z_done = sem("e_z_done")
        up_full = sem("up_full")
        silu_done = sem("silu_done")
        h_high = sem("h_high")
        h_done = sem("h_done")
        down_full = sem("down_full")
        bias_added = sem("bias_added")
        y_ready = sem("y_ready")
        turns = {e: sem("e_turns_" + e) for e in ("pool", "dve", "act")}

        def at_least(eng, s, value, carry=None):
            if isinstance(value, int) and value <= 0:
                return
            eng.wait_ge(s, value)
            if carry and not isinstance(value, int):
                eng.sem_inc(turns[carry], 1)

        def tile_steps(eng, step):
            for u in range(OWN):
                step(0, u)
            with eng.Fori(1, SORTED // OWN - 1) as i:
                for u in range(OWN):
                    step(i, u)
            for u in range(OWN):
                step(SORTED // OWN - 1, u)

        def number(i, u):
            return OWN * i + u

        def exists(i, u):
            return not (isinstance(i, int) and number(i, u) >= SORTED)

        block = stack.enter_context(nc.Block())

        @block.sync
        def _(sp):
            sp.dma_start(b1_rows[:, :], b1.rearrange("e (k p) -> (e k) p", p=P)).then_inc(small_loaded, 16)
            sp.dma_start(wg[:, :, :], Wg.rearrange("(k p) e -> p k e", p=P)).then_inc(small_loaded, 16)
            sp.dma_start(bg_all[:, :], bg.rearrange("(o e) -> o e", o=1).to_broadcast([P, E])).then_inc(small_loaded, 16)
            sp.dma_start(b2_all[:, :, :].rearrange("p e d -> p (e d)"),
                         b2.rearrange("(o e) d -> o (e d)", o=1).to_broadcast([P, E * D])).then_inc(small_loaded, 16)
            for b in range(B):
                sp.dma_start(x2_all[:, b * NT:b * NT + NT, :], x2_tiles[b]).then_inc(x2_loaded, 16)
            w1_rows = W1.rearrange("e (k p) n -> e p k n", p=P)
            w2_rows = W2.rearrange("e (k p) n -> e p k n", p=P)

            def load(e, i, src):
                dst = stage[i][:, :].rearrange("p (k n) -> p k n", k=src.shape[2])
                sp.dma_start(dst, src[ds(e, 1), :, :, :].rearrange("o p k n -> (o p) k n")).then_inc(e_loaded[i], 16)

            load(0, 0, w1_rows)
            load(0, 1, w2_rows)
            with sp.Fori(1, E) as e:
                sp.wait_ge(e_low, 2 * e - 1)
                load(e, 0, w1_rows)
                sp.wait_ge(e_low, 2 * e)
                load(e, 1, w2_rows)
            sp.wait_ge(listed, 16 * TT)
            sp.dma_start(meta[:, :, :], listing.rearrange("(k p) c -> p k c", p=P)).then_inc(meta_loaded, 16)

        @block.gpsimd
        def _(pool):
            nc.gpsimd.memset(ident[:, :], 0.0).then_inc(c_step, 1)
            nc.gpsimd.memset(ones[:, :], 1.0).then_inc(c_step, 1)
            pool.wait_ge(c_step, 2)
            nc.gpsimd.affine_select(out=ident[:, :], in_=ident[:, :], compare_op=ALU.not_equal, fill=1.0,
                                    base=0, pattern=[[-1, P]], channel_multiplier=1).then_inc(c_step, 1)
            nc.gpsimd.affine_select(out=upper[:, :], in_=ones[:, :], compare_op=ALU.is_gt, fill=0.0,
                                    base=0, pattern=[[1, P]], channel_multiplier=-1).then_inc(c_step, 1)
            nc.gpsimd.iota(e_less[:, :], [[1, E]], base=-E, channel_multiplier=0,
                           allow_small_or_imprecise_dtypes=True).then_inc(c_step, 1)
            nc.gpsimd.iota(starts[:, :], [[P, SORTED]], base=0, channel_multiplier=0,
                           allow_small_or_imprecise_dtypes=True).then_inc(c_step, 1)
            nc.gpsimd.iota(token[:, :], [[P, TT]], base=0, channel_multiplier=1).then_inc(c_step, 1)
            nc.gpsimd.memset(fill[:, :, :], 0.0).then_inc(c_step, 1)
            pool.wait_ge(c_step, 8)
            nc.gpsimd.iota(fill_i[:, :, 0], [[0, SORTED]], base=NOBODY, channel_multiplier=0).then_inc(c_step, 1)
            pool.wait_ge(c_step, 9)
            nc.gpsimd.memset(eps_col[:, :], EPS).then_inc(consts, 1)
            pool.dma_start(listing.rearrange("(k p) c -> p k c", p=P), fill[:, :, :]).then_inc(filled, 16)
            with pool.Fori(0, E) as e:
                for i, w in enumerate((w1, w2)):
                    high, low = [m[:, ds(e, 1), :, :].rearrange("p o k n -> p (o k n)") for m in w]
                    pool.wait_ge(e_high, 2 * e + i + 1)
                    pool.sem_inc(turns["pool"], 1)
                    nc.gpsimd.tensor_tensor(out=low, in0=stage[i][:, :], in1=high, op=ALU.subtract)\
                        .then_inc(e_low, 1)
            pool.wait_ge(filled, 16)
            pool.wait_ge(placed, 1)
            for t in range(TT):
                nc.gpsimd.indirect_dma_start(out=listing, out_offset=bass.IndirectOffsetOnAxis(place_i[:, t:t + 1], 0),
                                             in_=rows[:, t, :], in_offset=None).then_inc(listed, 16)
            pool.wait_ge(meta_ready, 1)

            def gather(i, u):
                if not exists(i, u):
                    return
                q = u % OWN
                at_least(pool, scattered[q], 16 * (i + u // OWN), "pool")
                k = number(i, u)
                nc.gpsimd.tensor_copy(read_col[q][:, :], read_i[:, ds(k, 1)]).then_inc(col_step, 1)
                nc.gpsimd.tensor_copy(write_col[q][:, :], meta_i[:, ds(k, 1), 0]).then_inc(col_step, 1)
                at_least(pool, col_step, 2 * k + 2, "pool")
                nc.gpsimd.indirect_dma_start(out=own_rows[q], out_offset=None, in_=x2_dram,
                                             in_offset=bass.IndirectOffsetOnAxis(read_col[q][:, :], 0))\
                    .then_inc(gathered[q], 16)

            def step(i, u):
                gather(i, u + 2)
                at_least(pool, y_ready, number(i, u) + 1, "pool")
                nc.gpsimd.indirect_dma_start(out=out_rows, out_offset=bass.IndirectOffsetOnAxis(write_col[u][:, :], 0),
                                             in_=own_rows[u], in_offset=None, bounds_check=TOK - 1,
                                             oob_is_err=False).then_inc(scattered[u], 16)

            gather(0, 0)
            gather(0, 1)
            tile_steps(pool, step)
            for q in range(OWN):
                pool.wait_ge(scattered[q], 16 * (SORTED // OWN))

        @block.scalar
        def _(act):
            act.wait_ge(consts, 1)
            act.wait_ge(r_var, 1)
            nc.scalar.activation(std[:, :], mean_var[:, :, 1], ACT.Sqrt, bias=eps_col[:, :]).then_inc(r_std, 1)

            def high_weights(e):
                for i, w in enumerate((w1, w2)):
                    act.wait_ge(e_loaded[i], 16 * (e + 1))
                    act.sem_inc(turns["act"], 1)
                    nc.scalar.activation(w[0][:, ds(e, 1), :, :].rearrange("p o k n -> p (o k n)"), stage[i][:, :],
                                         ACT.Copy).then_inc(e_high, 1)

            act.sem_inc(g_logits, 1)
            with act.Fori(0, TT // GROUP // 2) as i:
                for par in range(2):
                    g = 2 * i + par
                    act.wait_ge(g_turned, g + 1)
                    act.wait_ge(g_logits, g + 1)
                    nc.scalar.activation(z_cols[:, :, :, :].rearrange("p t k c -> p (t k c)"), up[par][:, :],
                                         ACT.Copy).then_inc(g_cols, 1)
                high_weights(i)
            act.wait_ge(shifted, 1)
            nc.scalar.activation(work[1][:, :, :], work[0][:, :, :], ACT.Exp).then_inc(powers, 1)
            with act.Fori(TT // GROUP // 2, E) as e:
                high_weights(e)

            act.wait_ge(meta_ready, 1)

            def z_high_half(i, u):
                if not exists(i, u):
                    return
                at_least(act, z_turned, number(i, u) + 1)
                nc.scalar.activation(z_split[0][u % 2], turned[u % 2][:, 0:D].rearrange("p (k t) -> p k t", t=P),
                                     ACT.Copy).then_inc(z_high, 1)

            def hidden_layer(i, u):
                if not exists(i, u):
                    return
                k = number(i, u)
                e = act.value_load(tile_expert[0:1, ds(k, 1)], min_val=0, max_val=E - 1)
                at_least(act, h_done, k - 1)
                for c in range(KF):
                    if c % BANK == 0:
                        at_least(act, up_full, KF // BANK * k + c // BANK + 1, "act")
                    nc.scalar.activation(hidden[u % 2][:, c * P:c * P + P], up[u % 2][:, c * P:c * P + P], ACT.Silu,
                                         bias=b1_cols[:, ds(e * KF + c, 1)]).then_inc(silu_done, 1)

            def hidden_high(i, u):
                if not exists(i, u):
                    return
                k = number(i, u)
                at_least(act, down_full, k - 1)
                at_least(act, silu_done, KF * k + KF)
                nc.scalar.activation(hidden_split[0][u % 2].rearrange("p k t -> p (k t)"), hidden[u % 2], ACT.Copy)\
                    .then_inc(h_high, 1)

            z_high_half(0, 0)
            hidden_layer(0, 0)
            z_high_half(0, 1)
            hidden_high(0, 0)

            def step(i, u):
                hidden_layer(i, u + 1)
                z_high_half(i, u + 2)
                hidden_high(i, u + 1)

            tile_steps(act, step)

        @block.vector
        def _(dve):
            r = Steps(r_step, 0)

            def link(ins):
                r.mark(ins)
                dve.wait_ge(r_step, r.reached())

            dve.wait_ge(b1_turned, 1)
            nc.vector.tensor_copy(b1_cols[:, :], turned[0][:, 0:E * KF]).then_inc(b1_ready, 1)
            for b in range(B):
                dve.wait_ge(x2_loaded, 16 * B)
                for t in range(b * NT, b * NT + NT):
                    last = nc.vector.bn_stats(parts[:, t, :], x2_all[:, t, :])
            link(last)
            for t in range(TT):
                last = nc.vector.bn_aggr(mean_var[:, t, :], parts[:, t, :])
            last.then_inc(r_var, 1)
            dve.wait_ge(r_std, 1)
            link(nc.vector.reciprocal(rstd[:, :], std[:, :]))
            dve.wait_ge(small_loaded, 64)

            def group_rows(i, par, ahead):
                g = 2 * i + par
                if ahead:
                    dve.wait_ge(g_turned, g - 1)
                for q in range(GROUP):
                    t = GROUP * g + q
                    last = nc.vector.tensor_scalar(
                        z_group[par][:, q, :], x2_all[:, ds(t, 1), :].rearrange("p o d -> p (o d)"),
                        mean_var[:, ds(t, 1), 0], rstd[:, ds(t, 1)], ALU.subtract, ALU.mult)
                last.then_inc(g_rows, 1)

            def take_logits(i, par):
                g = 2 * i + par
                dve.wait_ge(g_logits, g + 2)
                nc.vector.tensor_tensor(out=logits[:, ds(GROUP * g, GROUP), :],
                                        in0=down[par][:, 0:GROUP * E].rearrange("p (t e) -> p t e", e=E),
                                        in1=bg_all[:, :].unsqueeze(1).to_broadcast([P, GROUP, E]),
                                        op=ALU.add).then_inc(g_taken, 1)

            group_rows(0, 0, False)
            group_rows(0, 1, False)
            with dve.Fori(1, TT // GROUP // 2) as i:
                for par in range(2):
                    group_rows(i, par, True)
                for par in range(2):
                    take_logits(i - 1, par)
            for par in range(2):
                take_logits(TT // GROUP // 2 - 1, par)
            dve.wait_ge(g_taken, TT // GROUP)

            def tt(out, a, b, op):
                link(nc.vector.tensor_tensor(out=out, in0=a, in1=b, op=op))

            def per_token(a):
                return a.unsqueeze(2).to_broadcast([P, TT, E])

            def per_expert(a):
                return a.unsqueeze(1).to_broadcast([P, TT, E])

            dve.wait_ge(consts, 1)
            link(nc.vector.tensor_reduce(top[:, :], logits[:, :, :], AX.X, ALU.max))
            nc.vector.tensor_tensor(out=work[0][:, :, :], in0=logits[:, :, :], in1=per_token(top[:, :]),
                                    op=ALU.subtract).then_inc(shifted, 1)
            tt(work[2][:, :, :], logits[:, :, :], per_token(top[:, :]), ALU.is_equal)
            tt(work[2][:, :, :], work[2][:, :, :], per_expert(e_less[:, :]), ALU.mult)
            link(nc.vector.tensor_reduce(first[:, :], work[2][:, :, :], AX.X, ALU.min))
            dve.wait_ge(powers, 1)
            nc.vector.tensor_tensor(out=chosen[:, :, :], in0=per_expert(e_less[:, :]), in1=per_token(first[:, :]),
                                    op=ALU.is_equal).then_inc(chosen_ready, 1)
            link(nc.vector.tensor_reduce(place[:, :], work[1][:, :, :], AX.X, ALU.add))
            link(nc.vector.reciprocal(rows[:, :, 1], place[:, :]))
            nc.vector.tensor_copy(rows_i[:, :, 0], token[:, :])
            nc.vector.tensor_copy(rows[:, :, 2], mean_var[:, :, 0])
            nc.vector.tensor_copy(rows[:, :, 3], rstd[:, :])
            dve.wait_ge(ranks, 1)
            before = turned[0][:, 0:TT * E].rearrange("p (t e) -> p t e", e=E)
            totals = turned[1][:, 0:TT * E].rearrange("p (t e) -> p t e", e=E)
            link(nc.vector.tensor_copy(work[0][:, :, :], totals))
            at, to, reach = 0, 1, 1
            while reach < TT:
                nc.vector.tensor_copy(work[to][:, 0:reach, :], work[at][:, 0:reach, :])
                tt(work[to][:, reach:TT, :], work[at][:, reach:TT, :], work[at][:, 0:TT - reach, :], ALU.add)
                at, to, reach = to, at, 2 * reach
            sums, spare = work[at], work[to]
            link(nc.vector.tensor_scalar(counts[:, :], sums[:, TT - 1, :], float(P - 1), None, ALU.add))
            link(nc.vector.tensor_copy(counts_i[:, :], counts[:, :]))
            shift = P.bit_length() - 1
            link(nc.vector.tensor_scalar(counts_i[:, :], counts_i[:, :], shift, shift, ALU.logical_shift_right,
                                         ALU.logical_shift_left))
            link(nc.vector.tensor_copy(counts[:, :], counts_i[:, :]))
            link(nc.vector.tensor_copy(ends[0][:, :], counts[:, :]))
            e_at, e_to, reach = 0, 1, 1
            while reach < E:
                nc.vector.tensor_copy(ends[e_to][:, 0:reach], ends[e_at][:, 0:reach])
                tt(ends[e_to][:, reach:E], ends[e_at][:, reach:E], ends[e_at][:, 0:E - reach], ALU.add)
                e_at, e_to, reach = e_to, e_at, 2 * reach
            end, start = ends[e_at], ends[e_to]
            tt(start[:, :], end[:, :], counts[:, :], ALU.subtract)
            tt(spare[:, :, :], totals, sums[:, :, :], ALU.subtract)
            tt(sums[:, :, :], before, spare[:, :, :], ALU.subtract)
            tt(sums[:, :, :], sums[:, :, :], per_expert(start[:, :]), ALU.add)
            tt(sums[:, :, :], sums[:, :, :], chosen[:, :, :], ALU.mult)
            link(nc.vector.tensor_reduce(place[:, :], sums[:, :, :], AX.X, ALU.add))
            nc.vector.tensor_copy(place_i[:, :], place[:, :]).then_inc(placed, 1)
            tt(past, end[:, :].unsqueeze(1).to_broadcast([P, SORTED, E]),
               starts[:, :].unsqueeze(2).to_broadcast([P, SORTED, E]), ALU.is_le)
            link(nc.vector.tensor_reduce(tile_f[:, :], past, AX.X, ALU.add))
            link(nc.vector.tensor_scalar(tile_expert[:, :], tile_f[:, :], float(E - 1), None, ALU.min))
            dve.wait_ge(meta_loaded, 16)
            link(nc.vector.tensor_copy(read_f[:, :], meta_i[:, :, 0]))
            nc.vector.tensor_scalar(read_i[:, :], read_f[:, :], float(TOK - 1), None, ALU.min).then_inc(meta_ready, 1)

            def normalise_rows(i, u):
                if not exists(i, u):
                    return
                k = number(i, u)
                at_least(dve, gathered[u % OWN], 16 * (i + u // OWN + 1))
                at_least(dve, z_turned, k - 1)
                nc.vector.tensor_scalar(z_rows[u % 2], own_rows[u % OWN], meta[:, ds(k, 1), 2], meta[:, ds(k, 1), 3],
                                        ALU.subtract, ALU.mult).then_inc(z_ready, 1)

            def z_low_half(i, u):
                if not exists(i, u):
                    return
                at_least(dve, z_high, number(i, u) + 1)
                nc.vector.tensor_tensor(out=z_split[1][u % 2],
                                        in0=turned[u % 2][:, 0:D].rearrange("p (k t) -> p k t", t=P),
                                        in1=z_split[0][u % 2], op=ALU.subtract).then_inc(z_done, 1)

            def hidden_low(i, u):
                if not exists(i, u):
                    return
                at_least(dve, h_high, number(i, u) + 1)
                nc.vector.tensor_tensor(out=hidden_split[1][u % 2].rearrange("p k t -> p (k t)"), in0=hidden[u % 2],
                                        in1=hidden_split[0][u % 2].rearrange("p k t -> p (k t)"),
                                        op=ALU.subtract).then_inc(h_done, 1)

            def finish(i, u):
                k = number(i, u)
                e = dve.value_load(tile_expert[0:1, ds(k, 1)], min_val=0, max_val=E - 1)
                at_least(dve, down_full, k + 1)
                nc.vector.tensor_tensor(out=biased[u % 2], in0=down[u % 2][:, 0:D],
                                        in1=b2_all[:, ds(e, 1), :].rearrange("p o d -> p (o d)"),
                                        op=ALU.add).then_inc(bias_added, 1)
                at_least(dve, bias_added, k + 1)
                nc.vector.scalar_tensor_tensor(out=own_rows[u], in0=biased[u % 2], scalar=meta[:, ds(k, 1), 1],
                                               in1=own_rows[u], op0=ALU.mult, op1=ALU.add).then_inc(y_ready, 1)

            normalise_rows(0, 0)
            normalise_rows(0, 1)
            z_low_half(0, 0)
            z_low_half(0, 1)
            hidden_low(0, 0)

            def step(i, u):
                normalise_rows(i, u + 2)
                z_low_half(i, u + 2)
                hidden_low(i, u + 1)
                finish(i, u)

            tile_steps(dve, step)

        @block.tensor
        def _(pe):
            pe.wait_ge(consts, 1)
            pe.wait_ge(small_loaded, 64)
            nc.tensor.transpose(turned[0][:, 0:E * KF], b1_rows[:, :], ident[0:E * KF, 0:E * KF])\
                .then_inc(b1_turned, 1)

            def turn_group(i, par, again):
                g = 2 * i + par
                pe.wait_ge(g_rows, g + 1)
                if again:
                    pe.wait_ge(g_cols, g - 1)
                for q in range(GROUP):
                    for k in range(KD):
                        lo = (q * KD + k) * P
                        last = nc.tensor.transpose(up[par][:, lo:lo + P], z_group[par][:, q, k * P:k * P + P],
                                                   ident[:, :])
                last.then_inc(g_turned, 1)

            def gate(i, par, again):
                g = 2 * i + par
                pe.wait_ge(g_cols, g + 1)
                if again:
                    pe.wait_ge(g_taken, g - 1)
                for q in range(GROUP):
                    for k in range(KD):
                        last = nc.tensor.matmul(down[par][:, q * E:q * E + E], z_cols[:, q, k, :], wg[:, k, :],
                                                start=(k == 0), stop=(k == KD - 1))
                last.then_inc(g_logits, 1)

            def groups(i, again):
                for par in range(2):
                    turn_group(i, par, again)
                for par in range(2):
                    gate(i, par, again)

            groups(0, False)
            with pe.Fori(1, TT // GROUP // 2) as i:
                groups(i, True)
            pe.wait_ge(chosen_ready, 1)
            pe.wait_ge(b1_ready, 1)
            one_hot = chosen[:, :, :].rearrange("p t e -> p (t e)")
            nc.tensor.matmul(turned[0][:, 0:TT * E], upper[:, :], one_hot, start=True, stop=True)
            nc.tensor.matmul(turned[1][:, 0:TT * E], ones[:, :], one_hot, start=True, stop=True).then_inc(ranks, 1)
            pe.wait_ge(e_low, 2 * E)
            pe.wait_ge(meta_ready, 1)

            def turn(i, u):
                if not exists(i, u):
                    return
                k = number(i, u)
                at_least(pe, z_ready, k + 1)
                at_least(pe, z_done, k - 1)
                for c in range(KD):
                    last = nc.tensor.transpose(turned[u % 2][:, c * P:c * P + P], z_rows[u % 2][:, c * P:c * P + P],
                                               ident[:, :])
                last.then_inc(z_turned, 1)

            def upward(i, u):
                if not exists(i, u):
                    return
                k = number(i, u)
                e = pe.value_load(tile_expert[0:1, ds(k, 1)], min_val=0, max_val=E - 1)
                at_least(pe, z_done, k + 1)
                at_least(pe, silu_done, KF * (k - 1))
                for c in range(KF):
                    n = 0
                    for kk in range(KD):
                        for a, b in ((0, 0), (0, 1), (1, 0)):
                            lhs = w1[a][:, ds(e, 1), kk, c * P:c * P + P].rearrange("p o n -> p (o n)")
                            last = nc.tensor.matmul(up[u % 2][:, c * P:c * P + P], lhs, z_split[b][u % 2][:, kk, :],
                                                    start=(n == 0), stop=(n == 3 * KD - 1))
                            n += 1
                    if c % BANK == BANK - 1:
                        last.then_inc(up_full, 1)

            def downward(i, u):
                k = number(i, u)
                e = pe.value_load(tile_expert[0:1, ds(k, 1)], min_val=0, max_val=E - 1)
                at_least(pe, h_done, k + 1)
                at_least(pe, y_ready, k - 1)
                n = 0
                for kk in range(KF):
                    for a, b in ((0, 0), (0, 1), (1, 0)):
                        rhs = w2[b][:, ds(e, 1), kk, :].rearrange("p o n -> p (o n)")
                        last = nc.tensor.matmul(down[u % 2][:, 0:D], hidden_split[a][u % 2][:, kk, :], rhs,
                                                start=(n == 0), stop=(n == 3 * KF - 1))
                        n += 1
                last.then_inc(down_full, 1)

            turn(0, 0)
            upward(0, 0)
            turn(0, 1)

            def step(i, u):
                upward(i, u + 1)
                turn(i, u + 2)
                downward(i, u)

            tile_steps(pe, step)


def build_kernel(nc, x, ctx_1024, lmg, lmb, llg, llb, Wq, Wkv, Wout, Wg, bg, W1, b1, W2, b2, out):
    x2 = nc.dram_tensor("x2", (TOK, D), F32, kind="Internal").ap()
    listing = nc.dram_tensor("listing", (SORTED * P, 4), F32, kind="Internal").ap()
    attention(nc, x, ctx_1024, (llg, llb, lmg, lmb), Wq, Wkv, Wout, x2)
    experts(nc, x2, listing, Wg, bg, W1, b1, W2, b2, out)


_INS = ['x', 'ctx_1024', 'L0_xattn_ln_m_g', 'L0_xattn_ln_m_b', 'L0_xattn_ln_l_g', 'L0_xattn_ln_l_b',
        'L0_xattn_Wq', 'L0_xattn_Wkv', 'L0_xattn_Wout', 'L0_ffn_Wg', 'L0_ffn_bg', 'L0_ffn_W1', 'L0_ffn_b1',
        'L0_ffn_W2', 'L0_ffn_b2']


def kernel(**inputs):
    import numpy as np
    import concourse.bacc as bacc
    from concourse.bass_utils import run_bass_kernel_spmd

    nc = bacc.Bacc("TRN2", target_bir_lowering=False, num_devices=1)
    arrays, args = {}, []
    for name in _INS:
        a = np.ascontiguousarray(inputs[name])
        arrays["in_" + name] = a
        args.append(nc.dram_tensor("in_" + name, a.shape, mybir.dt.from_np(a.dtype), kind="ExternalInput").ap())
    out = nc.dram_tensor("out", (B, N, D), F32, kind="ExternalOutput").ap()
    build_kernel(nc, *args, out)
    result = run_bass_kernel_spmd(nc, [arrays], core_ids=[0])
    return result.results[0]["out"]
```

```python
import concourse.bass as bass
from concourse import mybir
from contextlib import ExitStack

F32 = mybir.dt.float32
F16 = mybir.dt.float16
I32 = mybir.dt.int32
ALU = mybir.AluOpType
ACT = mybir.ActivationFunctionType
AX = mybir.AxisListType
ds = bass.ds

P = 128
B, N, D = 4, 1024, 256
C = 154
H, DH = 16, 64
INNER = H * DH
E, F = 8, 1024
KD = D // P
NT = N // P
KEYS = N + C
JT = 10
TAIL = C - P
PAIRS = H // 2
CT = B * C
CTILES = -(-CT // P)
TOK = B * N
TT = TOK // P
EPS = 1e-5
SCALE = float(DH) ** -0.5
HALF = 512
SORTED = TT + E
NOBODY = 2 * TOK
STATS = 6


def key_rows(j):
    return TAIL if j == JT - 1 else P


MAX_TAILS = [(0, 1, 2), (3, 4, 5), (6, 7)]
VALUE_TILES = [(0, 1, 2), (3, 4, 5), (6, 7), (8, 9)]
SLOTS = 4 * JT
QK = 3
AHEAD_STEPS = 2
SPLITS = 5

POOL_SPLITS = (2, 3, 4, 7, 8)
POOL_FIRST = 3
VECTOR_SPLITS = [j for j in range(JT) if j not in POOL_SPLITS]
MAX_SLOTS = [s for s in range(SLOTS) if (s % 4 != 2 or s // 4 + 1 in POOL_SPLITS) and s > 0]
TURN_SLOT = 23
VALUE_SLOTS = (24, 26, 28, 30)
QK_SLOTS = (31, 34, 36)


def schedule(name):
    at = {s: [] for s in range(SLOTS)}
    if name == "start":
        at[0] += [("qk", c, 0, 0) for c in range(QK)]
    maxima = [("max", t, c) for t in range(NT) for c in range(2)] + [("tail", g) for g in range(len(MAX_TAILS))]
    for s, chunk in zip(MAX_SLOTS, maxima):
        at[s].append(chunk)
    at[TURN_SLOT].append(("turn",))
    if name != 0:
        for g, s in enumerate(VALUE_SLOTS):
            at[s].append(("v", g))
    for c, s in enumerate(QK_SLOTS):
        at[s].append(("qk", c, 1 if name == "start" else 1 - name, 1))
    n, out = 0, {}
    for s in range(SLOTS):
        out[s] = []
        for chunk in at[s]:
            out[s].append((n, chunk))
            n += 1
    return out, n


AHEAD, AMOUNT = {}, {}
for name in (1, 0, "start"):
    AHEAD[name], AMOUNT[name] = schedule(name)
N_PAIR = AMOUNT[0] + AMOUNT[1]
PARITY = {"start": 0, 1: AMOUNT["start"] % 2, 0: (AMOUNT["start"] + AMOUNT[1]) % 2}
TURN = {name: max(n for c in at.values() for n, k in c if k[0] == "turn") for name, at in AHEAD.items()}
LAST_VALUES = {name: max(n for c in AHEAD[name].values() for n, k in c if k[0] == "v") for name in (1, "start")}
assert N_PAIR % 2 == 0


class Steps:

    def __init__(self, sem, start):
        self.sem, self.start, self.n = sem, start, 0

    def mark(self, ins):
        ins.then_inc(self.sem, 1)
        self.n += 1

    def reached(self):
        return self.start + self.n


def attention(nc, x, ctx_in, ln, Wq, Wkv, Wout, x2_dram, x2_stats, early_loads):
    x_rows = x.rearrange("b (t p) d -> b p t d", p=P)
    ctx_rows = ctx_in.rearrange("b c d -> (b c) d")
    x2_rows = x2_dram.rearrange("(b t p) d -> b t p d", b=B, p=P)
    weights = [Wq.rearrange("(k p) n -> p k n", p=P),
               Wkv[:, 0:INNER].rearrange("(k p) n -> p k n", p=P),
               Wkv[:, INNER:2 * INNER].rearrange("(k p) n -> p k n", p=P),
               Wout.rearrange("(k p) n -> p k n", p=P)]

    stack = ExitStack()
    with stack:
        def sb(name, shape, dt):
            return stack.enter_context(nc.sbuf_tensor(name, shape, dt))

        def pb(name, shape, dt):
            return stack.enter_context(nc.psum_tensor(name, shape, dt))

        def sem(name):
            return stack.enter_context(nc.semaphore(name))

        ident = sb("ident", [P, P], F32)
        ln_rows = sb("ln_rows", [8, P], F32)
        ln_cols = sb("ln_cols", [P, 8], F32)
        wqk = [sb(f"wqk{i}", [P, KD, H, 2, DH], F16) for i in range(2)]
        wv = [sb(f"wv{i}", [P, KD, INNER], F16) for i in range(2)]
        wo = [sb(f"wo{i}", [P, INNER // P, D], F16) for i in range(2)]
        zx = [sb(f"zx{i}", [P, KD, TOK], F16) for i in range(2)]
        zc = [sb(f"zc{i}", [P, KD, CT], F16) for i in range(2)]
        q_both = [sb(f"q_both{i}", [P, N], F16) for i in range(2)]
        k_high = [sb(f"k_high{i}", [P, KEYS], F16) for i in range(2)]
        q_max = [sb(f"q_max{i}", [DH + 1, N], F16) for i in range(2)]
        k_low = [sb(f"k_low{i}", [DH + 1, KEYS], F16) for i in range(2)]
        max_row = [sb(f"max_row{i}", [NT, P], F16) for i in range(2)]
        max_parts = sb("max_parts", [P, NT, 3], F32)
        neg_max = sb("neg_max", [P, NT], F32)
        probs = [sb(f"probs{i}", [P, N], F32) for i in range(2)]
        probs_split = [[sb(f"probs_split{h}{i}", [P, N], F16) for i in range(SPLITS)] for h in range(2)]
        values = [sb(f"values{i}", [P, JT, 3, DH], F16) for i in range(2)]
        values_pair = sb("values_pair", [P, JT, 2, 2, DH], F16)
        head_sums = sb("head_sums", [P, 2, NT // 2, DH + 1], F32)
        recip = sb("recip", [P, NT], F32)
        att_rows = sb("att_rows", [P, NT, H, DH], F32)
        att_cols = [[sb(f"att_cols{h}{i}", [P, INNER // P, P], F16) for i in range(2)] for h in range(2)]
        x_res = [sb(f"x_res{i}", [P, D], F32) for i in range(2)]
        x2_tile = [sb(f"x2_tile{i}", [P, D], F32) for i in range(2)]
        stats = sb("stats", [P, NT, STATS], F32)
        mean_var = sb("mean_var", [P, NT, 2], F32)
        std = sb("std", [P, NT], F32)
        rstd = sb("rstd", [P, NT], F32)
        eps_col = sb("eps_col", [P, 1], F32)
        eps_square = sb("eps_square", [P, 1], F32)
        staging = att_rows[:, :, :, :].rearrange("p t h d -> p (t h d)")
        w_stage = [staging[:, i * KD * N:(i + 1) * KD * N] for i in range(2)]
        x_stage = [staging[:, (i + 2) * KD * N:(i + 3) * KD * N].rearrange("p (t d) -> p t d", d=D) for i in range(2)]

        score = [pb(f"score{i}", [P, N], F32) for i in range(2)]
        acc = pb("acc", [P, N], F32)
        aux = [pb(f"aux{i}", [P, HALF], F32) for i in range(2)]

        pool_turns = sem("pool_turns")
        dve_turns = sem("dve_turns")
        ident_ready = sem("ident_ready")
        ln_loaded = sem("ln_loaded")
        ln_turned = sem("ln_turned")
        ln_ready = sem("ln_ready")
        w_loaded = [sem(f"w_loaded{i}") for i in range(2)]
        w_high = sem("w_high")
        w_low = sem("w_low")
        x_loaded = [sem(f"x_loaded{i}") for i in range(2)]
        z_step = sem("z_step")
        var_ready = sem("var_ready")
        std_ready = sem("std_ready")
        z_ready = sem("z_ready")
        z_turned = sem("z_turned")
        z_affine = sem("z_affine")
        z_high = sem("z_high")
        z_low = sem("z_low")
        ones_ready = sem("ones_ready")
        aux_full = sem("aux_full")
        aux_high = sem("aux_high")
        aux_done = sem("aux_done")
        q_copied = sem("q_copied")
        max_ready = sem("max_ready")
        max_sent = sem("max_sent")
        values_moved = [sem("even_values"), sem("odd_values")]
        score_full = sem("score_full")
        exp_done = sem("exp_done")
        values_high = sem("values_high")
        act_turns = sem("act_turns")
        probs_high = sem("probs_high")
        probs_low = sem("probs_low")
        pool_low = sem("pool_low")
        av_done = sem("av_done")
        acc_copied = sem("acc_copied")
        recip_done = sem("recip_done")
        rows_taken = sem("rows_taken")
        att_turned = sem("att_turned")
        att_high = sem("att_high")
        att_low = sem("att_low")
        res_loaded = [sem(f"res_loaded{i}") for i in range(2)]
        x2_stored = [sem(f"x2_stored{i}") for i in range(2)]

        def group_of(group):
            if group == 0:
                return 4, lambda w, i, cols: zc[w][:, :, HALF * i:HALF * i + cols], [sum(h) for h in C_HALVES]
            first = (group - 1) * N
            return 0, lambda w, i, cols: zx[w][:, :, first + i * HALF:first + i * HALF + cols], [HALF, HALF]

        SUMS = NT // 2 * (DH + 1)
        sums_in_acc = acc[:, :].rearrange("p (i c) -> p i c", i=2)[:, :, 0:SUMS]

        C_ROWS = [min(P, CT - t * P) for t in range(CTILES)]
        C_HALVES = [C_ROWS[0:4], C_ROWS[4:]]
        X_HALVES = [[P] * 4, [P] * 4]

        def beside_even(n, outs):
            return n * N_PAIR + outs * NT + AMOUNT["start"]

        def beside_odd(n, outs):
            return n * N_PAIR + outs * NT + AMOUNT["start"] + AMOUNT[1]

        def out_base(b):
            return beside_odd((b + 1) * PAIRS, b)

        LAST_OUT = beside_even(B * PAIRS, B - 1)

        def aux_bank(name, place):
            return aux[(PARITY[name] + place) % 2]

        OUT_PARITY = PARITY[0]
        FINAL_PARITY = PARITY[1]

        def value_groups(g):
            js = VALUE_TILES[g]
            return [(js, P)] if js[-1] < JT - 1 else [(js[:-1], P), (js[-1:], TAIL)]

        def value_bank(bank, g):
            return bank[:, 0:len(VALUE_TILES[g]) * P].rearrange("p (j c d) -> p j c d", c=2, d=DH)

        def whole_program(loop, head, put_out, finish):
            head(0, 0, 0, 0, 0)

            def rest(b):
                head(1, b * PAIRS, b, 0, b)
                with loop.Fori(1, PAIRS) as hp:
                    for par in range(2):
                        head(par, b * PAIRS + hp, b, hp, b)

            with loop.Fori(0, B - 1) as b:
                rest(b)
                head(0, b * PAIRS + PAIRS, b + 1, 0, b)
                put_out(b, out_base(b), OUT_PARITY)
            rest(B - 1)
            finish()

        def wait_low(eng, g, j):
            if j >= JT:
                g, j = g + 1, j - JT
            if j in POOL_SPLITS:
                eng.wait_ge(pool_low, len(POOL_SPLITS) * g + POOL_SPLITS.index(j) + 1)
            else:
                eng.wait_ge(probs_low, len(VECTOR_SPLITS) * g + VECTOR_SPLITS.index(j) + 1)

        block = stack.enter_context(nc.Block())

        @block.sync
        def _(sp):
            for i, v in enumerate(ln):
                sp.dma_start(ln_rows[2 * i:2 * i + 2, :], v.rearrange("(k p) -> k p", p=P)).then_inc(ln_loaded, 16)
            full = CTILES - 1
            sp.dma_start(x_stage[0][:, 0:full, :], ctx_rows[0:full * P, :].rearrange("(t p) d -> p t d", p=P))\
                .then_inc(x_loaded[0], 16)
            sp.dma_start(x_stage[0][0:C_ROWS[full], full, :], ctx_rows[full * P:CT, :]).then_inc(x_loaded[0], 16)
            for i in range(2):
                sp.dma_start(w_stage[i].rearrange("p (k n) -> p k n", k=KD), weights[i]).then_inc(w_loaded[i], 16)
            for b in range(B):
                if b >= 1:
                    sp.wait_ge(z_turned, 2 * b)
                i = (b + 1) % 2
                sp.dma_start(x_stage[i], x_rows[b]).then_inc(x_loaded[i], 16)
                if b < 2:
                    sp.wait_ge(w_low, b + 1)
                    sp.dma_start(w_stage[b].rearrange("p (k n) -> p k n", k=weights[b + 2].shape[1]),
                                 weights[b + 2]).then_inc(w_loaded[b], 16)

            for dst, src, loaded in early_loads:
                sp.dma_start(dst[:, :].rearrange("p (k n) -> p k n", k=src.shape[1]), src).then_inc(loaded, 16)

            def send_max(sent, buf):
                sp.wait_ge(aux_done, sent)
                sp.dma_start(q_max[buf][DH:DH + 1, :], max_row[buf][:, :]).then_inc(max_sent, 16)

            def head(par, n, b, hp, outs):
                base = beside_odd(n, outs) if par else beside_even(n, outs)
                send_max(base + TURN[1 - par] + 1, 1 - par)

            def put_out(b, base, parity):
                for t in range(NT):
                    if t >= 2:
                        sp.wait_ge(aux_done, base + t - 1)
                    sp.dma_start(x_res[t % 2][:, :], x_rows[ds(b, 1), :, t, :].rearrange("o p d -> (o p) d"))\
                        .then_inc(res_loaded[t % 2], 16)
                    if t >= 1:
                        sp.wait_ge(aux_done, base + t)
                        sp.dma_start(x2_rows[ds(b, 1), t - 1, :, :].rearrange("o p d -> (o p) d"),
                                     x2_tile[(t - 1) % 2][:, :]).then_inc(x2_stored[(t - 1) % 2], 16)
                sp.wait_ge(aux_done, base + NT)
                sp.dma_start(x2_rows[ds(b, 1), NT - 1, :, :].rearrange("o p d -> (o p) d"),
                             x2_tile[(NT - 1) % 2][:, :]).then_inc(x2_stored[(NT - 1) % 2], 16)

            send_max(TURN["start"] + 1, 0)
            whole_program(sp, head, put_out, lambda: put_out(B - 1, LAST_OUT, FINAL_PARITY))
            for i in range(2):
                sp.wait_ge(x2_stored[i], 16 * TT // 2)

        @block.gpsimd
        def _(pool):
            nc.gpsimd.memset(ident[:, :], 0.0).then_inc(ident_ready, 1)
            pool.wait_ge(ident_ready, 1)
            nc.gpsimd.affine_select(out=ident[:, :], in_=ident[:, :], compare_op=ALU.not_equal, fill=1.0,
                                    base=0, pattern=[[-1, P]], channel_multiplier=1).then_inc(ident_ready, 1)

            for i in range(2):
                pool.wait_ge(w_high, i + 1)
                nc.gpsimd.tensor_tensor(out=wqk[1][:, :, :, i, :].rearrange("p k h d -> p (k h) d"),
                                        in0=w_stage[i].rearrange("p (k d) -> p k d", d=DH),
                                        in1=wqk[0][:, :, :, i, :].rearrange("p k h d -> p (k h) d"),
                                        op=ALU.subtract).then_inc(w_low, 1)
            for i, w in enumerate((wv, wo)):
                pool.wait_ge(w_high, i + 3)
                nc.gpsimd.tensor_tensor(out=w[1][:, :, :].rearrange("p k n -> p (k n)"), in0=w_stage[i],
                                        in1=w[0][:, :, :].rearrange("p k n -> p (k n)"), op=ALU.subtract)\
                    .then_inc(w_low, 1)

            def copy_q(idx, buf):
                pool.wait_ge(aux_high, idx * QK + 2)
                pool.sem_inc(pool_turns, 1)
                nc.gpsimd.tensor_copy(q_max[buf][0:DH, :], q_both[buf][0:DH, :]).then_inc(q_copied, 1)
                pool.wait_ge(q_copied, idx + 1)
                pool.sem_inc(pool_turns, 1)

            def move_values(par, count):
                nc.gpsimd.tensor_copy(values[par][:, :, 0:3:2, :], values_pair[:, :, par, :, :])\
                    .then_inc(values_moved[par], 1)
                pool.wait_ge(values_moved[par], count)
                pool.sem_inc(pool_turns, 1)

            def split(g, j):
                pool.wait_ge(probs_high, JT * g + j + 1)
                r = key_rows(j)
                nc.gpsimd.tensor_tensor(out=probs_split[1][j % SPLITS][0:r, :], in0=probs[j % 2][0:r, :],
                                        in1=probs_split[0][j % SPLITS][0:r, :], op=ALU.subtract).then_inc(pool_low, 1)

            def head(par, n, b, hp, outs):
                for j in POOL_SPLITS[:POOL_FIRST]:
                    split(2 * n + par, j)
                if par == 0:
                    if not isinstance(n, int):
                        pool.wait_ge(av_done, SPLITS + 2 * JT * n)
                        pool.sem_inc(pool_turns, 1)
                    move_values(1, n + 1)
                else:
                    pool.wait_ge(aux_done, beside_even(n, outs) + LAST_VALUES[1] + 1)
                    pool.wait_ge(av_done, SPLITS + 2 * JT * n + JT)
                    pool.sem_inc(pool_turns, 1)
                    move_values(0, n + 2)
                for j in POOL_SPLITS[POOL_FIRST:]:
                    split(2 * n + par, j)
                copy_q(2 * n + 2 + par, par)

            copy_q(0, 0)
            pool.wait_ge(aux_done, LAST_VALUES["start"] + 1)
            move_values(0, 1)
            copy_q(1, 1)
            whole_program(pool, head, lambda b, base, parity: None, lambda: None)

        @block.scalar
        def _(act):
            for i in range(2):
                act.wait_ge(w_loaded[i], 16)
                nc.scalar.activation(wqk[0][:, :, :, i, :].rearrange("p k h d -> p (k h) d"),
                                     w_stage[i].rearrange("p (k d) -> p k d", d=DH), ACT.Copy).then_inc(w_high, 1)

            def late_weight(i):
                w = (wv, wo)[i]
                act.wait_ge(w_loaded[i], 32)
                nc.scalar.activation(w[0][:, :, :].rearrange("p k n -> p (k n)"), w_stage[i], ACT.Copy)\
                    .then_inc(w_high, 1)

            def root(group):
                act.wait_ge(var_ready, group + 1)
                if group == 0:
                    nc.scalar.activation(std[:, 0:CTILES], mean_var[:, 0:CTILES, 1], ACT.Sqrt, bias=eps_col[:, :])\
                        .then_inc(std_ready, 1)
                else:
                    nc.scalar.activation(std[:, 0:NT], mean_var[:, 0:NT, 1], ACT.Sqrt, scale=1.0 + EPS,
                                         bias=eps_square[:, :]).then_inc(std_ready, 1)

            def affine(group):
                param, dst, halves = group_of(group)
                for i, cols in enumerate(halves):
                    act.wait_ge(z_turned, 2 * group + i + 1)
                    if group >= 1:
                        act.wait_ge(z_low, 2 * group - 1 + i)
                    for k in range(KD):
                        last = nc.scalar.activation(probs[i][:, k * HALF:k * HALF + cols],
                                                    score[i][:, k * HALF:k * HALF + cols], ACT.Identity,
                                                    scale=ln_cols[:, param + k:param + k + 1],
                                                    bias=ln_cols[:, param + 2 + k:param + 3 + k])
                    last.then_inc(z_affine, 1)
                    act.wait_ge(z_affine, 2 * group + i + 1)
                    src = probs[i][:, :].rearrange("p (k c) -> p k c", k=KD)[:, :, 0:cols]
                    nc.scalar.activation(dst(0, i, cols), src, ACT.Copy).then_inc(z_high, 1)

            act.wait_ge(ones_ready, 1)
            root(0)
            act.wait_ge(ln_ready, 1)
            for group in range(B + 1):
                if group < B:
                    root(group + 1)
                affine(group)
                if group in (1, 2):
                    late_weight(group - 1)

            def high_parts(name, base, n, slots):
                for s in slots:
                    for place, chunk in AHEAD[name][s]:
                        bank = aux_bank(name, place)
                        if chunk[0] == "qk":
                            act.wait_ge(aux_full, base + place + 1)
                            of = chunk[2]
                            lo = chunk[1] * HALF
                            hi = min(lo + HALF, KEYS)
                            last = nc.scalar.activation(k_high[of][DH:P, lo:hi], bank[DH:P, 0:hi - lo], ACT.Copy)
                            if lo < N:
                                last = nc.scalar.activation(q_both[of][0:DH, lo:hi], bank[0:DH, 0:hi - lo], ACT.Copy)
                            last.then_inc(aux_high, 1)
                        elif chunk[0] == "v":
                            act.wait_ge(aux_full, base + place + 1)
                            if name != "start" and chunk[1] == 0:
                                act.wait_ge(values_moved[1], n + 1)
                            for js, r in value_groups(chunk[1]):
                                both = value_bank(bank, chunk[1])
                                a = js[0] - VALUE_TILES[chunk[1]][0]
                                last = nc.scalar.activation(
                                    values_pair[0:r, js[0]:js[-1] + 1, :, 0, :],
                                    both[0:r, a:a + len(js), :, :], ACT.Copy)
                            last.then_inc(values_high, 1)

            def exponent(tile, j, g=None):
                act.wait_ge(score_full, tile + 1)
                if g is not None:
                    wait_low(act, g, j)
                j = (j + AHEAD_STEPS) % JT if g is not None else j
                r = key_rows(j)
                nc.scalar.activation(probs[j % 2][0:r, :], score[j % 2][0:r, :], ACT.Exp, scale=SCALE)\
                    .then_inc(exp_done, 1)

            def probs_high_half(tile, j):
                r = key_rows(j)
                act.wait_ge(exp_done, tile + 3)
                act.wait_ge(av_done, tile + 1)
                nc.scalar.activation(probs_split[0][j % SPLITS][0:r, :], probs[j % 2][0:r, :], ACT.Copy)\
                    .then_inc(probs_high, 1)

            def head(par, n, b, hp, outs):
                g = 2 * n + par
                nxt = 1 - par
                base = beside_odd(n, outs) if par else beside_even(n, outs)
                for j in range(JT):
                    high_parts(nxt, base, n, (4 * j, 4 * j + 1))
                    exponent(JT * g + j + AHEAD_STEPS, j, g)
                    probs_high_half(JT * g + j + AHEAD_STEPS, (j + AHEAD_STEPS) % JT)
                    high_parts(nxt, base, n, (4 * j + 2, 4 * j + 3))
                act.wait_ge(av_done, JT * g + JT + SPLITS)
                act.wait_ge(rows_taken, g)
                nc.scalar.activation(head_sums[:, :, :, :].rearrange("p i t c -> p i (t c)"), sums_in_acc,
                                     ACT.Copy).then_inc(acc_copied, 1)

            def put_out(b, base, parity):
                for t in range(NT):
                    act.wait_ge(att_turned, b * NT + t + 1)
                    act.sem_inc(act_turns, 1)
                    nc.scalar.activation(att_cols[0][t % 2][:, :, :].rearrange("p k t -> p (k t)"), acc[:, :],
                                         ACT.Copy).then_inc(att_high, 1)

            high_parts("start", 0, 0, range(SLOTS))
            for j in range(AHEAD_STEPS):
                exponent(j, j)
                probs_high_half(j, j)
            whole_program(act, head, put_out, lambda: put_out(B - 1, 0, 0))

        @block.vector
        def _(dve):
            for i in range(2):
                nc.vector.memset(values[i][:, :, 1, :], 1.0)
                nc.vector.memset(k_low[i][DH:DH + 1, :], 1.0)
            nc.vector.memset(values_pair[:, :, :, :, :], 0.0)
            nc.vector.memset(eps_square[:, :], EPS * EPS)
            nc.vector.memset(eps_col[:, :], EPS).then_inc(ones_ready, 1)
            nc.vector.memset(mean_var[:, :, :], 1.0).then_inc(z_step, 1)
            dve.wait_ge(z_step, 1)
            dve.wait_ge(ln_turned, 1)
            nc.vector.tensor_copy(ln_cols[:, :], aux[0][:, 0:8]).then_inc(ln_ready, 1)
            dve.wait_ge(ln_ready, 1)

            steps = Steps(z_step, 1)

            def normalise(group):
                rows, tiles = (x_stage[0], C_ROWS) if group == 0 else (x_stage[group % 2], [P] * NT)
                for t, r in enumerate(tiles):
                    last = nc.vector.bn_stats(stats[0:r, t, :], rows[0:r, t, :])
                steps.mark(last)
                dve.wait_ge(z_step, steps.reached())
                for t, r in enumerate(tiles):
                    last = nc.vector.bn_aggr(mean_var[0:r, t, :], stats[0:r, t, :])
                last.then_inc(var_ready, 1)
                dve.wait_ge(std_ready, group + 1)
                steps.mark(nc.vector.reciprocal(rstd[:, 0:len(tiles)], std[:, 0:len(tiles)]))
                dve.wait_ge(z_step, steps.reached())
                for t, r in enumerate(tiles):
                    last = nc.vector.tensor_scalar(rows[0:r, t, :], rows[0:r, t, :], mean_var[0:r, t, 0:1],
                                                   rstd[0:r, t:t + 1], ALU.subtract, ALU.mult)
                last.then_inc(z_ready, 1)

            def split(group):
                _, dst, halves = group_of(group)
                for i, cols in enumerate(halves):
                    dve.wait_ge(z_high, 2 * group + i + 1)
                    nc.vector.tensor_tensor(out=dst(1, i, cols),
                                            in0=probs[i][:, :].rearrange("p (k c) -> p k c", k=KD)[:, :, 0:cols],
                                            in1=dst(0, i, cols), op=ALU.subtract).then_inc(z_low, 1)

            dve.wait_ge(x_loaded[0], 32)
            normalise(0)
            for b in range(B):
                dve.wait_ge(x_loaded[(b + 1) % 2], 16 * (b // 2 + 1) + (32 if b % 2 else 0))
                normalise(b + 1)
                split(b)
            split(B)

            def consume(name, idx, base, n, slots):
                par = 1 if name == 1 else 0
                for s in slots:
                    for place, chunk in AHEAD[name][s]:
                        bank = aux_bank(name, place)
                        kind = chunk[0]
                        if kind == "qk":
                            of = chunk[2]
                            lo = chunk[1] * HALF
                            hi = min(lo + HALF, KEYS)
                            dve.wait_ge(aux_high, QK * (idx + chunk[3]) + chunk[1] + 1)
                            if lo < N:
                                nc.vector.tensor_tensor(out=q_both[of][DH:P, lo:hi], in0=bank[0:DH, 0:hi - lo],
                                                        in1=q_both[of][0:DH, lo:hi], op=ALU.subtract)
                            nc.vector.tensor_copy(k_high[of][0:DH, lo:hi], k_high[of][DH:P, lo:hi])
                            nc.vector.tensor_tensor(out=k_low[of][0:DH, lo:hi], in0=bank[DH:P, 0:hi - lo],
                                                    in1=k_high[of][DH:P, lo:hi], op=ALU.subtract)\
                                .then_inc(aux_done, 1)
                            continue
                        if kind == "v":
                            dve.wait_ge(values_high, len(VALUE_TILES) * n + chunk[1] + 1)
                            for js, r in value_groups(chunk[1]):
                                both = value_bank(bank, chunk[1])
                                a = js[0] - VALUE_TILES[chunk[1]][0]
                                last = nc.vector.tensor_tensor(out=values_pair[0:r, js[0]:js[-1] + 1, :, 1, :],
                                                               in0=both[0:r, a:a + len(js), :, :],
                                                               in1=values_pair[0:r, js[0]:js[-1] + 1, :, 0, :],
                                                               op=ALU.subtract)
                            last.then_inc(aux_done, 1)
                            continue
                        dve.wait_ge(aux_full, base + place + 1)
                        if kind == "max":
                            _, t, c = chunk
                            nc.vector.tensor_reduce(max_parts[:, t, c:c + 1], bank[:, :], AX.X, ALU.max)\
                                .then_inc(aux_done, 1)
                        elif kind == "tail":
                            ts = MAX_TAILS[chunk[1]]
                            nc.vector.tensor_reduce(max_parts[:, ts[0]:ts[-1] + 1, 2],
                                                    bank[:, 0:C * len(ts)].rearrange("p (t c) -> p t c", c=C),
                                                    AX.X, ALU.max).then_inc(aux_done, 1)
                            if chunk[1] == len(MAX_TAILS) - 1:
                                dve.wait_ge(aux_done, base + place + 1)
                                nc.vector.tensor_reduce(neg_max[:, :], max_parts[:, :, :], AX.X, ALU.max,
                                                        negate=True).then_inc(max_ready, 1)
                        elif kind == "turn":
                            nc.vector.tensor_copy(max_row[par][:, :], bank[0:NT, 0:P]).then_inc(aux_done, 1)

            def take_rows(g, head_col):
                dve.wait_ge(acc_copied, g + 2)
                nc.vector.reciprocal(recip[:, :].rearrange("p (i t) -> p i t", i=2), head_sums[:, :, :, DH])\
                    .then_inc(recip_done, 1)
                dve.wait_ge(recip_done, g + 1)
                nc.vector.tensor_tensor(
                    out=att_rows[:, :, ds(head_col, 1), :].rearrange("p t o d -> p t (o d)"),
                    in0=head_sums[:, :, :, 0:DH].rearrange("p i t d -> p (i t) d"),
                    in1=recip[:, :].unsqueeze(2).to_broadcast([P, NT, DH]), op=ALU.mult).then_inc(rows_taken, 1)

            def probs_low_half(tile, j):
                r = key_rows(j)
                dve.wait_ge(probs_high, tile + 1)
                nc.vector.tensor_tensor(out=probs_split[1][j % SPLITS][0:r, :], in0=probs[j % 2][0:r, :],
                                        in1=probs_split[0][j % SPLITS][0:r, :], op=ALU.subtract).then_inc(probs_low, 1)

            def head(par, n, b, hp, outs):
                g = 2 * n + par
                nxt = 1 - par
                base = beside_odd(n, outs) if par else beside_even(n, outs)
                before = 2 * hp if par else ((2 * hp + H - 1) & (H - 1) if not isinstance(hp, int)
                                             else (2 * hp + H - 1) % H)
                for j in range(JT):
                    consume(nxt, g + 1, base, n + 1, (4 * j, 4 * j + 1))
                    if (j + 1) % JT in VECTOR_SPLITS:
                        probs_low_half(JT * g + j + 1, (j + 1) % JT)
                    if j == 0 and not (isinstance(g, int) and g == 0):
                        take_rows(g - 1, before)
                    consume(nxt, g + 1, base, n + 1, (4 * j + 2, 4 * j + 3))

            def put_out(b, base, parity):
                for t in range(NT):
                    dve.wait_ge(att_high, b * NT + t + 1)
                    nc.vector.tensor_tensor(out=att_cols[1][t % 2][:, :, :].rearrange("p k t -> p (k t)"),
                                            in0=acc[:, :],
                                            in1=att_cols[0][t % 2][:, :, :].rearrange("p k t -> p (k t)"),
                                            op=ALU.subtract).then_inc(att_low, 1)
                    if t >= 1:
                        add_residual(b, base, parity, t - 1)
                add_residual(b, base, parity, NT - 1)
                for i in range(2):
                    dve.wait_ge(x2_stored[i], 16 * (b + 1) * (NT // 2))
                    dve.sem_inc(dve_turns, 1)

            def add_residual(b, base, parity, t):
                dve.wait_ge(aux_full, base + t + 1)
                dve.wait_ge(res_loaded[t % 2], 16 * (b * (NT // 2) + t // 2 + 1))
                if t >= 2:
                    dve.wait_ge(x2_stored[t % 2], 16 * (b * (NT // 2) + t // 2))
                nc.vector.tensor_tensor(out=x2_tile[t % 2][:, :], in0=aux[(parity + t) % 2][:, 0:D],
                                        in1=x_res[t % 2][:, :], op=ALU.add).then_inc(aux_done, 1)
                dve.wait_ge(aux_done, base + t + 1)
                nc.vector.bn_stats(x2_stats[:, ds(b * NT + t, 1), :].rearrange("p o c -> p (o c)"), x2_tile[t % 2][:, :])

            def finish():
                take_rows(B * H - 1, H - 1)
                put_out(B - 1, LAST_OUT, FINAL_PARITY)

            consume("start", 0, 0, 0, range(SLOTS))
            probs_low_half(0, 0)
            whole_program(dve, head, put_out, finish)

        @block.tensor
        def _(pe):
            pe.sem_inc(av_done, SPLITS)
            pe.sem_inc(exp_done, 2)
            pe.sem_inc(acc_copied, 1)
            pe.wait_ge(ident_ready, 2)
            pe.wait_ge(ln_loaded, 64)
            nc.tensor.transpose(aux[0][:, 0:8], ln_rows[:, :], ident[0:8, 0:8]).then_inc(ln_turned, 1)

            def turn(rows, group, halves):
                pe.wait_ge(z_ready, group + 1)
                t = 0
                for i, half in enumerate(halves):
                    if group >= 1:
                        pe.wait_ge(z_affine, 2 * group + i - 1)
                    for q, r in enumerate(half):
                        for k in range(KD):
                            lo = k * HALF + q * P
                            last = nc.tensor.transpose(score[i][:, lo:lo + r], rows[0:r, t, k * P:k * P + P],
                                                       ident[0:r, 0:r])
                        t += 1
                    last.then_inc(z_turned, 1)

            turn(x_stage[0], 0, C_HALVES)
            for group in range(1, B + 1):
                turn(x_stage[group % 2], group, X_HALVES)
            pe.wait_ge(z_low, 2 * (B + 1))
            pe.wait_ge(w_low, 3)
            pe.wait_ge(ones_ready, 1)

            def summed(out, pairs):
                for i, (a, b) in enumerate(pairs):
                    last = nc.tensor.matmul(out, a, b, start=(i == 0), stop=(i == len(pairs) - 1))
                return last

            def produce(name, idx, base, batch, pair, slots):
                par = 1 if name == 1 else 0
                for s in slots:
                    for place, chunk in AHEAD[name][s]:
                        bank = aux_bank(name, place)
                        if not (isinstance(base, int) and base + place < 2):
                            pe.wait_ge(aux_done, base + place - 1)
                        kind = chunk[0]
                        if kind == "qk":
                            c = chunk[1]
                            if c < 2:
                                cols = HALF
                                rhs = [[z[:, k, ds(batch * N + c * HALF, HALF)] for z in zx] for k in range(KD)]
                            else:
                                cols = C
                                rhs = [[z[:, k, ds(batch * C, C)] for z in zc] for k in range(KD)]
                            pairs = []
                            for k in range(KD):
                                lhs = [m[:, k, ds(2 * pair + chunk[2], 1), :, :].rearrange("p o c d -> p (o c d)") for m in wqk]
                                pairs += [(lhs[0], rhs[k][0]), (lhs[0], rhs[k][1]), (lhs[1], rhs[k][0])]
                            last = summed(bank[:, 0:cols], pairs)
                        elif kind == "max":
                            _, t, c = chunk
                            if t == 0 and c == 0:
                                pe.wait_ge(aux_done, base + (QK if name == "start" else 0))
                            last = summed(bank[:, :], [(q_both[par][:, t * P:t * P + P],
                                                        k_high[par][:, c * HALF:c * HALF + HALF])])
                        elif kind == "tail":
                            for i, t in enumerate(MAX_TAILS[chunk[1]]):
                                last = summed(bank[:, i * C:i * C + C],
                                              [(q_both[par][:, t * P:t * P + P], k_high[par][:, N:KEYS])])
                        elif kind == "turn":
                            pe.wait_ge(max_ready, idx + 1)
                            last = nc.tensor.transpose(bank[0:NT, 0:P], neg_max[:, :], ident[:, :])
                        else:
                            js = VALUE_TILES[chunk[1]]
                            for i, j in enumerate(js):
                                r = key_rows(j)
                                pairs = []
                                for k in range(KD):
                                    if j < NT:
                                        lhs = [z[:, k, ds(batch * N + j * P, r)] for z in zx]
                                    else:
                                        lhs = [z[:, k, ds(batch * C + (j - NT) * P, r)] for z in zc]
                                    rhs = [m[:, k, ds(pair * P, P)] for m in wv]
                                    pairs += [(lhs[0], rhs[0]), (lhs[0], rhs[1]), (lhs[1], rhs[0])]
                                last = summed(bank[0:r, i * P:i * P + P], pairs)
                        last.then_inc(aux_full, 1)

            def scores(name, idx, base, tile, j, i):
                par = 1 if name == 1 else 0
                if i == 0:
                    pe.wait_ge(exp_done, tile + 1)
                    if j == 0:
                        pe.wait_ge(aux_done, base + TURN[name] + 1)
                        pe.wait_ge(q_copied, idx + 1)
                        pe.wait_ge(max_sent, 16 * (idx + 1))
                r = key_rows(j)
                cols = slice(i * HALF, i * HALF + HALF)
                last = summed(score[j % 2][0:r, cols], [(k_high[par][:, j * P:j * P + r], q_both[par][:, cols]),
                                                        (k_low[par][:, j * P:j * P + r], q_max[par][:, cols])])
                if i == 1:
                    last.then_inc(score_full, 1)

            def weigh(par, g, n, j, i):
                if i == 0:
                    wait_low(pe, g, j)
                    if j == 0:
                        pe.wait_ge(acc_copied, g + 1)
                        pe.wait_ge(values_moved[par], n + 1)
                r = key_rows(j)
                value = values[par][0:r, j, :, :].rearrange("p c d -> p (c d)")
                for q in range(NT // 2):
                    out = sums_in_acc[:, i, q * (DH + 1):(q + 1) * (DH + 1)]
                    t = i * (NT // 2) + q
                    high, low = [p[j % SPLITS][0:r, t * P:t * P + P] for p in probs_split]
                    nc.tensor.matmul(out, high, value[:, 0:DH + 1], start=(j == 0 and q == 0), stop=False)
                    nc.tensor.matmul(out[:, 0:DH], high, value[:, P:P + DH], start=False, stop=False)
                    last = nc.tensor.matmul(out, low, value[:, 0:DH + 1], start=False,
                                            stop=(j == JT - 1 and q == NT // 2 - 1))
                if i == 1:
                    last.then_inc(av_done, 1)

            def head(par, n, b, hp, outs):
                g = 2 * n + par
                nxt = 1 - par
                base = beside_odd(n, outs) if par else beside_even(n, outs)
                m = n + 1
                batch = pe.snap((m >> 3) & (B - 1)) if not isinstance(m, int) else (m // PAIRS) % B
                pair = pe.snap(m & (PAIRS - 1)) if not isinstance(m, int) else m % PAIRS
                for j in range(JT):
                    jj = j + AHEAD_STEPS
                    for i in range(2):
                        if jj < JT:
                            scores(par, g, None, JT * g + jj, jj, i)
                        else:
                            scores(nxt, g + 1, base, JT * g + jj, jj - JT, i)
                        produce(nxt, g + 1, base, batch, pair, (4 * j + i,))
                    for i in range(2):
                        weigh(par, g, n, j, i)
                        produce(nxt, g + 1, base, batch, pair, (4 * j + 2 + i,))

            def turn_tile(b, t):
                if t >= 1:
                    pe.wait_ge(att_low, b * NT + t)
                for k in range(INNER // P):
                    last = nc.tensor.transpose(acc[:, k * P:k * P + P], att_rows[:, t, 2 * k:2 * k + 2, :]
                                               .rearrange("p h d -> p (h d)"), ident[:, :])
                last.then_inc(att_turned, 1)

            def project(b, base, parity, t):
                pe.wait_ge(att_low, b * NT + t + 1)
                pe.wait_ge(aux_done, base + t - 1)
                pairs = []
                for k in range(INNER // P):
                    lhs = [a[t % 2][:, k, :] for a in att_cols]
                    rhs = [w[:, k, :] for w in wo]
                    pairs += [(lhs[0], rhs[0]), (lhs[0], rhs[1]), (lhs[1], rhs[0])]
                summed(aux[(parity + t) % 2][:, 0:D], pairs).then_inc(aux_full, 1)

            def put_out(b, base, parity):
                pe.wait_ge(w_low, 4)
                pe.wait_ge(rows_taken, H * (b + 1))
                pe.wait_ge(acc_copied, heads_before_out(b))
                turn_tile(b, 0)
                for t in range(NT):
                    if t + 1 < NT:
                        turn_tile(b, t + 1)
                    project(b, base, parity, t)

            def heads_before_out(b):
                return min(H * (b + 1) + 1, B * H) + 1 if isinstance(b, int) else H * (b + 1) + 2

            def finish():
                put_out(B - 1, LAST_OUT, FINAL_PARITY)

            produce("start", 0, 0, 0, 0, range(SLOTS))
            for j in range(AHEAD_STEPS):
                for i in range(2):
                    scores("start", 0, 0, j, j, i)
            whole_program(pe, head, put_out, finish)


def experts(nc, x2_dram, x2_stats, stage, e_loaded, Wg, bg, W1, b1, W2, b2, out):
    x2_tiles = x2_dram.rearrange("(b t p) d -> b p t d", b=B, p=P)
    out_rows = out.rearrange("b n d -> (b n) d")
    KF = F // P
    GROUP = 4
    BANK = HALF // P
    META = 4
    OWN = 4

    stack = ExitStack()
    with stack:
        def sb(name, shape, dt):
            return stack.enter_context(nc.sbuf_tensor(name, shape, dt))

        def pb(name, shape, dt):
            return stack.enter_context(nc.psum_tensor(name, shape, dt))

        def sem(name):
            return stack.enter_context(nc.semaphore(name))

        ident = sb("e_ident", [P, P], F32)
        w1 = [sb(f"w1_{i}", [P, E, KD, F], F16) for i in range(2)]
        w2 = [sb(f"w2_{i}", [P, E, KF, D], F16) for i in range(2)]
        b2_all = sb("b2_all", [P, E, D], F32)
        b1_rows = sb("b1_rows", [E * KF, P], F32)
        b1_cols = sb("b1_cols", [P, E * KF], F32)
        wg = sb("wg", [P, KD, E], F32)
        bg_all = sb("bg_all", [P, E], F32)
        eps_col = sb("e_eps_col", [P, 1], F32)
        x2_all = sb("x2_all", [P, TT, D], F32)
        shared = x2_all[:, :, :].rearrange("p t d -> p (t d)")
        hidden = [shared[:, i * F:i * F + F] for i in range(2)]
        hidden_split = [[shared[:, (4 + 2 * h + i) * (F // 2):(5 + 2 * h + i) * (F // 2)].bitcast(F16)
                         .rearrange("p (k t) -> p k t", t=P) for i in range(2)] for h in range(2)]
        base = 8 * (F // 2)
        own_rows = [shared[:, base + i * D:base + i * D + D] for i in range(OWN)]
        base += OWN * D
        z_rows = [shared[:, base + i * D:base + i * D + D] for i in range(2)]
        base += 2 * D
        y_rows = [shared[:, base + i * D:base + i * D + D] for i in range(OWN)]
        base += OWN * D
        biased = [shared[:, base + i * D:base + i * D + D] for i in range(2)]
        base += 2 * D
        z_split = [[shared[:, base + (2 * h + i) * (D // 2):base + (2 * h + i + 1) * (D // 2)].bitcast(F16)
                    .rearrange("p (k t) -> p k t", t=P) for i in range(2)] for h in range(2)]
        base += 4 * (D // 2)
        z_groups = sb("z_groups", [P, 2 * GROUP * D], F32)
        z_group = [z_groups[:, i * GROUP * D:(i + 1) * GROUP * D].rearrange("p (t d) -> p t d", d=D) for i in range(2)]
        QUARTER = TT // 4
        SPREAD = QUARTER * SORTED * META
        lanes = [shared[:, q * QUARTER * P:(q + 1) * QUARTER * P].rearrange("p (t c) -> p t c", c=P) for q in range(4)]
        spread = [shared[:, TT * P + q * SPREAD:TT * P + (q + 1) * SPREAD] for q in range(3)] + [z_groups[:, 0:SPREAD]]
        spread = [v.rearrange("p (t s c) -> p t s c", s=SORTED, c=META) for v in spread]
        z_cols = [sb("z_cols", [P, GROUP, KD, P], F32),
                  b2_all[:, 0:GROUP * KD * P // D, :].rearrange("p (t k) (h c) -> p t (k h) c", k=1, c=P)]
        mean_var = sb("e_mean_var", [P, TT, 2], F32)
        std = sb("e_std", [P, TT], F32)
        rstd = sb("e_rstd", [P, TT], F32)
        logits = sb("logits", [P, TT, E], F32)
        top = sb("top", [P, TT], F32)
        work = [sb(f"work{i}", [P, TT, E], F32) for i in range(3)]
        chosen = sb("chosen", [P, TT, E], F16)
        first = sb("first", [P, TT], F32)
        e_less = sb("e_less", [P, E], F32)
        counts = sb("counts", [P, E], F32)
        counts_i = sb("counts_i", [P, E], I32)
        ends = [sb(f"ends{i}", [P, E], F32) for i in range(2)]
        place = sb("place", [P, TT], F32)
        place_i = sb("place_i", [P, TT], I32)
        token = sb("token", [P, TT], F32)
        place_tile = sb("place_tile", [P, TT], F32)
        place_lane = sb("place_lane", [P, TT], F32)
        lane = sb("lane", [P, P], F32)
        z_words = z_cols[0][:, :, :, :].rearrange("p t k c -> p (t k c)")
        MARKS = QUARTER * SORTED
        in_tile = [z_words[:, q * MARKS:(q + 1) * MARKS] for q in range(3)] + \
            [z_groups[:, SPREAD + SORTED * E:SPREAD + SORTED * E + MARKS]]
        in_tile = [v.rearrange("p (t s) -> p t s", s=SORTED) for v in in_tile]
        rows = sb("rows", [P, TT, META], F32)
        upper = sb("upper", [P, P], F16)
        ones = sb("ones", [P, P], F16)
        meta = sb("meta", [P, SORTED, META], F32)
        owner = sb("owner", [P, SORTED], F32)
        write_i = sb("write_i", [P, SORTED], I32)
        read_i = sb("read_i", [P, SORTED], I32)
        starts = sb("starts", [P, SORTED], F32)
        past = z_groups[:, SPREAD:SPREAD + SORTED * E].rearrange("p (t e) -> p t e", e=E)
        tile_f = sb("tile_f", [P, SORTED], F32)
        tile_expert = sb("tile_expert", [P, SORTED], I32)
        read_col = [sb(f"read_col{i}", [P, 1], I32) for i in range(OWN)]
        write_col = [sb(f"write_col{i}", [P, 1], I32) for i in range(OWN)]

        turned = [pb(f"turned{i}", [P, HALF], F32) for i in range(2)]
        up = [pb(f"up{i}", [P, F], F32) for i in range(2)]
        down = [pb(f"down{i}", [P, HALF], F32) for i in range(2)]

        c_step = sem("c_step")
        consts = sem("consts")
        small_loaded = sem("small_loaded")
        b2_loaded = sem("b2_loaded")
        b1_turned = sem("b1_turned")
        b1_ready = sem("b1_ready")
        x2_loaded = [sem(f"x2_loaded{b}") for b in range(B)]
        r_step = sem("r_step")
        r_var = sem("r_var")
        r_std = sem("r_std")
        g_rows = sem("g_rows")
        g_turned = sem("g_turned")
        g_cols = sem("g_cols")
        g_logits = sem("g_logits")
        g_taken = sem("g_taken")
        shifted = sem("shifted")
        powers = sem("powers")
        chosen_ready = sem("chosen_ready")
        ranks = sem("ranks")
        e_high = sem("e_high")
        w1_low = sem("w1_low")
        w2_low = sem("w2_low")
        rows_spread = sem("rows_spread")
        meta_summed = sem("meta_summed")
        meta_ready = sem("meta_ready")
        read_step = sem("read_step")
        write_step = sem("write_step")
        gathered = [sem(f"gathered{i}") for i in range(OWN)]
        scattered = [sem(f"scattered{i}") for i in range(OWN)]
        z_ready = sem("e_z_ready")
        z_turned = sem("e_z_turned")
        z_high = sem("e_z_high")
        z_done = sem("e_z_done")
        up_full = sem("up_full")
        silu_done = sem("silu_done")
        h_high = sem("h_high")
        h_done = sem("h_done")
        down_full = sem("down_full")
        bias_added = sem("bias_added")
        y_ready = sem("y_ready")
        turns = {e: sem("e_turns_" + e) for e in ("pool", "dve", "act")}

        def at_least(eng, s, value, carry=None):
            if isinstance(value, int) and value <= 0:
                return
            eng.wait_ge(s, value)
            if carry and not isinstance(value, int):
                eng.sem_inc(turns[carry], 1)

        def tile_steps(eng, step):
            for u in range(OWN):
                step(0, u)
            with eng.Fori(1, SORTED // OWN - 1) as i:
                for u in range(OWN):
                    step(i, u)
            for u in range(OWN):
                step(SORTED // OWN - 1, u)

        def number(i, u):
            return OWN * i + u

        def halves_of(split, half):
            return split[:, half * BANK:half * BANK + BANK, :].rearrange("p k t -> p (k t)")

        def exists(i, u):
            return not (isinstance(i, int) and number(i, u) >= SORTED)

        block = stack.enter_context(nc.Block())

        def low_half(engine, w, e, i, done):
            high, low = [m[:, ds(e, 1), :, :].rearrange("p o k n -> p (o k n)") for m in w]
            engine.tensor_tensor(out=low, in0=stage[i][:, :], in1=high, op=ALU.subtract).then_inc(done, 1)

        @block.sync
        def _(sp):
            for b in range(B):
                sp.dma_start(x2_all[:, b * NT:b * NT + NT, :], x2_tiles[b]).then_inc(x2_loaded[b], 16)
            sp.dma_start(b1_rows[:, :], b1.rearrange("e (k p) -> (e k) p", p=P)).then_inc(small_loaded, 16)
            sp.dma_start(wg[:, :, :], Wg.rearrange("(k p) e -> p k e", p=P)).then_inc(small_loaded, 16)
            sp.dma_start(bg_all[:, :], bg.rearrange("(o e) -> o e", o=1).to_broadcast([P, E])).then_inc(small_loaded, 16)
            w1_rows = W1.rearrange("e (k p) n -> e p k n", p=P)
            w2_rows = W2.rearrange("e (k p) n -> e p k n", p=P)

            def load(e, i, src):
                dst = stage[i][:, :].rearrange("p (k n) -> p k n", k=src.shape[2])
                sp.dma_start(dst, src[ds(e, 1), :, :, :].rearrange("o p k n -> (o p) k n")).then_inc(e_loaded[i], 16)

            with sp.Fori(1, E) as e:
                sp.wait_ge(w1_low, e)
                load(e, 0, w1_rows)
                sp.wait_ge(w2_low, e)
                load(e, 1, w2_rows)
            sp.wait_ge(g_logits, 2 + TT // GROUP)
            sp.dma_start(b2_all[:, :, :].rearrange("p e d -> p (e d)"),
                         b2.rearrange("(o e) d -> o (e d)", o=1).to_broadcast([P, E * D])).then_inc(b2_loaded, 16)

        @block.gpsimd
        def _(pool):
            nc.gpsimd.memset(ident[:, :], 0.0).then_inc(c_step, 1)
            nc.gpsimd.memset(ones[:, :], 1.0).then_inc(c_step, 1)
            pool.wait_ge(c_step, 2)
            nc.gpsimd.affine_select(out=ident[:, :], in_=ident[:, :], compare_op=ALU.not_equal, fill=1.0,
                                    base=0, pattern=[[-1, P]], channel_multiplier=1).then_inc(c_step, 1)
            nc.gpsimd.affine_select(out=upper[:, :], in_=ones[:, :], compare_op=ALU.is_gt, fill=0.0,
                                    base=0, pattern=[[1, P]], channel_multiplier=-1).then_inc(c_step, 1)
            nc.gpsimd.iota(e_less[:, :], [[1, E]], base=-E, channel_multiplier=0,
                           allow_small_or_imprecise_dtypes=True).then_inc(c_step, 1)
            nc.gpsimd.iota(starts[:, :], [[P, SORTED]], base=0, channel_multiplier=0,
                           allow_small_or_imprecise_dtypes=True).then_inc(c_step, 1)
            nc.gpsimd.iota(lane[:, :], [[1, P]], base=0, channel_multiplier=0,
                           allow_small_or_imprecise_dtypes=True).then_inc(c_step, 1)
            nc.gpsimd.iota(token[:, :], [[P, TT]], base=-NOBODY, channel_multiplier=1,
                           allow_small_or_imprecise_dtypes=True).then_inc(c_step, 1)
            pool.wait_ge(c_step, 8)
            nc.gpsimd.memset(eps_col[:, :], EPS).then_inc(consts, 1)
            def split(i, e, w, done):
                pool.wait_ge(e_high, 2 * e + i + 1)
                pool.sem_inc(turns["pool"], 1)
                low_half(nc.gpsimd, w, e, i, done)

            with pool.Fori(0, E) as e:
                split(0, e, w1, w1_low)
            pool.wait_ge(meta_ready, 1)

            def gather(i, u):
                if not exists(i, u):
                    return
                q, k = u % OWN, number(i, u)
                nc.gpsimd.tensor_copy(read_col[q][:, :], read_i[:, ds(k, 1)]).then_inc(read_step, 1)
                at_least(pool, read_step, k + 1, "pool")
                nc.gpsimd.indirect_dma_start(out=own_rows[q], out_offset=None, in_=x2_dram,
                                             in_offset=bass.IndirectOffsetOnAxis(read_col[q][:, :], 0))\
                    .then_inc(gathered[q], 16)

            def step(i, u):
                k = number(i, u)
                at_least(pool, scattered[u], 16 * i, "pool")
                nc.gpsimd.tensor_copy(write_col[u][:, :], write_i[:, ds(k, 1)]).then_inc(write_step, 1)
                at_least(pool, write_step, k + 1, "pool")
                at_least(pool, y_ready, k + 1, "pool")
                nc.gpsimd.indirect_dma_start(out=out_rows, out_offset=bass.IndirectOffsetOnAxis(write_col[u][:, :], 0),
                                             in_=y_rows[u], in_offset=None, bounds_check=TOK - 1,
                                             oob_is_err=False).then_inc(scattered[u], 16)
                gather(i, u + OWN)

            for u in range(OWN):
                gather(0, u)
            tile_steps(pool, step)
            for q in range(OWN):
                pool.wait_ge(scattered[q], 16 * (SORTED // OWN))

        @block.scalar
        def _(act):
            def high_weights(e):
                for i, w in enumerate((w1, w2)):
                    act.wait_ge(e_loaded[i], 16 * (e + 1))
                    act.sem_inc(turns["act"], 1)
                    nc.scalar.activation(w[0][:, ds(e, 1), :, :].rearrange("p o k n -> p (o k n)"), stage[i][:, :],
                                         ACT.Copy).then_inc(e_high, 1)

            high_weights(0)
            act.wait_ge(consts, 1)
            act.wait_ge(r_var, 1)
            nc.scalar.activation(std[:, :], mean_var[:, :, 1], ACT.Sqrt, bias=eps_col[:, :]).then_inc(r_std, 1)

            act.sem_inc(g_logits, 2)
            with act.Fori(0, TT // GROUP // 2) as i:
                for par in range(2):
                    g = 2 * i + par
                    act.wait_ge(g_turned, g + 1)
                    act.wait_ge(g_logits, g + 1)
                    nc.scalar.activation(z_cols[par][:, :, :, :].rearrange("p t k c -> p (t k c)"), up[par][:, :],
                                         ACT.Copy).then_inc(g_cols, 1)
                high_weights(i + 1)
            act.wait_ge(shifted, 1)
            nc.scalar.activation(work[1][:, :, :], work[0][:, :, :], ACT.Exp).then_inc(powers, 1)
            with act.Fori(TT // GROUP // 2 + 1, E) as e:
                high_weights(e)

            act.wait_ge(meta_ready, 1)

            def z_high_half(i, u):
                if not exists(i, u):
                    return
                at_least(act, z_turned, number(i, u) + 1)
                nc.scalar.activation(z_split[0][u % 2], turned[u % 2][:, 0:D].rearrange("p (k t) -> p k t", t=P),
                                     ACT.Copy).then_inc(z_high, 1)

            def hidden_layer(i, u, half):
                if not exists(i, u):
                    return
                k = number(i, u)
                e = act.value_load(tile_expert[0:1, ds(k, 1)], min_val=0, max_val=E - 1)
                if half == 0:
                    at_least(act, h_done, 2 * (k - 1))
                at_least(act, up_full, 2 * k + half + 1, "act")
                for c in range(half * BANK, half * BANK + BANK):
                    nc.scalar.activation(hidden[u % 2][:, c * P:c * P + P], up[u % 2][:, c * P:c * P + P], ACT.Silu,
                                         bias=b1_cols[:, ds(e * KF + c, 1)]).then_inc(silu_done, 1)
                if half == 0:
                    at_least(act, down_full, k - 1)
                at_least(act, silu_done, KF * k + BANK * (half + 1))
                nc.scalar.activation(halves_of(hidden_split[0][u % 2], half), hidden[u % 2][:, half * HALF:half * HALF + HALF],
                                     ACT.Copy).then_inc(h_high, 1)

            z_high_half(0, 0)
            z_high_half(0, 1)
            hidden_layer(0, 0, 0)

            def step(i, u):
                hidden_layer(i, u, 1)
                hidden_layer(i, u + 1, 0)
                z_high_half(i, u + 2)

            tile_steps(act, step)

        @block.vector
        def _(dve):
            r = Steps(r_step, 0)

            def link(ins):
                r.mark(ins)
                dve.wait_ge(r_step, r.reached())

            dve.wait_ge(b1_turned, 1)
            nc.vector.tensor_copy(b1_cols[:, :], turned[0][:, 0:E * KF]).then_inc(b1_ready, 1)
            for t in range(TT):
                last = nc.vector.bn_aggr(mean_var[:, t, :], x2_stats[:, t, :])
            last.then_inc(r_var, 1)
            dve.wait_ge(r_std, 1)
            link(nc.vector.reciprocal(rstd[:, :], std[:, :]))
            dve.wait_ge(small_loaded, 48)
            def split(e):
                dve.wait_ge(e_high, 2 * e + 2)
                dve.sem_inc(turns["dve"], 1)
                low_half(nc.vector, w2, e, 1, w2_low)

            split(0)
            for b in range(B):
                dve.wait_ge(x2_loaded[b], 16)

            def group_rows(i, par, ahead):
                g = 2 * i + par
                if ahead:
                    dve.wait_ge(g_turned, g - 1)
                for q in range(GROUP):
                    t = GROUP * g + q
                    last = nc.vector.tensor_scalar(
                        z_group[par][:, q, :], x2_all[:, ds(t, 1), :].rearrange("p o d -> p (o d)"),
                        mean_var[:, ds(t, 1), 0], rstd[:, ds(t, 1)], ALU.subtract, ALU.mult)
                last.then_inc(g_rows, 1)

            def take_logits(i, par):
                g = 2 * i + par
                dve.wait_ge(g_logits, g + 3)
                nc.vector.tensor_tensor(out=logits[:, ds(GROUP * g, GROUP), :],
                                        in0=down[par][:, 0:GROUP * E].rearrange("p (t e) -> p t e", e=E),
                                        in1=bg_all[:, :].unsqueeze(1).to_broadcast([P, GROUP, E]),
                                        op=ALU.add).then_inc(g_taken, 1)

            group_rows(0, 0, False)
            group_rows(0, 1, False)
            with dve.Fori(1, TT // GROUP // 2) as i:
                for par in range(2):
                    group_rows(i, par, True)
                for par in range(2):
                    take_logits(i - 1, par)
                split(i)
            for par in range(2):
                take_logits(TT // GROUP // 2 - 1, par)
            split(TT // GROUP // 2)
            dve.wait_ge(g_taken, TT // GROUP)

            def tt(out, a, b, op):
                link(nc.vector.tensor_tensor(out=out, in0=a, in1=b, op=op))

            def per_token(a):
                return a.unsqueeze(2).to_broadcast([P, TT, E])

            def per_expert(a):
                return a.unsqueeze(1).to_broadcast([P, TT, E])

            dve.wait_ge(consts, 1)
            link(nc.vector.tensor_reduce(top[:, :], logits[:, :, :], AX.X, ALU.max))
            nc.vector.tensor_tensor(out=work[0][:, :, :], in0=logits[:, :, :], in1=per_token(top[:, :]),
                                    op=ALU.subtract).then_inc(shifted, 1)
            tt(work[2][:, :, :], logits[:, :, :], per_token(top[:, :]), ALU.is_equal)
            tt(work[2][:, :, :], work[2][:, :, :], per_expert(e_less[:, :]), ALU.mult)
            link(nc.vector.tensor_reduce(first[:, :], work[2][:, :, :], AX.X, ALU.min))
            dve.wait_ge(powers, 1)
            nc.vector.tensor_tensor(out=chosen[:, :, :], in0=per_expert(e_less[:, :]), in1=per_token(first[:, :]),
                                    op=ALU.is_equal).then_inc(chosen_ready, 1)
            link(nc.vector.tensor_reduce(place[:, :], work[1][:, :, :], AX.X, ALU.add))
            link(nc.vector.reciprocal(rows[:, :, 1], place[:, :]))
            nc.vector.tensor_copy(rows[:, :, 0], token[:, :])
            nc.vector.tensor_copy(rows[:, :, 2], mean_var[:, :, 0])
            nc.vector.tensor_copy(rows[:, :, 3], rstd[:, :])
            dve.wait_ge(ranks, 1)
            before = turned[0][:, 0:TT * E].rearrange("p (t e) -> p t e", e=E)
            totals = turned[1][:, 0:TT * E].rearrange("p (t e) -> p t e", e=E)
            link(nc.vector.tensor_copy(work[0][:, :, :], totals))
            at, to, reach = 0, 1, 1
            while reach < TT:
                nc.vector.tensor_copy(work[to][:, 0:reach, :], work[at][:, 0:reach, :])
                tt(work[to][:, reach:TT, :], work[at][:, reach:TT, :], work[at][:, 0:TT - reach, :], ALU.add)
                at, to, reach = to, at, 2 * reach
            sums, spare = work[at], work[to]
            link(nc.vector.tensor_scalar(counts[:, :], sums[:, TT - 1, :], float(P - 1), None, ALU.add))
            link(nc.vector.tensor_copy(counts_i[:, :], counts[:, :]))
            shift = P.bit_length() - 1
            link(nc.vector.tensor_scalar(counts_i[:, :], counts_i[:, :], shift, shift, ALU.logical_shift_right,
                                         ALU.logical_shift_left))
            link(nc.vector.tensor_copy(counts[:, :], counts_i[:, :]))
            link(nc.vector.tensor_copy(ends[0][:, :], counts[:, :]))
            e_at, e_to, reach = 0, 1, 1
            while reach < E:
                nc.vector.tensor_copy(ends[e_to][:, 0:reach], ends[e_at][:, 0:reach])
                tt(ends[e_to][:, reach:E], ends[e_at][:, reach:E], ends[e_at][:, 0:E - reach], ALU.add)
                e_at, e_to, reach = e_to, e_at, 2 * reach
            end, start = ends[e_at], ends[e_to]
            tt(start[:, :], end[:, :], counts[:, :], ALU.subtract)
            tt(spare[:, :, :], totals, sums[:, :, :], ALU.subtract)
            tt(sums[:, :, :], before, spare[:, :, :], ALU.subtract)
            split(TT // GROUP // 2 + 1)
            tt(sums[:, :, :], sums[:, :, :], per_expert(start[:, :]), ALU.add)
            tt(sums[:, :, :], sums[:, :, :], chosen[:, :, :], ALU.mult)
            link(nc.vector.tensor_reduce(place[:, :], sums[:, :, :], AX.X, ALU.add))
            link(nc.vector.tensor_copy(place_i[:, :], place[:, :]))
            link(nc.vector.tensor_scalar(place_i[:, :], place_i[:, :], shift, shift, ALU.logical_shift_right,
                                         ALU.logical_shift_left))
            link(nc.vector.tensor_copy(place_tile[:, :], place_i[:, :]))
            tt(place_lane[:, :], place[:, :], place_tile[:, :], ALU.subtract)
            for q in range(4):
                ts = slice(q * QUARTER, (q + 1) * QUARTER)
                nc.vector.tensor_tensor(out=lanes[q], in0=lane[:, :].unsqueeze(1).to_broadcast([P, QUARTER, P]),
                                        in1=place_lane[:, ts].unsqueeze(2).to_broadcast([P, QUARTER, P]),
                                        op=ALU.is_equal)
                tt(in_tile[q], starts[:, :].unsqueeze(1).to_broadcast([P, QUARTER, SORTED]),
                   place_tile[:, ts].unsqueeze(2).to_broadcast([P, QUARTER, SORTED]), ALU.is_equal)
                nc.vector.tensor_tensor(
                    out=spread[q], in0=in_tile[q].unsqueeze(3).to_broadcast([P, QUARTER, SORTED, META]),
                    in1=rows[:, ts, :].unsqueeze(2).to_broadcast([P, QUARTER, SORTED, META]),
                    op=ALU.mult).then_inc(rows_spread, 1)
                if q == 1:
                    split(E - 2)
            tt(past, end[:, :].unsqueeze(1).to_broadcast([P, SORTED, E]),
               starts[:, :].unsqueeze(2).to_broadcast([P, SORTED, E]), ALU.is_le)
            link(nc.vector.tensor_reduce(tile_f[:, :], past, AX.X, ALU.add))
            link(nc.vector.tensor_scalar(tile_expert[:, :], tile_f[:, :], float(E - 1), None, ALU.min))
            dve.wait_ge(meta_summed, 1)
            summed = up[0][:, 0:SORTED * META].rearrange("p (s c) -> p s c", c=META)
            nc.vector.tensor_copy(meta[:, :, :], summed)
            link(nc.vector.tensor_scalar(owner[:, :], summed[:, :, 0], float(NOBODY), None, ALU.add))
            nc.vector.tensor_copy(write_i[:, :], owner[:, :])
            nc.vector.tensor_scalar(read_i[:, :], owner[:, :], float(TOK - 1), None, ALU.min).then_inc(meta_ready, 1)
            dve.wait_ge(meta_ready, 1)
            split(E - 1)

            def normalise_rows(i, u):
                if not exists(i, u):
                    return
                k = number(i, u)
                at_least(dve, gathered[u % OWN], 16 * (i + u // OWN + 1))
                at_least(dve, z_turned, k - 1)
                nc.vector.tensor_scalar(z_rows[u % 2], own_rows[u % OWN], meta[:, ds(k, 1), 2], meta[:, ds(k, 1), 3],
                                        ALU.subtract, ALU.mult).then_inc(z_ready, 1)

            def z_low_half(i, u):
                if not exists(i, u):
                    return
                at_least(dve, z_high, number(i, u) + 1)
                nc.vector.tensor_tensor(out=z_split[1][u % 2],
                                        in0=turned[u % 2][:, 0:D].rearrange("p (k t) -> p k t", t=P),
                                        in1=z_split[0][u % 2], op=ALU.subtract).then_inc(z_done, 1)

            def hidden_low(i, u, half):
                if not exists(i, u):
                    return
                at_least(dve, h_high, 2 * number(i, u) + half + 1)
                nc.vector.tensor_tensor(out=halves_of(hidden_split[1][u % 2], half),
                                        in0=hidden[u % 2][:, half * HALF:half * HALF + HALF],
                                        in1=halves_of(hidden_split[0][u % 2], half), op=ALU.subtract)\
                    .then_inc(h_done, 1)

            def finish(i, u):
                k = number(i, u)
                e = dve.value_load(tile_expert[0:1, ds(k, 1)], min_val=0, max_val=E - 1)
                at_least(dve, down_full, k + 1)
                nc.vector.tensor_tensor(out=biased[u % 2], in0=down[u % 2][:, 0:D],
                                        in1=b2_all[:, ds(e, 1), :].rearrange("p o d -> p (o d)"),
                                        op=ALU.add).then_inc(bias_added, 1)
                at_least(dve, bias_added, k + 1)
                at_least(dve, scattered[u], 16 * i)
                nc.vector.scalar_tensor_tensor(out=y_rows[u], in0=biased[u % 2], scalar=meta[:, ds(k, 1), 1],
                                               in1=own_rows[u], op0=ALU.mult, op1=ALU.add).then_inc(y_ready, 1)

            normalise_rows(0, 0)
            normalise_rows(0, 1)
            z_low_half(0, 0)
            z_low_half(0, 1)
            hidden_low(0, 0, 0)
            dve.wait_ge(b2_loaded, 16)

            def step(i, u):
                hidden_low(i, u, 1)
                normalise_rows(i, u + 2)
                z_low_half(i, u + 2)
                hidden_low(i, u + 1, 0)
                finish(i, u)

            tile_steps(dve, step)

        @block.tensor
        def _(pe):
            pe.wait_ge(consts, 1)
            pe.wait_ge(small_loaded, 48)
            nc.tensor.transpose(turned[0][:, 0:E * KF], b1_rows[:, :], ident[0:E * KF, 0:E * KF])\
                .then_inc(b1_turned, 1)

            def turn_group(i, par, again):
                g = 2 * i + par
                pe.wait_ge(g_rows, g + 1)
                if again:
                    pe.wait_ge(g_cols, g - 1)
                for q in range(GROUP):
                    for k in range(KD):
                        lo = (q * KD + k) * P
                        last = nc.tensor.transpose(up[par][:, lo:lo + P], z_group[par][:, q, k * P:k * P + P],
                                                   ident[:, :])
                last.then_inc(g_turned, 1)

            def gate(i, par, again):
                g = 2 * i + par
                pe.wait_ge(g_cols, g + 1)
                if again:
                    pe.wait_ge(g_taken, g - 1)
                for q in range(GROUP):
                    for k in range(KD):
                        last = nc.tensor.matmul(down[par][:, q * E:q * E + E], z_cols[par][:, q, k, :], wg[:, k, :],
                                                start=(k == 0), stop=(k == KD - 1))
                last.then_inc(g_logits, 1)

            def groups(i, again):
                for par in range(2):
                    turn_group(i, par, again)
                for par in range(2):
                    gate(i, par, again)

            groups(0, False)
            with pe.Fori(1, TT // GROUP // 2) as i:
                groups(i, True)
            pe.wait_ge(chosen_ready, 1)
            pe.wait_ge(b1_ready, 1)
            one_hot = chosen[:, :, :].rearrange("p t e -> p (t e)")
            nc.tensor.matmul(turned[0][:, 0:TT * E], upper[:, :], one_hot, start=True, stop=True)
            nc.tensor.matmul(turned[1][:, 0:TT * E], ones[:, :], one_hot, start=True, stop=True).then_inc(ranks, 1)
            for q in range(4):
                pe.wait_ge(rows_spread, q + 1)
                for i in range(QUARTER):
                    t = q * QUARTER + i
                    last = nc.tensor.matmul(up[0][:, 0:SORTED * META], lanes[q][:, i, :],
                                            spread[q][:, i, :, :].rearrange("p s c -> p (s c)"),
                                            start=(t == 0), stop=(t == TT - 1))
            last.then_inc(meta_summed, 1)
            pe.wait_ge(w1_low, E)
            pe.wait_ge(w2_low, E)
            pe.wait_ge(meta_ready, 1)

            def turn(i, u):
                if not exists(i, u):
                    return
                k = number(i, u)
                at_least(pe, z_ready, k + 1)
                at_least(pe, z_done, k - 1)
                for c in range(KD):
                    last = nc.tensor.transpose(turned[u % 2][:, c * P:c * P + P], z_rows[u % 2][:, c * P:c * P + P],
                                               ident[:, :])
                last.then_inc(z_turned, 1)

            def expert_of(i, u):
                return pe.value_load(tile_expert[0:1, ds(number(i, u), 1)], min_val=0, max_val=E - 1)

            def upward(i, u, e, c):
                k = number(i, u)
                if c == 0:
                    at_least(pe, z_done, k + 1)
                    at_least(pe, silu_done, KF * (k - 1))
                n = 0
                for kk in range(KD):
                    for a, b in ((0, 0), (0, 1), (1, 0)):
                        lhs = w1[a][:, ds(e, 1), kk, c * P:c * P + P].rearrange("p o n -> p (o n)")
                        last = nc.tensor.matmul(up[u % 2][:, c * P:c * P + P], lhs, z_split[b][u % 2][:, kk, :],
                                                start=(n == 0), stop=(n == 3 * KD - 1))
                        n += 1
                if c % BANK == BANK - 1:
                    last.then_inc(up_full, 1)

            def downward(i, u, e, c):
                k = number(i, u)
                if c == 0:
                    at_least(pe, y_ready, k - 1)
                if c % BANK == 0:
                    at_least(pe, h_done, 2 * k + c // BANK + 1)
                for n, (a, b) in enumerate(((0, 0), (0, 1), (1, 0))):
                    rhs = w2[b][:, ds(e, 1), c, :].rearrange("p o n -> p (o n)")
                    last = nc.tensor.matmul(down[u % 2][:, 0:D], hidden_split[a][u % 2][:, c, :], rhs,
                                            start=(c == 0 and n == 0), stop=(c == KF - 1 and n == 2))
                if c == KF - 1:
                    last.then_inc(down_full, 1)

            turn(0, 0)
            turn(0, 1)
            e = expert_of(0, 0)
            for c in range(KF):
                upward(0, 0, e, c)

            experts_of = {}

            def step(i, u):
                more = exists(i, u + 1)
                if u == 0:
                    experts_of[0], experts_of[1] = expert_of(i, 0), expert_of(i, 1)
                for c in range(KF):
                    if more:
                        upward(i, u + 1, experts_of[u + 1], c)
                    downward(i, u, experts_of[u], c)
                    if c == BANK:
                        turn(i, u + 2)
                        if u + 2 <= OWN and exists(i, u + 2):
                            experts_of[u + 2] = expert_of(i, u + 2)

            tile_steps(pe, step)


def build_kernel(nc, x, ctx_1024, lmg, lmb, llg, llb, Wq, Wkv, Wout, Wg, bg, W1, b1, W2, b2, out):
    x2 = nc.dram_tensor("x2", (TOK, D), F32, kind="Internal").ap()
    with ExitStack() as stack:
        x2_stats = stack.enter_context(nc.sbuf_tensor("x2_stats", [P, TT, STATS], F32))
        stage = [stack.enter_context(nc.sbuf_tensor(f"e_stage{i}", [P, KD * F], F32)) for i in range(2)]
        e_loaded = [stack.enter_context(nc.semaphore(f"e_loaded{i}")) for i in range(2)]
        attention(nc, x, ctx_1024, (llg, llb, lmg, lmb), Wq, Wkv, Wout, x2, x2_stats,
                  [(stage[i], W[0:1].rearrange("o (k p) n -> p (o k) n", p=P), e_loaded[i])
                   for i, W in enumerate((W1, W2))])
        experts(nc, x2, x2_stats, stage, e_loaded, Wg, bg, W1, b1, W2, b2, out)


_INS = ['x', 'ctx_1024', 'L0_xattn_ln_m_g', 'L0_xattn_ln_m_b', 'L0_xattn_ln_l_g', 'L0_xattn_ln_l_b',
        'L0_xattn_Wq', 'L0_xattn_Wkv', 'L0_xattn_Wout', 'L0_ffn_Wg', 'L0_ffn_bg', 'L0_ffn_W1', 'L0_ffn_b1',
        'L0_ffn_W2', 'L0_ffn_b2']


def kernel(**inputs):
    import numpy as np
    import concourse.bacc as bacc
    from concourse.bass_utils import run_bass_kernel_spmd

    nc = bacc.Bacc("TRN2", target_bir_lowering=False, num_devices=1)
    arrays, args = {}, []
    for name in _INS:
        a = np.ascontiguousarray(inputs[name])
        arrays["in_" + name] = a
        args.append(nc.dram_tensor("in_" + name, a.shape, mybir.dt.from_np(a.dtype), kind="ExternalInput").ap())
    out = nc.dram_tensor("out", (B, N, D), F32, kind="ExternalOutput").ap()
    build_kernel(nc, *args, out)
    result = run_bass_kernel_spmd(nc, [arrays], core_ids=[0])
    return result.results[0]["out"]
```
